# Optimizing a Trainium2 kernel written in Bass

```python
import numpy as np
import jax
import jax.numpy as jnp

def _softmax(x, axis=-1):
    return jax.nn.softmax(x, axis=axis)

def _gelu(x):
    return jax.nn.gelu(x, approximate=True)

def _silu(x):
    return jax.nn.silu(x)

def _sigmoid(x):
    return jax.nn.sigmoid(x)

def _layernorm(x, axis=-1, eps=1e-05):
    m = jnp.mean(x, axis=axis, keepdims=True)
    v = jnp.var(x, axis=axis, keepdims=True)
    return (x - m) / jnp.sqrt(v + eps)

def _scatter_add(tgt, idx, src, axis=0):
    return tgt.at[idx].add(src)

def _segment_sum(src, seg, n):
    return jax.ops.segment_sum(src, seg, n)
kernel_name = 'mk_seq_postln_d1_jaxref_r8_4b2c8f'

def setup_inputs(seed: int=0):
    np.random.seed(seed)
    _w = jnp.asarray

    def _L0_attn_setup():
        import jax, jax.numpy as jnp
        import numpy as np
        D = 128
        H = 16
        KVH = 4
        HD = D // H
        LAT = 32
        WIN = 32
        B, S = (1, 256)
        BASE_G, BASE_L = (1000000.0, 10000.0)
        EPS = 1e-06

        def rmsnorm(x, w):
            return x * jax.lax.rsqrt(jnp.mean(x * x, axis=-1, keepdims=True) + EPS) * w

        def qk_norm(x):
            return x * jax.lax.rsqrt(jnp.mean(x * x, axis=-1, keepdims=True) + EPS)

        def rope(x, base):
            s, hd = (x.shape[-2], x.shape[-1])
            inv_freq = 1.0 / base ** (jnp.arange(0, hd, 2, dtype=jnp.float32) / hd)
            freqs = jnp.arange(s, dtype=jnp.float32)[:, None] * inv_freq[None, :]
            cos, sin = (jnp.cos(freqs), jnp.sin(freqs))
            xe, xo = (x[..., ::2], x[..., 1::2])
            out = jnp.stack([xe * cos - xo * sin, xe * sin + xo * cos], axis=-1)
            return out.reshape(x.shape)

        def split_heads(x, n_heads):
            b, s, _ = x.shape
            return x.reshape(b, s, n_heads, HD).transpose(0, 2, 1, 3)

        def repeat_kv(x):
            return jnp.repeat(x, H // KVH, axis=1)

        def sdpa(q, k, v, mask):
            scores = jnp.einsum('bhqd,bhkd->bhqk', q, k) / np.sqrt(HD).astype(np.float32)
            scores = jnp.where(mask, scores, jnp.float32(-1e+30))
            probs = jax.nn.softmax(scores, axis=-1)
            return jnp.einsum('bhqk,bhkd->bhqd', probs, v)

        def merge_heads(x):
            b, h, s, hd = x.shape
            return x.transpose(0, 2, 1, 3).reshape(b, s, h * hd)

        def global_latent_attn(x, wq, w_kv_down, w_k_up, w_v_up, wo):
            q = split_heads(x @ wq, H)
            latent = x @ w_kv_down
            k = split_heads(latent @ w_k_up, KVH)
            v = split_heads(latent @ w_v_up, KVH)
            q, k = (rope(q, BASE_G), rope(k, BASE_G))
            q, k = (qk_norm(q), qk_norm(k))
            k, v = (repeat_kv(k), repeat_kv(v))
            i = jnp.arange(x.shape[1])
            causal = i[:, None] >= i[None, :]
            return merge_heads(sdpa(q, k, v, causal)) @ wo

        def local_gqa_attn(x, wq, wk, wv, wo):
            q = split_heads(x @ wq, H)
            k = split_heads(x @ wk, KVH)
            v = split_heads(x @ wv, KVH)
            q, k = (rope(q, BASE_L), rope(k, BASE_L))
            q, k = (qk_norm(q), qk_norm(k))
            k, v = (repeat_kv(k), repeat_kv(v))
            i = jnp.arange(x.shape[1])
            diff = i[:, None] - i[None, :]
            mask = (diff >= 0) & (diff < WIN)
            return merge_heads(sdpa(q, k, v, mask)) @ wo
        key = jax.random.key(seed)
        ks = jax.random.split(key, 12)
        std = 0.02
        return {'hidden': jax.random.normal(ks[0], (B, S, D), dtype=jnp.float32), 'norm1_w': jnp.ones((D,), jnp.float32), 'norm2_w': jnp.ones((D,), jnp.float32), 'g_wq': jax.random.normal(ks[1], (D, H * HD), jnp.float32) * std, 'g_kv_down': jax.random.normal(ks[2], (D, LAT), jnp.float32) * std, 'g_k_up': jax.random.normal(ks[3], (LAT, KVH * HD), jnp.float32) * std, 'g_v_up': jax.random.normal(ks[4], (LAT, KVH * HD), jnp.float32) * std, 'g_wo': jax.random.normal(ks[5], (D, D), jnp.float32) * std, 'l_wq': jax.random.normal(ks[6], (D, H * HD), jnp.float32) * std, 'l_wk': jax.random.normal(ks[7], (D, KVH * HD), jnp.float32) * std, 'l_wv': jax.random.normal(ks[8], (D, KVH * HD), jnp.float32) * std, 'l_wo': jax.random.normal(ks[9], (D, D), jnp.float32) * std}
    _L0_attn_in = _L0_attn_setup()

    def _L0_ffn_setup():
        import jax, jax.numpy as jnp
        import numpy as np
        H = 128
        I = 256
        E = 8
        TOP_K = 2
        NUM_SHARED = 1
        key = jax.random.key(seed)
        ks = jax.random.split(key, 9)
        s = 0.02
        x = jax.random.normal(ks[0], (2, 256, H), dtype=jnp.float32)
        sg_w = jax.random.normal(ks[1], (I, H), dtype=jnp.float32) * s
        su_w = jax.random.normal(ks[2], (I, H), dtype=jnp.float32) * s
        sd_w = jax.random.normal(ks[3], (H, I), dtype=jnp.float32) * s
        router_w = jax.random.normal(ks[4], (E, H), dtype=jnp.float32) * s
        routing_bias = jnp.zeros((E,), dtype=jnp.float32)
        wg = jax.random.normal(ks[5], (E, I, H), dtype=jnp.float32) * s
        wu = jax.random.normal(ks[6], (E, I, H), dtype=jnp.float32) * s
        wd = jax.random.normal(ks[7], (E, H, I), dtype=jnp.float32) * s
        return {'x': x, 'sg_w': sg_w, 'su_w': su_w, 'sd_w': sd_w, 'router_w': router_w, 'routing_bias': routing_bias, 'wg': wg, 'wu': wu, 'wd': wd}
    _L0_ffn_in = _L0_ffn_setup()
    _d = {'L0_attn_hidden': _L0_attn_in['hidden'], 'L0_attn_norm1_w': _L0_attn_in['norm1_w'], 'L0_attn_norm2_w': _L0_attn_in['norm2_w'], 'L0_attn_g_wq': _L0_attn_in['g_wq'], 'L0_attn_g_kv_down': _L0_attn_in['g_kv_down'], 'L0_attn_g_k_up': _L0_attn_in['g_k_up'], 'L0_attn_g_v_up': _L0_attn_in['g_v_up'], 'L0_attn_g_wo': _L0_attn_in['g_wo'], 'L0_attn_l_wq': _L0_attn_in['l_wq'], 'L0_attn_l_wk': _L0_attn_in['l_wk'], 'L0_attn_l_wv': _L0_attn_in['l_wv'], 'L0_attn_l_wo': _L0_attn_in['l_wo'], 'L0_ffn_sg_w': _L0_ffn_in['sg_w'], 'L0_ffn_su_w': _L0_ffn_in['su_w'], 'L0_ffn_sd_w': _L0_ffn_in['sd_w'], 'L0_ffn_router_w': _L0_ffn_in['router_w'], 'L0_ffn_routing_bias': _L0_ffn_in['routing_bias'], 'L0_ffn_wg': _L0_ffn_in['wg'], 'L0_ffn_wu': _L0_ffn_in['wu'], 'L0_ffn_wd': _L0_ffn_in['wd']}
    _x0 = _d['L0_attn_hidden']
    _d['L0_attn_hidden'] = jax.random.normal(jax.random.fold_in(jax.random.key(seed), 1), (4, 1024, 128), dtype=_x0.dtype)
    del _x0
    return _d

def reference(L0_attn_hidden, L0_attn_norm1_w, L0_attn_norm2_w, L0_attn_g_wq, L0_attn_g_kv_down, L0_attn_g_k_up, L0_attn_g_v_up, L0_attn_g_wo, L0_attn_l_wq, L0_attn_l_wk, L0_attn_l_wv, L0_attn_l_wo, L0_ffn_sg_w, L0_ffn_su_w, L0_ffn_sd_w, L0_ffn_router_w, L0_ffn_routing_bias, L0_ffn_wg, L0_ffn_wu, L0_ffn_wd):

    def _L0_attn_ref(hidden, norm1_w, norm2_w, g_wq, g_kv_down, g_k_up, g_v_up, g_wo, l_wq, l_wk, l_wv, l_wo):
        import jax, jax.numpy as jnp
        import numpy as np
        D = 128
        H = 16
        KVH = 4
        HD = D // H
        LAT = 32
        WIN = 32
        B, S = (1, 256)
        BASE_G, BASE_L = (1000000.0, 10000.0)
        EPS = 1e-06

        def rmsnorm(x, w):
            return x * jax.lax.rsqrt(jnp.mean(x * x, axis=-1, keepdims=True) + EPS) * w

        def qk_norm(x):
            return x * jax.lax.rsqrt(jnp.mean(x * x, axis=-1, keepdims=True) + EPS)

        def rope(x, base):
            s, hd = (x.shape[-2], x.shape[-1])
            inv_freq = 1.0 / base ** (jnp.arange(0, hd, 2, dtype=jnp.float32) / hd)
            freqs = jnp.arange(s, dtype=jnp.float32)[:, None] * inv_freq[None, :]
            cos, sin = (jnp.cos(freqs), jnp.sin(freqs))
            xe, xo = (x[..., ::2], x[..., 1::2])
            out = jnp.stack([xe * cos - xo * sin, xe * sin + xo * cos], axis=-1)
            return out.reshape(x.shape)

        def split_heads(x, n_heads):
            b, s, _ = x.shape
            return x.reshape(b, s, n_heads, HD).transpose(0, 2, 1, 3)

        def repeat_kv(x):
            return jnp.repeat(x, H // KVH, axis=1)

        def sdpa(q, k, v, mask):
            scores = jnp.einsum('bhqd,bhkd->bhqk', q, k) / np.sqrt(HD).astype(np.float32)
            scores = jnp.where(mask, scores, jnp.float32(-1e+30))
            probs = jax.nn.softmax(scores, axis=-1)
            return jnp.einsum('bhqk,bhkd->bhqd', probs, v)

        def merge_heads(x):
            b, h, s, hd = x.shape
            return x.transpose(0, 2, 1, 3).reshape(b, s, h * hd)

        def global_latent_attn(x, wq, w_kv_down, w_k_up, w_v_up, wo):
            q = split_heads(x @ wq, H)
            latent = x @ w_kv_down
            k = split_heads(latent @ w_k_up, KVH)
            v = split_heads(latent @ w_v_up, KVH)
            q, k = (rope(q, BASE_G), rope(k, BASE_G))
            q, k = (qk_norm(q), qk_norm(k))
            k, v = (repeat_kv(k), repeat_kv(v))
            i = jnp.arange(x.shape[1])
            causal = i[:, None] >= i[None, :]
            return merge_heads(sdpa(q, k, v, causal)) @ wo

        def local_gqa_attn(x, wq, wk, wv, wo):
            q = split_heads(x @ wq, H)
            k = split_heads(x @ wk, KVH)
            v = split_heads(x @ wv, KVH)
            q, k = (rope(q, BASE_L), rope(k, BASE_L))
            q, k = (qk_norm(q), qk_norm(k))
            k, v = (repeat_kv(k), repeat_kv(v))
            i = jnp.arange(x.shape[1])
            diff = i[:, None] - i[None, :]
            mask = (diff >= 0) & (diff < WIN)
            return merge_heads(sdpa(q, k, v, mask)) @ wo
        x = hidden
        x = x + global_latent_attn(rmsnorm(x, norm1_w), g_wq, g_kv_down, g_k_up, g_v_up, g_wo)
        x = x + local_gqa_attn(rmsnorm(x, norm2_w), l_wq, l_wk, l_wv, l_wo)
        return x

    def _L0_ffn_ref(x, sg_w, su_w, sd_w, router_w, routing_bias, wg, wu, wd):
        import jax, jax.numpy as jnp
        import numpy as np
        H = 128
        I = 256
        E = 8
        TOP_K = 2
        NUM_SHARED = 1
        orig_shape = x.shape
        xt = x.reshape(-1, H)
        T = xt.shape[0]
        shared = jax.nn.silu(xt @ sg_w.T) * (xt @ su_w.T) @ sd_w.T
        shared = shared / NUM_SHARED
        logits = xt @ router_w.T + routing_bias
        probs = jax.nn.sigmoid(logits)
        topk_p, topk_idx = jax.lax.top_k(probs, TOP_K)
        topk_p = topk_p / jnp.sum(topk_p, axis=-1, keepdims=True)
        w = jnp.zeros((T, E), dtype=xt.dtype)
        w = w.at[jnp.arange(T)[:, None], topk_idx].add(topk_p)
        g = jnp.einsum('th,eih->tei', xt, wg)
        u = jnp.einsum('th,eih->tei', xt, wu)
        h = jax.nn.silu(g) * u
        y = jnp.einsum('tei,ehi->teh', h, wd)
        routed = jnp.einsum('te,teh->th', w, y)
        return (shared + routed).reshape(orig_shape)
    x = L0_attn_hidden
    x = _layernorm(x + _L0_attn_ref(x, L0_attn_norm1_w, L0_attn_norm2_w, L0_attn_g_wq, L0_attn_g_kv_down, L0_attn_g_k_up, L0_attn_g_v_up, L0_attn_g_wo, L0_attn_l_wq, L0_attn_l_wk, L0_attn_l_wv, L0_attn_l_wo), axis=-1)
    x = _layernorm(x + _L0_ffn_ref(x, L0_ffn_sg_w, L0_ffn_su_w, L0_ffn_sd_w, L0_ffn_router_w, L0_ffn_routing_bias, L0_ffn_wg, L0_ffn_wu, L0_ffn_wd), axis=-1)
    return x

_drawn_inputs = setup_inputs


def setup_inputs(seed=0):
    import zlib

    import numpy as np

    out = dict(_drawn_inputs(seed))
    spreads = {'L0_attn_norm1_w': (1.0, 0.6),
     'L0_attn_norm2_w': (1.0, 0.6),
     'L0_ffn_routing_bias': (0.0, 0.8)}
    factors = {'L0_attn_g_wq': 8.0,
     'L0_attn_g_kv_down': 8.0,
     'L0_attn_g_k_up': 8.0,
     'L0_attn_g_v_up': 8.0,
     'L0_attn_g_wo': 8.0,
     'L0_attn_l_wq': 8.0,
     'L0_attn_l_wk': 8.0,
     'L0_attn_l_wv': 7.999,
     'L0_attn_l_wo': 8.0,
     'L0_ffn_sg_w': 6.704,
     'L0_ffn_su_w': 6.511,
     'L0_ffn_sd_w': 6.453,
     'L0_ffn_router_w': 8.0,
     'L0_ffn_wg': 8.0,
     'L0_ffn_wu': 8.0,
     'L0_ffn_wd': 8.0}
    for name, (base, spread) in spreads.items():
        noise = np.random.default_rng([zlib.crc32(name.encode()), seed]).standard_normal(out[name].shape)
        drawn = base * np.exp(spread * noise) if base else spread * noise
        out[name] = jnp.asarray(drawn.astype(out[name].dtype))
    for name, factor in factors.items():
        out[name] = (out[name] * factor).astype(out[name].dtype)
    return out
```

```python
from contextlib import ExitStack

import concourse.bass as bass
from concourse import mybir

F32 = mybir.dt.float32
BF16 = mybir.dt.bfloat16
ALU = mybir.AluOpType
ACT = mybir.ActivationFunctionType
AX = mybir.AxisListType

P = 128
D = 128
HEADS, GROUPS, HD = 16, 4, 8
REP = HEADS // GROUPS
B, S = 4, 1024
TPB = S // P
TILES = B * TPB
WINDOW = 32
CT = 4
CN = CT * P
CHUNKS = TILES // CT
QK = (HEADS + GROUPS) * HD
KV = GROUPS * HD
PROJ = QK + KV
PARTS = 3
ROWS = PARTS * PARTS * HD
KPAD = 96
VW = 32
EXPERTS, FF = 8, 256
UNITS = (1 + EXPERTS) * FF // P
EXPERT_LOADS = 6
RMS_EPS, LN_EPS = 1e-6, 1e-5
BANK = 512
SLOT = 3
NPROB = 4
PV_LAG = 3


AHEAD = 2


def count(unit, per, nth):
    return (unit + AHEAD) * per + nth


def pair_count(c, par):
    return (c - par) * 8 + (AHEAD + 1) * 16


def prime(engine, semaphore, per):
    engine.nop().then_inc(semaphore, AHEAD * per)


def nth(steps, name):
    return steps.index(name) + 1


def prepare_phase(nc, tag, st):
    x, wall, norm_w, cos, sin = st["x"], st["wall"], st["norm_w"], st["cos"], st["sin"]
    ident, ident_bf, eps, v_all, q_dram, k_dram = (
        st["ident"], st["ident_bf"], st["rms_eps"], st["v_all"], st["q_dram"], st["k_dram"])
    ROPE = ["cosine", "sine_even", "sine_odd", "values"]
    NORM = ["head_sum", "head_scale", "normed", "part1", "rest", "part2", "part3"]
    with ExitStack() as ctx:
        def sb(name, shape, dt=F32):
            return ctx.enter_context(nc.sbuf_tensor(f"{name}_{tag}", shape, dt))

        def ps(name, shape, dt=F32):
            return ctx.enter_context(nc.psum_tensor(f"{name}_{tag}", shape, dt))

        def sem(name):
            return ctx.enter_context(nc.semaphore(f"{name}_{tag}"))

        sq = sb("sq", [P, TILES, D])
        rs = sb("rs", [P, TILES])
        xn = [sb(f"xn{p}", [P, CT, D]) for p in range(2)]
        xt = [sb(f"xt{p}", [P, CN]) for p in range(2)]
        tcos = [sb(f"tcos{p}", [P, CT * QK]) for p in range(2)]
        tsin = [sb(f"tsin{p}", [P, CT * QK]) for p in range(2)]
        roped = [sb(f"roped{p}", [P, CT * QK]) for p in range(2)]
        sqh = [sb(f"sqh{p}", [P, CT * QK]) for p in range(2)]
        hs = [sb(f"hs{p}", [P, CT * QK // HD]) for p in range(2)]
        hr = [sb(f"hr{p}", [P, CT * QK // HD]) for p in range(2)]
        hi = [sb(f"hi{p}", [P, CT * QK // HD]) for p in range(2)]
        part = [[sb(f"part{i}_{p}", [P, CT * QK], BF16) for i in range(PARTS)] for p in range(2)]
        zq = [sb(f"zq{p}", [P, PARTS, CN], BF16) for p in range(2)]
        zk = [sb(f"zk{p}", [PARTS * KV, CN], BF16) for p in range(2)]
        ps_x = [ps(f"ps_x{p}", [P, CT, D]) for p in range(2)]
        ps_p = [ps(f"ps_p{p}", [P, CT, 256]) for p in range(2)]
        ps_z = [ps(f"ps_z{p}", [P, 2, PARTS + 1, P], BF16) for p in range(2)]

        squared, summed, rooted, rs_ready = sem("squared"), sem("summed"), sem("rooted"), sem("rs_ready")
        xn_ready, xt_turned, xt_ready = sem("xn_ready"), sem("xt_turned"), sem("xt_ready")
        projected, rope, roped_ready, head_squared = (
            sem("projected"), sem("rope"), sem("roped_ready"), sem("head_squared"))
        head_rooted, norm, turned, parts_out = (
            sem("head_rooted"), sem("norm"), sem("turned"), sem("parts_out"))
        stored = [sem(f"stored{p}") for p in range(2)]

        def heads(ap):
            return ap.rearrange("p (n d) -> p n d", d=HD)

        block = ctx.enter_context(nc.Block())

        @block.gpsimd
        def _(pool):
            def scale_tokens(c, par):
                pool.wait_ge(xt_turned, count(c, 1, -1))
                pool.tensor_tensor(xn[par][:], x[:, bass.ds(c * CT, CT), :],
                                   rs[:, bass.ds(c * CT, CT)].unsqueeze(2).to_broadcast([P, CT, D]),
                                   ALU.mult).then_inc(xn_ready, 1)

            def add_rope(c, par):
                pool.wait_ge(rope, count(c, len(ROPE), nth(ROPE, "sine_odd")))
                pool.wait_ge(head_squared, count(c, 1, -1))
                pool.wait_ge(norm, count(c - 2, len(NORM), nth(NORM, "normed")))
                pool.tensor_tensor(roped[par][:], tcos[par][:], tsin[par][:], ALU.add).then_inc(roped_ready, 1)

            prime(pool, xn_ready, 1)
            prime(pool, roped_ready, 1)
            pool.wait_ge(rs_ready, 1)
            scale_tokens(0, 0)
            with pool.Fori(0, CHUNKS // 2 - 1) as i:
                for par in range(2):
                    scale_tokens(i * 2 + (par + 1), 1 - par)
                    add_rope(i * 2 + par, par)
            scale_tokens(CHUNKS - 1, 1)
            add_rope(CHUNKS - 2, 0)
            add_rope(CHUNKS - 1, 1)

        @block.vector
        def _(dve):
            prime(dve, rope, len(ROPE))
            prime(dve, norm, len(NORM))
            with dve.Fori(0, B) as b:
                dve.wait_ge(squared, b + 1)
                dve.tensor_reduce(rs[:, bass.ds(b * TPB, TPB)], sq[:, bass.ds(b * TPB, TPB), :],
                                  AX.X, ALU.add).then_inc(summed, 1)
            dve.wait_ge(rooted, 1)
            dve.reciprocal(rs[:], rs[:]).then_inc(rs_ready, 1)

            def rotate(c, par):
                dve.wait_ge(projected, count(c, 1, 1))
                dve.wait_ge(roped_ready, count(c, 1, -1))
                dve.wait_ge(norm, count(c - 2, len(NORM), nth(NORM, "part3")))
                pq = ps_p[par][:, :, 0:QK]
                half = pq.rearrange("p t (h i two) -> p t h i two", i=HD // 2, two=2)
                cs = cos[:, par * CT:(par + 1) * CT, :].unsqueeze(2).to_broadcast([P, CT, QK // HD, HD])
                dve.tensor_tensor(tcos[par][:].rearrange("p (t h d) -> p t h d", t=CT, d=HD),
                                  pq.rearrange("p t (h d) -> p t h d", d=HD), cs, ALU.mult).then_inc(rope, 1)
                out = tsin[par][:].rearrange("p (t h i two) -> p t h i two", t=CT, i=HD // 2, two=2)
                sn = sin[:, par * CT:(par + 1) * CT, :].rearrange("p t (i two) -> p t i two", two=2)
                for to in range(2):
                    dve.tensor_tensor(out[:, :, :, :, to], half[:, :, :, :, 1 - to],
                                      sn[:, :, :, to].unsqueeze(2).to_broadcast([P, CT, QK // HD, HD // 2]),
                                      ALU.mult).then_inc(rope, 1)
                dve.tensor_copy(v_all[:, bass.ds(c * CT, CT), :], ps_p[par][:, :, QK:PROJ]).then_inc(rope, 1)

            def normalise(c, par):
                def done(name):
                    dve.wait_ge(norm, count(c, len(NORM), nth(NORM, name)))
                dve.wait_ge(head_squared, count(c, 1, 1))
                dve.wait_ge(head_rooted, count(c, 1, -1))
                dve.tensor_reduce(hs[par][:], heads(sqh[par][:]), AX.X, ALU.add).then_inc(norm, 1)
                dve.wait_ge(head_rooted, count(c, 1, 1))
                dve.reciprocal(hi[par][:], hr[par][:]).then_inc(norm, 1)
                done("head_scale")
                dve.tensor_tensor(heads(sqh[par][:]), heads(roped[par][:]),
                                  hi[par][:].unsqueeze(2).to_broadcast([P, CT * QK // HD, HD]),
                                  ALU.mult).then_inc(norm, 1)
                done("normed")
                dve.wait_ge(turned, count(c, 2, -2))
                dve.tensor_copy(part[par][0][:], sqh[par][:]).then_inc(norm, 1)
                done("part1")
                dve.tensor_tensor(tcos[par][:], sqh[par][:], part[par][0][:], ALU.subtract).then_inc(norm, 1)
                done("rest")
                dve.tensor_copy(part[par][1][:], tcos[par][:]).then_inc(norm, 1)
                done("part2")
                dve.tensor_tensor(part[par][2][:], tcos[par][:], part[par][1][:], ALU.subtract).then_inc(norm, 1)

            rotate(0, 0)
            with dve.Fori(0, CHUNKS // 2 - 1) as i:
                for par in range(2):
                    rotate(i * 2 + (par + 1), 1 - par)
                    normalise(i * 2 + par, par)
            rotate(CHUNKS - 1, 1)
            normalise(CHUNKS - 2, 0)
            normalise(CHUNKS - 1, 1)

        @block.scalar
        def _(act):
            for s in (xt_ready, head_squared, head_rooted):
                prime(act, s, 1)
            prime(act, parts_out, 4)
            with act.Fori(0, B) as b:
                act.activation(sq[:, bass.ds(b * TPB, TPB), :], x[:, bass.ds(b * TPB, TPB), :],
                               ACT.Square).then_inc(squared, 1)
            act.wait_ge(summed, B)
            act.activation(rs[:], rs[:], ACT.Sqrt, scale=1.0 / D, bias=eps[:]).then_inc(rooted, 1)

            def move_tokens(c, par):
                act.wait_ge(xt_turned, count(c, 1, 1))
                act.wait_ge(projected, count(c, 1, -1))
                act.activation(xt[par][:], ps_x[par][:], ACT.Copy, scale=norm_w[:]).then_inc(xt_ready, 1)

            def square_heads(c, par):
                act.wait_ge(roped_ready, count(c, 1, 1))
                act.wait_ge(norm, count(c - 2, len(NORM), nth(NORM, "rest")))
                act.activation(sqh[par][:], roped[par][:], ACT.Square).then_inc(head_squared, 1)

            def root_heads(c, par):
                act.wait_ge(norm, count(c, len(NORM), nth(NORM, "head_sum")))
                act.activation(hr[par][:], hs[par][:], ACT.Sqrt, scale=1.0 / HD, bias=eps[:]).then_inc(head_rooted, 1)

            def move_parts(b, par):
                c = b * 2 + par
                act.wait_ge(stored[par], count(b, 32, 0))
                for h in range(2):
                    act.wait_ge(turned, count(c, 2, h + 1))
                    act.activation(zq[par][:].rearrange("p i (t n) -> p t i n", n=P)[:, 2 * h:2 * h + 2],
                                   ps_z[h][:, :, 0:PARTS, :], ACT.Copy).then_inc(parts_out, 1)
                    act.activation(zk[par][:].rearrange("p (t n) -> p t n", n=P)[:, 2 * h:2 * h + 2],
                                   ps_z[h][0:PARTS * KV, :, PARTS, :], ACT.Copy).then_inc(parts_out, 1)

            move_tokens(0, 0)
            with act.Fori(0, CHUNKS // 2 - 1) as i:
                for par in range(2):
                    square_heads(i * 2 + par, par)
                    move_tokens(i * 2 + (par + 1), 1 - par)
                    root_heads(i * 2 + par, par)
                    move_parts(i, par)
            square_heads(CHUNKS - 2, 0)
            move_tokens(CHUNKS - 1, 1)
            root_heads(CHUNKS - 2, 0)
            move_parts(B - 1, 0)
            square_heads(CHUNKS - 1, 1)
            root_heads(CHUNKS - 1, 1)
            move_parts(B - 1, 1)

        @block.tensor
        def _(pe):
            for s in (xt_turned, projected):
                prime(pe, s, 1)
            prime(pe, turned, 2)

            def project(c, par):
                pe.wait_ge(xn_ready, count(c, 1, 1))
                pe.wait_ge(xt_ready, count(c, 1, -1))
                for t in range(CT):
                    last = pe.transpose(ps_x[par][:, t, :], xn[par][:, t, :], ident[:])
                last.then_inc(xt_turned, 1)
                pe.wait_ge(xt_ready, count(c, 1, 1))
                pe.wait_ge(rope, count(c - 2, len(ROPE), nth(ROPE, "values")))
                for t in range(CT):
                    last = pe.matmul(ps_p[par][:, t, 0:PROJ], xt[par][:, t * P:(t + 1) * P], wall[:],
                                     start=True, stop=True)
                last.then_inc(projected, 1)

            def turn_parts(c, par):
                pe.wait_ge(norm, count(c, len(NORM), nth(NORM, "part3")))
                for h in range(2):
                    pe.wait_ge(parts_out, count(c, 4, 2 * (h + 1) - 4))
                    for t in range(2):
                        at = (2 * h + t) * QK
                        for i in range(PARTS):
                            pe.transpose(ps_z[h][:, t, i, :], part[par][i][:, at:at + HEADS * HD], ident_bf[:])
                            last = pe.transpose(ps_z[h][i * KV:(i + 1) * KV, t, PARTS, :],
                                                part[par][i][:, at + HEADS * HD:at + QK], ident_bf[:])
                    last.then_inc(turned, 1)

            project(0, 0)
            with pe.Fori(0, CHUNKS // 2 - 1) as i:
                for par in range(2):
                    project(i * 2 + (par + 1), 1 - par)
                    turn_parts(i * 2 + par, par)
            project(CHUNKS - 1, 1)
            turn_parts(CHUNKS - 2, 0)
            turn_parts(CHUNKS - 1, 1)

        @block.sync
        def _(sp):
            for s in stored:
                prime(sp, s, 32)
            with sp.Fori(0, B) as b:
                for par in range(2):
                    sp.wait_ge(parts_out, count(b * 2 + par, 4, 4))
                    sp.dma_start(q_dram[bass.ds(b, 1), :, :, par * CN:(par + 1) * CN].rearrange("b i r n -> (b r) i n"),
                                 zq[par][:]).then_inc(stored[par], 16)
                    sp.dma_start(k_dram[bass.ds(b, 1), :, par * CN:(par + 1) * CN].rearrange("b r n -> (b r) n"),
                                 zk[par][:]).then_inc(stored[par], 16)
            for s in stored:
                sp.wait_ge(s, count(B, 32, 0))


def slots_of(local):
    slots = []
    for par in range(2):
        if local:
            for qt in range(TPB):
                slots.append([("full", par, qt, qt, g, g * BANK) for g in range(SLOT)])
                last = [("full", par, qt, qt, SLOT, 0)]
                if qt:
                    last.append(("corner", par, qt, qt - 1, None, BANK))
                slots.append(last)
        else:
            flat = [("full", par, qt, kt, g) for qt in range(TPB)
                    for kt in [qt] + list(range(qt)) for g in range(GROUPS)]
            for n in range(0, len(flat), SLOT):
                slots.append([item + (k * BANK,) for k, item in enumerate(flat[n:n + SLOT])])
    return slots


def attention_phase(nc, tag, st, local):
    x, wo, ident, v_all, q_dram, k_dram = (st[k] for k in ("x", "wo", "ident", "v_all", "q_dram", "k_dram"))
    slots = slots_of(local)
    N = len(slots)
    OUTS = 2 * TPB
    q_of = lambda it: it[1] * TPB + it[2]
    first_of, last_of, last_of_batch = {}, {}, {}
    for n, items in enumerate(slots):
        for it in items:
            first_of.setdefault(q_of(it), n)
            last_of[q_of(it)] = n
            last_of_batch[it[1]] = n
    pool_masks, dve_masks, pool_upto, dve_upto = {}, {}, [], []
    for n, items in enumerate(slots):
        diagonal = [it for it in items if it[0] == "full" and it[2] == it[3]]
        if local and len(items) < SLOT:
            pool_masks[n] = items
        elif diagonal:
            dve_masks[n] = diagonal
        pool_upto.append(sum(len(m) for m in pool_masks.values()))
        dve_upto.append(len(dve_masks))
    n_pool, n_dve = pool_upto[-1], dve_upto[-1]

    weighed_upto = [sum(len(items) for items in slots[:n + 1]) for n in range(N)]
    order = [q_of(it) for items in slots for it in items]
    tile_weighed = [len(order) - order[::-1].index(q) for q in range(OUTS)]
    W = len(order)
    turn_step, free_step = [], 0
    for q in range(OUTS):
        turn_step.append(max(last_of[q] + PV_LAG + 1, free_step))
        free_step = turn_step[q] + 2
    steps = turn_step[-1] + 3
    work = [(turn_step[q] + 2, 0, "add", q) for q in range(OUTS)]
    work += [(n + 1, 1, "mask", n) for n in dve_masks]
    work += [(last_of[q] + PV_LAG, 2, "sums", q) for q in range(OUTS)]
    work += [(turn_step[q], 3, "heads", q) for q in range(OUTS)]
    work += [(turn_step[q] + 1, 3, "move", q) for q in range(OUTS)]
    work.sort()
    POST = ["denominators", "heads", "heads_moved", "added"]

    with ExitStack() as ctx:
        def sb(name, shape, dt=F32):
            return ctx.enter_context(nc.sbuf_tensor(f"{name}_{tag}", shape, dt))

        def ps(name, shape, dt=F32):
            return ctx.enter_context(nc.psum_tensor(f"{name}_{tag}", shape, dt))

        def sem(name):
            return ctx.enter_context(nc.semaphore(f"{name}_{tag}"))

        qs = [sb(f"qs{p}", [KPAD, HEADS, S], BF16) for p in range(2)]
        ks = [sb(f"ks{p}", [KPAD, GROUPS, S], BF16) for p in range(2)]
        va = [sb(f"va{p}", [P, TPB, GROUPS, VW]) for p in range(2)]
        vc = [sb(f"vc{p}", [P, TPB, GROUPS, VW]) for p in range(2)] if local else [None, None]
        prob = [sb(f"prob{n}", [P, SLOT * BANK]) for n in range(NPROB)]
        sums = [sb(f"sums{p}", [P, REP, P]) for p in range(2)]
        rden = sb("rden", [P, REP, GROUPS])
        on = sb("on", [P, GROUPS, REP, HD])
        ot = sb("ot", [P, P])
        band = sb("band", [P, P])
        edge = sb("edge", [P, WINDOW]) if local else None
        ps_s = [ps(f"ps_s{n}", [P, SLOT * BANK]) for n in range(2)]
        ps_v = ps("ps_v", [P, REP, P])
        ps_m = ps("ps_m", [P, REP, P])

        cleared, masks_made, values = sem("cleared"), sem("masks_made"), sem("values")
        stacks, corners = [sem(f"stacks{p}") for p in range(2)], [sem(f"corners{p}") for p in range(2)]
        scored, exped, masked, masked_dve, weighed = (
            sem("scored"), sem("exped"), sem("masked"), sem("masked_dve"), sem("weighed"))
        post, sums_out, sums_turned, heads_turned, y_ready = (
            sem("post"), sem("sums_out"), sem("sums_turned"), sem("heads_turned"), sem("y_ready"))
        STACK_DMAS = 2 * PARTS * PARTS

        def post_value(pair, q, name):
            return count(pair * OUTS + q, len(POST), nth(POST, name))

        block = ctx.enter_context(nc.Block())

        @block.sync
        def _(sp):
            for s in stacks:
                prime(sp, s, STACK_DMAS * 16)
            for s in corners:
                prime(sp, s, GROUPS * 16)
            sp.wait_ge(cleared, 4)
            with sp.Fori(0, B // 2) as pair:
                for par in range(2):
                    sp.wait_ge(weighed, count(pair - 1, W, weighed_upto[last_of_batch[par]]))
                    for i in range(PARTS):
                        for j in range(PARTS):
                            r = (i * PARTS + j) * HD
                            sp.dma_start(qs[par][r:r + HD, :, :],
                                         q_dram[bass.ds(pair * 2 + par, 1), i].rearrange(
                                             "b (h d) n -> (b d) h n", d=HD)).then_inc(stacks[par], 16)
                            sp.dma_start(ks[par][r:r + HD, :, :],
                                         k_dram[bass.ds(pair * 2 + par, 1), j * KV:(j + 1) * KV].rearrange(
                                             "b (g d) n -> (b d) g n", d=HD)).then_inc(stacks[par], 16)
                    if local:
                        sp.wait_ge(values, count(pair, 2, par + 1))
                        for g in range(GROUPS):
                            sp.dma_start(vc[par][g * WINDOW:(g + 1) * WINDOW, :, g, :],
                                         va[par][P - WINDOW:P, :, g, :]).then_inc(corners[par], 16)

        @block.gpsimd
        def _(pool):
            prime(pool, values, 2)
            prime(pool, masked, max(n_pool, 1))
            for p in range(2):
                pool.memset(qs[p][64:KPAD, :, :], 0.0).then_inc(cleared, 1)
                pool.memset(ks[p][64:KPAD, :, :], 0.0).then_inc(cleared, 1)
            pool.wait_ge(cleared, 4)
            for p in range(2):
                pool.memset(va[p][:], 0.0).then_inc(masks_made, 1)
                if local:
                    pool.memset(vc[p][:], 0.0).then_inc(masks_made, 1)
            made = 4 if local else 2
            pool.wait_ge(masks_made, made)
            for p in range(2):
                pool.memset(va[p][:, :, :, HD:HD + 1], 1.0).then_inc(masks_made, 1)
            made += 2
            pool.memset(band[:], 1.0).then_inc(masks_made, 1)
            if local:
                pool.memset(edge[:], 1.0).then_inc(masks_made, 1)
            made += 2 if local else 1
            pool.wait_ge(masks_made, made)
            pool.affine_select(out=band[:], in_=band[:], compare_op=ALU.is_ge, fill=0.0, base=0,
                               pattern=[[1, P]], channel_multiplier=-1).then_inc(masks_made, 1)
            made += 1
            if local:
                pool.wait_ge(masks_made, made)
                pool.affine_select(out=band[:], in_=band[:], compare_op=ALU.is_ge, fill=0.0, base=WINDOW - 1,
                                   pattern=[[-1, P]], channel_multiplier=1).then_inc(masks_made, 1)
                for g in range(GROUPS):
                    pool.wait_ge(masks_made, made + 1 + g)
                    rows = edge[g * WINDOW:(g + 1) * WINDOW, :]
                    pool.affine_select(out=rows, in_=rows, compare_op=ALU.is_gt, fill=0.0, base=0,
                                       pattern=[[-1, WINDOW]], channel_multiplier=1).then_inc(masks_made, 1)
                made += 1 + GROUPS
            pool.wait_ge(masks_made, made)
            with pool.Fori(0, B // 2) as pair:
                for par in range(2):
                    pool.wait_ge(weighed, count(pair - 1, W, weighed_upto[last_of_batch[par]]))
                    if local:
                        pool.wait_ge(corners[par], count(pair, GROUPS * 16, 0))
                    pool.tensor_copy(va[par][:, :, :, 0:HD],
                                     v_all[:, bass.ds((pair * 2 + par) * TPB, TPB), :].rearrange(
                                         "p t (g d) -> p t g d", d=HD)).then_inc(values, 1)
                    for n in sorted(pool_masks):
                        items = pool_masks[n]
                        if items[0][1] != par:
                            continue
                        pool.wait_ge(exped, count(pair, N, n + 1))
                        for it in items:
                            full = it[0] == "full"
                            mask, width = (band, P) if full else (edge, WINDOW)
                            region = prob[n % NPROB][:, it[5]:it[5] + REP * width].rearrange(
                                "p (r q) -> p r q", r=REP)
                            pool.tensor_tensor(region, region, mask[:].unsqueeze(1).to_broadcast([P, REP, width]),
                                               ALU.mult).then_inc(masked, 1)

        @block.scalar
        def _(act):
            prime(act, exped, N)
            with act.Fori(0, B // 2) as pair:
                for n, items in enumerate(slots):
                    act.wait_ge(scored, count(pair, N, n + 1))
                    act.wait_ge(weighed, count(pair, W, weighed_upto[n - NPROB] if n >= NPROB
                                               else weighed_upto[n - NPROB] - W))
                    width = sum(REP * (P if it[0] == "full" else WINDOW) for it in items)
                    act.activation(prob[n % NPROB][:, 0:width], ps_s[n % 2][:, 0:width], ACT.Exp,
                                   scale=HD ** -0.5).then_inc(exped, 1)

        @block.vector
        def _(dve):
            prime(dve, post, len(POST))
            prime(dve, sums_out, OUTS)
            prime(dve, masked_dve, max(n_dve, 1))
            dve.wait_ge(masks_made, 4 + 2 + 3 + 1 + GROUPS if local else 2 + 2 + 2)

            def sums_of(pair, q):
                dve.wait_ge(weighed, count(pair, W, tile_weighed[q]))
                dve.wait_ge(sums_turned, count(pair, OUTS, q - 1))
                dve.tensor_copy(sums[q % 2][:], ps_v[:]).then_inc(sums_out, 1)

            def heads_of(pair, q):
                dve.wait_ge(sums_turned, count(pair, OUTS, q + 1))
                by_group = ps_m[:].rearrange("p r (g v) -> p r g v", v=VW)
                dve.reciprocal(rden[:], by_group[:, :, :, HD]).then_inc(post, 1)
                dve.wait_ge(post, post_value(pair, q, "denominators"))
                dve.tensor_tensor(on[:].rearrange("p g r d -> p r g d"), by_group[:, :, :, 0:HD],
                                  rden[:].unsqueeze(3).to_broadcast([P, REP, GROUPS, HD]),
                                  ALU.mult).then_inc(post, 1)

            def move_heads(pair, q):
                dve.wait_ge(heads_turned, count(pair, OUTS, q + 1))
                dve.tensor_copy(ot[:], ps_m[:, 0, :]).then_inc(post, 1)

            def add_tokens(pair, q):
                dve.wait_ge(y_ready, count(pair, OUTS, q + 1))
                tile = x[:, bass.ds(pair * OUTS + q, 1), :]
                dve.tensor_tensor(tile, tile, ps_m[:, 1:2, :], ALU.add).then_inc(post, 1)

            def mask_slot(pair, n):
                dve.wait_ge(exped, count(pair, N, n + 1))
                at, width = dve_masks[n][0][5], len(dve_masks[n]) * REP
                region = prob[n % NPROB][:, at:at + width * P].rearrange("p (r q) -> p r q", q=P)
                dve.tensor_tensor(region, region, band[:].unsqueeze(1).to_broadcast([P, width, P]),
                                  ALU.mult).then_inc(masked_dve, 1)

            do = {"sums": sums_of, "heads": heads_of, "move": move_heads, "add": add_tokens, "mask": mask_slot}
            with dve.Fori(0, B // 2) as pair:
                for _, _, what, which in work:
                    do[what](pair, which)

        @block.tensor
        def _(pe):
            prime(pe, scored, N)
            prime(pe, weighed, W)
            for s in (sums_turned, heads_turned, y_ready):
                prime(pe, s, OUTS)

            def score(pair, n):
                par = slots[n][0][1]
                if n == 0 or slots[n - 1][0][1] != par:
                    pe.wait_ge(stacks[par], count(pair, STACK_DMAS * 16, STACK_DMAS * 16))
                pe.wait_ge(exped, count(pair, N, n - 1))
                for kind, _, qt, kt, g, at in slots[n]:
                    if kind == "full":
                        last = pe.matmul(ps_s[n % 2][:, at:at + REP * P].rearrange("p (r q) -> p r q", q=P),
                                         ks[par][:, g, kt * P:(kt + 1) * P],
                                         qs[par][:, g * REP:(g + 1) * REP, qt * P:(qt + 1) * P],
                                         start=True, stop=True)
                        continue
                    for h in range(GROUPS):
                        last = pe.matmul(ps_s[n % 2][h * WINDOW:(h + 1) * WINDOW,
                                                     at:at + REP * WINDOW].rearrange("p (r q) -> p r q", r=REP),
                                         ks[par][:, h, (kt + 1) * P - WINDOW:(kt + 1) * P],
                                         qs[par][:, h * REP:(h + 1) * REP, qt * P:qt * P + WINDOW],
                                         start=True, stop=True)
                last.then_inc(scored, 1)

            def weigh(pair, m):
                par = slots[m][0][1]
                if m == 0 or slots[m - 1][0][1] != par:
                    pe.wait_ge(values, count(pair, 2, par + 1))
                    if local:
                        pe.wait_ge(corners[par], count(pair, GROUPS * 16, GROUPS * 16))
                pe.wait_ge(exped, count(pair, N, m + 1))
                if m in pool_masks:
                    pe.wait_ge(masked, count(pair, n_pool, pool_upto[m]))
                if m in dve_masks:
                    pe.wait_ge(masked_dve, count(pair, n_dve, dve_upto[m]))
                for it in slots[m]:
                    kind, _, qt, kt, g, at = it
                    q = q_of(it)
                    first = kt == qt
                    if first and g == 0:
                        pe.wait_ge(sums_out, count(pair, OUTS, q))
                    if kind == "full":
                        pe.matmul(ps_v[g * VW:(g + 1) * VW, :, :], va[par][:, kt, g, :],
                                         prob[m % NPROB][:, at:at + REP * P].rearrange("p (r q) -> p r q", q=P),
                                         start=first, stop=(qt == 0 if local else kt == max(qt - 1, 0))
                                         ).then_inc(weighed, 1)
                        continue
                    for h in range(GROUPS):
                        last = pe.matmul(ps_v[h * VW:(h + 1) * VW, :, 0:WINDOW], vc[par][:, kt, h, :],
                                         prob[m % NPROB][:, at:at + REP * WINDOW].rearrange(
                                             "p (r q) -> p r q", r=REP), start=False, stop=True)
                    last.then_inc(weighed, 1)

            def turn_sums(pair, q):
                pe.wait_ge(sums_out, count(pair, OUTS, q + 1))
                pe.wait_ge(post, post_value(pair, q - 1, "added"))
                for r in range(REP):
                    last = pe.transpose(ps_m[:, r, :], sums[q % 2][:, r, :], ident[:])
                last.then_inc(sums_turned, 1)

            def turn_heads(pair, q):
                pe.wait_ge(post, post_value(pair, q, "heads"))
                pe.transpose(ps_m[:, 0, :], on[:].rearrange("p g r d -> p (g r d)"), ident[:]
                             ).then_inc(heads_turned, 1)

            def project(pair, q):
                pe.wait_ge(post, post_value(pair, q, "heads_moved"))
                pe.matmul(ps_m[:, 1, :], ot[:], wo[:], start=True, stop=True).then_inc(y_ready, 1)

            with pe.Fori(0, B // 2) as pair:
                for n in range(steps):
                    if n - 2 in turn_step:
                        project(pair, turn_step.index(n - 2))
                    if n < N:
                        score(pair, n)
                    if 0 <= n - PV_LAG < N:
                        weigh(pair, n - PV_LAG)
                    if n in turn_step:
                        turn_sums(pair, turn_step.index(n))
                    if n - 1 in turn_step:
                        turn_heads(pair, turn_step.index(n - 1))


def expert_phase(nc, ins, out, st):
    x, ident = st["x"], st["ident"]
    w_gate, w_up, w_down, w_router, bias, rank = (
        st[k] for k in ("w_gate", "w_up", "w_down", "w_router", "bias", "rank"))
    ROUTE_AT = {"r_load": 0, "r_center": 2, "r_scale": 3, "r_turn": 4, "r_logits": 5, "r_exp": 6, "r_pick": 7,
                "r_weights": 8, "r_spread": 9}
    END_AT = {"f_move": 0, "f_turn": 1, "f_center": 2, "f_scale": 11}
    R_DVE = ["sum", "mean", "center", "square", "var", "var_eps", "token", "logit", "one_plus", "prob",
             "top1", "is1", "place1", "first1", "pick1", "others", "top2", "is2", "place2", "first2",
             "pick2", "picks", "picked", "total", "inverse", "weight", "moved"]
    F_DVE = ["sum", "mean", "center", "square", "var", "var_eps", "token"]
    with ExitStack() as ctx:
        def sb(name, shape, dt=F32):
            return ctx.enter_context(nc.sbuf_tensor(name, shape, dt))

        def ps(name, shape, dt=F32):
            return ctx.enter_context(nc.psum_tensor(name, shape, dt))

        def sem(name):
            return ctx.enter_context(nc.semaphore(name))

        x_in = [sb(f"x_in{p}", [P, CT, D]) for p in range(2)]
        token = [sb(f"token{p}", [P, CT, D]) for p in range(2)]
        tokens_t = [sb(f"tokens_t{p}", [P, CN]) for p in range(2)]
        spread = [sb(f"spread{p}", [P, EXPERTS, CN]) for p in range(2)]
        weight_t = sb("weight_t", [EXPERTS, CN])
        scaled = [sb(f"scaled{p}", [P, CN]) for p in range(2)]
        gated = [sb(f"gated{p}", [P, CN]) for p in range(2)]
        hidden = [sb(f"hidden{p}", [P, CN]) for p in range(2)]
        y_t = sb("y_t", [P, CN])
        result = [sb(f"result{p}", [P, CT, D]) for p in range(2)]
        half = sb("half", [P, CT])
        norms = {}
        for who in ("r", "f"):
            norms[who] = dict(
                centered=sb(f"{who}_centered", [P, CT, D]), squares=sb(f"{who}_squares", [P, CT, D]),
                total=sb(f"{who}_total", [P, CT]), var=sb(f"{who}_var", [P, CT]), rstd=sb(f"{who}_rstd", [P, CT]))
        route = {n: sb(f"route_{n}", [P, CT, EXPERTS]) for n in
                 ("logit", "exp", "one_plus", "prob", "is_", "place", "pick1", "others", "pick2", "weight")}
        tops = {n: sb(f"tops_{n}", [P, CT]) for n in ("top1", "first", "top2", "total")}
        w_dram = [nc.dram_tensor(f"w_dram{p}", [EXPERTS, CN], F32).ap() for p in range(2)]
        ps_g = [ps(f"ps_g{p}", [P, CN]) for p in range(2)]
        ps_u = [ps(f"ps_u{p}", [P, CN]) for p in range(2)]
        ps_y = ps("ps_y", [P, CN])
        ps_t = ps("ps_t", [P, CT, D])
        ps_f = ps("ps_f", [P, CT, D])
        ps_r = ps("ps_r", [P, CN])

        gates, ups, downs, silus, hiddens, scales = (
            sem(n) for n in ("gates", "ups", "downs", "silus", "hiddens", "scales"))
        r_dve, r_rstd, r_turned, r_moved, r_logits, r_exped, w_turned = (
            sem(n) for n in ("r_dve", "r_rstd", "r_turned", "r_moved", "r_logits", "r_exped", "w_turned"))
        f_dve, f_rstd, f_moved, f_turned = (sem(n) for n in ("f_dve", "f_rstd", "f_moved", "f_turned"))
        x_loaded, w_stored, w_spread, out_stored = (
            [sem(f"{n}{p}") for p in range(2)] for n in ("x_loaded", "w_stored", "w_spread", "out_stored"))
        half_made = sem("half_made")

        def over_chunks(engine, main, routing, ending):
            def stages(table, fn, c, par, unit):
                for name, at in table.items():
                    if at == unit:
                        fn(name, c, par)

            def chunk(c, par, routes=True):
                for unit in range(UNITS):
                    main(c, par, unit)
                    stages(END_AT, ending, c - 1, 1 - par, unit) if not isinstance(c, int) or c else None
                    stages(ROUTE_AT, routing, c + 1, 1 - par, unit) if routes else None

            for name in ROUTE_AT:
                routing(name, 0, 0)
            chunk(0, 0)
            with engine.Fori(0, CHUNKS // 2 - 1) as i:
                for par in range(2):
                    chunk(i * 2 + (par + 1), 1 - par)
            chunk(CHUNKS - 1, 1, routes=False)
            for name in END_AT:
                ending(name, CHUNKS - 1, 1)

        block = ctx.enter_context(nc.Block())

        @block.sync
        def _(sp):
            for s in x_loaded + out_stored + w_stored + w_spread:
                prime(sp, s, 16)

            def main(c, par, unit):
                pass

            def routing(name, c, par):
                if name == "r_load":
                    sp.wait_ge(r_dve, count(c - 2, len(R_DVE), nth(R_DVE, "sum")))
                    sp.dma_start(x_in[par][:], st["hidden_tiles"][:, bass.ds(c * CT, CT), :]
                                 ).then_inc(x_loaded[par], 16)
                if name == "r_spread":
                    sp.wait_ge(r_dve, count(c, len(R_DVE), nth(R_DVE, "moved")))
                    sp.dma_start(w_dram[par], weight_t[:]).then_inc(w_stored[par], 16)
                    sp.wait_ge(w_stored[par], pair_count(c, par))
                    sp.dma_start(spread[par][:], w_dram[par].partition_broadcast(P)).then_inc(w_spread[par], 16)

            def ending(name, c, par):
                if name == "f_scale":
                    sp.wait_ge(f_dve, count(c, len(F_DVE), nth(F_DVE, "token")))
                    sp.dma_start(out.rearrange("b (t p) d -> p (b t) d", p=P)[:, bass.ds(c * CT, CT), :],
                                 result[par][:]).then_inc(out_stored[par], 16)

            over_chunks(sp, main, routing, ending)
            for s in out_stored:
                sp.wait_ge(s, count(CHUNKS // 2, 16, 0))

        @block.gpsimd
        def _(pool):
            prime(pool, scales, EXPERTS)
            prime(pool, r_rstd, 1)
            prime(pool, f_rstd, 1)
            pool.memset(half[:], -0.5).then_inc(half_made, 1)
            pool.wait_ge(half_made, 1)

            def main(c, par, unit):
                e = unit // 2 + 1
                if unit % 2 or e > EXPERTS:
                    return
                if e == 1:
                    pool.wait_ge(w_spread[par], pair_count(c, par))
                    pool.wait_ge(r_moved, count(c, 1, 1))
                done = count(c, UNITS, 2 * (e - 1)) if e > 2 else count(c - 1, UNITS, 2 * (EXPERTS - 1 + e))
                pool.wait_ge(ups, done)
                pool.tensor_tensor(scaled[e % 2][:], tokens_t[par][:], spread[par][:, e - 1, :],
                                   ALU.mult).then_inc(scales, 1)

            def power(who, steps, dve_sem, rstd_sem, c):
                pool.wait_ge(dve_sem, count(c, len(steps), nth(steps, "var_eps")))
                pool.tensor_tensor(norms[who]["rstd"][:], norms[who]["var"][:], half[:], ALU.pow).then_inc(rstd_sem, 1)

            def routing(name, c, par):
                if name == "r_scale":
                    power("r", R_DVE, r_dve, r_rstd, c)

            def ending(name, c, par):
                if name == "f_scale":
                    power("f", F_DVE, f_dve, f_rstd, c)

            over_chunks(pool, main, routing, ending)

        @block.scalar
        def _(act):
            for s in (r_moved, r_exped, f_moved):
                prime(act, s, 1)
            prime(act, silus, UNITS)

            def main(c, par, unit):
                act.wait_ge(gates, count(c, UNITS, unit + 1))
                act.wait_ge(hiddens, count(c, UNITS, unit - 1))
                act.activation(gated[unit % 2][:], ps_g[unit % 2][:], ACT.Silu).then_inc(silus, 1)

            def routing(name, c, par):
                if name == "r_turn":
                    act.wait_ge(r_turned, count(c, 1, 1))
                    act.wait_ge(ups, count(c - 2, UNITS, UNITS))
                    act.wait_ge(scales, count(c - 2, EXPERTS, EXPERTS))
                    act.activation(tokens_t[par][:], ps_t[:], ACT.Copy).then_inc(r_moved, 1)
                if name == "r_exp":
                    act.wait_ge(r_dve, count(c, len(R_DVE), nth(R_DVE, "logit")))
                    act.activation(route["exp"][:], route["logit"][:], ACT.Exp, scale=-1.0).then_inc(r_exped, 1)

            def ending(name, c, par):
                if name == "f_move":
                    act.wait_ge(downs, count(c, UNITS, UNITS))
                    act.wait_ge(f_turned, count(c, 1, 0))
                    act.activation(y_t[:], ps_y[:], ACT.Copy).then_inc(f_moved, 1)

            over_chunks(act, main, routing, ending)

        @block.vector
        def _(dve):
            prime(dve, r_dve, len(R_DVE))
            prime(dve, f_dve, len(F_DVE))
            prime(dve, hiddens, UNITS)
            dve.wait_ge(st["experts_loaded"], 16 * EXPERT_LOADS)

            def main(c, par, unit):
                dve.wait_ge(silus, count(c, UNITS, unit + 1))
                dve.wait_ge(ups, count(c, UNITS, unit + 1))
                dve.wait_ge(downs, count(c, UNITS, unit - 1))
                dve.tensor_tensor(hidden[unit % 2][:], ps_u[unit % 2][:], gated[unit % 2][:],
                                  ALU.mult).then_inc(hiddens, 1)

            class Steps:
                def __init__(self, steps, semaphore, c):
                    self.steps, self.semaphore, self.c = steps, semaphore, c

                def __call__(self, name, instruction, *operands):
                    dve.wait_ge(self.semaphore, count(self.c, len(self.steps), nth(self.steps, name) - 1))
                    instruction(*operands).then_inc(self.semaphore, 1)

            def center(step, who, first, second):
                n = norms[who]
                wide = [P, CT, D]
                step("sum", dve.tensor_tensor, n["centered"][:], first, second, ALU.add)
                step("mean", dve.tensor_reduce, n["total"][:], n["centered"][:], AX.X, ALU.add)
                step("center", dve.scalar_tensor_tensor, n["centered"][:],
                     n["total"][:].unsqueeze(2).to_broadcast(wide), -1.0 / D, n["centered"][:], ALU.mult, ALU.add)
                step("square", dve.tensor_tensor, n["squares"][:], n["centered"][:], n["centered"][:], ALU.mult)
                step("var", dve.tensor_reduce, n["var"][:], n["squares"][:], AX.X, ALU.add)
                step("var_eps", dve.tensor_scalar, n["var"][:], n["var"][:], 1.0 / D, LN_EPS, ALU.mult, ALU.add)

            def scale(step, who, to):
                step("token", dve.tensor_tensor, to, norms[who]["centered"][:],
                     norms[who]["rstd"][:].unsqueeze(2).to_broadcast([P, CT, D]), ALU.mult)

            def routing(name, c, par):
                step = Steps(R_DVE, r_dve, c)
                r, t = route, tops
                small = [P, CT, EXPERTS]
                wide = lambda ap: ap[:].unsqueeze(2).to_broadcast(small)
                if name == "r_center":
                    dve.wait_ge(x_loaded[par], pair_count(c, par))
                    center(step, "r", x[:, bass.ds(c * CT, CT), :], x_in[par][:])
                if name == "r_scale":
                    dve.wait_ge(r_rstd, count(c, 1, 1))
                    dve.wait_ge(f_dve, count(c - 2, len(F_DVE), nth(F_DVE, "sum")))
                    scale(step, "r", token[par][:])
                if name == "r_logits":
                    dve.wait_ge(r_logits, count(c, 1, 1))
                    step("logit", dve.tensor_tensor, r["logit"][:],
                         ps_r[:, 0:CT * EXPERTS].rearrange("p (t e) -> p t e", e=EXPERTS),
                         bias[:].unsqueeze(1).to_broadcast(small), ALU.add)
                if name == "r_pick":
                    ranks = rank[:].unsqueeze(1).to_broadcast(small)
                    dve.wait_ge(r_exped, count(c, 1, 1))
                    step("one_plus", dve.tensor_scalar, r["one_plus"][:], r["exp"][:], 1.0, None, ALU.add)
                    step("prob", dve.reciprocal, r["prob"][:], r["one_plus"][:])
                    step("top1", dve.tensor_reduce, t["top1"][:], r["prob"][:], AX.X, ALU.max)
                    step("is1", dve.tensor_tensor, r["is_"][:], r["prob"][:], wide(t["top1"]), ALU.is_equal)
                    step("place1", dve.tensor_tensor, r["place"][:], r["is_"][:], ranks, ALU.mult)
                    step("first1", dve.tensor_reduce, t["first"][:], r["place"][:], AX.X, ALU.max)
                    step("pick1", dve.tensor_tensor, r["pick1"][:], r["place"][:], wide(t["first"]), ALU.is_equal)
                    step("others", dve.scalar_tensor_tensor, r["others"][:], r["pick1"][:], -4.0, r["prob"][:],
                         ALU.mult, ALU.add)
                    step("top2", dve.tensor_reduce, t["top2"][:], r["others"][:], AX.X, ALU.max)
                    step("is2", dve.tensor_tensor, r["is_"][:], r["others"][:], wide(t["top2"]), ALU.is_equal)
                    step("place2", dve.tensor_tensor, r["place"][:], r["is_"][:], ranks, ALU.mult)
                    step("first2", dve.tensor_reduce, t["first"][:], r["place"][:], AX.X, ALU.max)
                    step("pick2", dve.tensor_tensor, r["pick2"][:], r["place"][:], wide(t["first"]), ALU.is_equal)
                if name == "r_weights":
                    step("picks", dve.tensor_tensor, r["pick1"][:], r["pick1"][:], r["pick2"][:], ALU.add)
                    step("picked", dve.tensor_tensor, r["pick1"][:], r["pick1"][:], r["prob"][:], ALU.mult)
                    step("total", dve.tensor_tensor, t["total"][:], t["top1"][:], t["top2"][:], ALU.add)
                    step("inverse", dve.reciprocal, t["total"][:], t["total"][:])
                    step("weight", dve.tensor_tensor, r["weight"][:], r["pick1"][:], wide(t["total"]), ALU.mult)
                if name == "r_spread":
                    dve.wait_ge(w_turned, count(c, 1, 1))
                    dve.wait_ge(w_stored[1 - par], pair_count(c - 1, 1 - par))
                    step("moved", dve.tensor_copy, weight_t[:], ps_r[0:EXPERTS, :])

            def ending(name, c, par):
                step = Steps(F_DVE, f_dve, c)
                if name == "f_center":
                    dve.wait_ge(f_turned, count(c, 1, 1))
                    center(step, "f", ps_f[:], token[par][:])
                if name == "f_scale":
                    dve.wait_ge(f_rstd, count(c, 1, 1))
                    dve.wait_ge(out_stored[par], pair_count(c - 2, par))
                    scale(step, "f", result[par][:])

            over_chunks(dve, main, routing, ending)

        @block.tensor
        def _(pe):
            for s in (gates, ups, downs):
                prime(pe, s, UNITS)
            for s in (r_turned, r_logits, w_turned, f_turned):
                prime(pe, s, 1)
            pe.wait_ge(st["experts_loaded"], 16 * EXPERT_LOADS)

            def down(c, unit):
                pe.wait_ge(hiddens, count(c, UNITS, unit + 1))
                if unit == 0:
                    pe.wait_ge(f_moved, count(c, 1, 0))
                pe.matmul(ps_y[:], w_down[:, unit, :], hidden[unit % 2][:], start=(unit == 0),
                          stop=(unit == UNITS - 1)).then_inc(downs, 1)

            def main(c, par, unit):
                if unit == 0:
                    pe.wait_ge(r_moved, count(c, 1, 1))
                pe.wait_ge(silus, count(c, UNITS, unit - 1))
                pe.matmul(ps_g[unit % 2][:], w_gate[:, unit, :], tokens_t[par][:], start=True,
                          stop=True).then_inc(gates, 1)
                e = unit // 2
                if e:
                    pe.wait_ge(scales, count(c, EXPERTS, e))
                pe.wait_ge(hiddens, count(c, UNITS, unit - 1))
                pe.matmul(ps_u[unit % 2][:], w_up[:, unit, :], scaled[e % 2][:] if e else tokens_t[par][:],
                          start=True, stop=True).then_inc(ups, 1)
                if unit:
                    down(c, unit - 1)
                if unit == UNITS - 1:
                    down(c, unit)

            def routing(name, c, par):
                if name == "r_turn":
                    pe.wait_ge(r_dve, count(c, len(R_DVE), nth(R_DVE, "token")))
                    pe.wait_ge(r_moved, count(c, 1, 0))
                    for t in range(CT):
                        last = pe.transpose(ps_t[:, t, :], token[par][:, t, :], ident[:])
                    last.then_inc(r_turned, 1)
                if name == "r_logits":
                    pe.wait_ge(r_moved, count(c, 1, 1))
                    pe.wait_ge(r_dve, count(c - 1, len(R_DVE), nth(R_DVE, "moved")))
                    for t in range(CT):
                        last = pe.matmul(ps_r[:, t * EXPERTS:(t + 1) * EXPERTS],
                                         tokens_t[par][:, t * P:(t + 1) * P], w_router[:], start=True, stop=True)
                    last.then_inc(r_logits, 1)
                if name == "r_weights":
                    pe.wait_ge(r_dve, count(c, len(R_DVE), nth(R_DVE, "weight")))
                    for t in range(CT):
                        last = pe.transpose(ps_r[0:EXPERTS, t * P:(t + 1) * P], route["weight"][:, t, :], ident[:])
                    last.then_inc(w_turned, 1)

            def ending(name, c, par):
                if name == "f_turn":
                    pe.wait_ge(f_moved, count(c, 1, 1))
                    pe.wait_ge(f_dve, count(c - 1, len(F_DVE), nth(F_DVE, "sum")))
                    for t in range(CT):
                        last = pe.transpose(ps_f[:, t, :], y_t[:, t * P:(t + 1) * P], ident[:])
                    last.then_inc(f_turned, 1)

            over_chunks(pe, main, routing, ending)


def setup_phase(nc, ins, st):
    with ExitStack() as ctx:
        down_t = ctx.enter_context(nc.sbuf_tensor("down_t", [32, D], F32))
        up = ctx.enter_context(nc.sbuf_tensor("up", [32, 2 * KV], F32))
        ps_w = ctx.enter_context(nc.psum_tensor("ps_w", [P, 2 * KV], F32))
        loaded, latent_loaded, made, folded = (
            ctx.enter_context(nc.semaphore(n)) for n in ("loaded", "latent_loaded", "made", "folded"))
        block = ctx.enter_context(nc.Block())
        loads = [
            (st["x"][:], ins["hidden"].rearrange("b (t p) d -> p (b t) d", p=P)),
            (st["wall"][0][:, 0:D], ins["g_wq"]),
            (st["wall"][1][:], ins["l_wqkv"]),
            (st["wo"][0][:], ins["g_wo"]),
            (st["wo"][1][:], ins["l_wo"]),
            (st["norm_w"][0][:], ins["norm1_w"].rearrange("(p a) -> p a", a=1)),
            (st["norm_w"][1][:], ins["norm2_w"].rearrange("(p a) -> p a", a=1)),
            (st["cos"][0][:], ins["cos_g"].rearrange("(t p) d -> p t d", p=P)),
            (st["sin"][0][:], ins["sin_g"].rearrange("(t p) d -> p t d", p=P)),
            (st["cos"][1][:], ins["cos_l"].rearrange("(t p) d -> p t d", p=P)),
            (st["sin"][1][:], ins["sin_l"].rearrange("(t p) d -> p t d", p=P)),
        ]

        @block.sync
        def _(sp):
            sp.dma_start(down_t[:], ins["g_kv_down_t"]).then_inc(latent_loaded, 16)
            sp.dma_start(up[:], ins["g_kv_up"]).then_inc(latent_loaded, 16)
            for to, of in loads:
                sp.dma_start(to, of).then_inc(loaded, 16)
            sp.wait_ge(loaded, 16 * len(loads))

        @block.scalar
        def _(act):
            for to, of in ((st["w_gate"], ins["w_gate"]), (st["w_up"], ins["w_up"]), (st["w_down"], ins["w_down"]),
                           (st["w_router"], ins["w_router"]), (st["bias"], ins["bias"].partition_broadcast(P)),
                           (st["rank"], ins["rank"].partition_broadcast(P))):
                act.dma_start(to[:], of).then_inc(st["experts_loaded"], 16)

        @block.gpsimd
        def _(pool):
            pool.memset(st["ident"][:], 0.0).then_inc(made, 1)
            pool.memset(st["ident_bf"][:], 0.0).then_inc(made, 1)
            pool.memset(st["rms_eps"][:], RMS_EPS).then_inc(made, 1)
            pool.wait_ge(made, 3)
            for m in ("ident", "ident_bf"):
                pool.affine_select(out=st[m][:], in_=st[m][:], compare_op=ALU.not_equal, fill=1.0, base=0,
                                   pattern=[[-1, P]], channel_multiplier=1).then_inc(made, 1)
            pool.wait_ge(made, 5)

        @block.tensor
        def _(pe):
            pe.wait_ge(latent_loaded, 32)
            pe.matmul(ps_w[:], down_t[:], up[:], start=True, stop=True).then_inc(folded, 1)

        @block.vector
        def _(dve):
            dve.wait_ge(folded, 1)
            dve.tensor_copy(st["wall"][0][:, D:PROJ], ps_w[:]).then_inc(folded, 1)
            dve.wait_ge(folded, 2)


def program(nc, ins, out):
    with ExitStack() as ctx:
        def sb(name, shape, dt=F32):
            return ctx.enter_context(nc.sbuf_tensor(name, shape, dt))

        st = {
            "x": sb("x", [P, TILES, D]),
            "ident": sb("ident", [P, P]), "ident_bf": sb("ident_bf", [P, P], BF16),
            "rms_eps": sb("rms_eps", [P, 1]),
            "wall": [sb(f"wall{n}", [P, PROJ]) for n in range(2)],
            "wo": [sb(f"wo{n}", [P, D]) for n in range(2)],
            "norm_w": [sb(f"norm_w{n}", [P, 1]) for n in range(2)],
            "cos": [sb(f"cos{n}", [P, TPB, HD]) for n in range(2)],
            "sin": [sb(f"sin{n}", [P, TPB, HD]) for n in range(2)],
        }
        st.update(
            w_gate=sb("w_gate", [P, UNITS, P]), w_up=sb("w_up", [P, UNITS, P]), w_down=sb("w_down", [P, UNITS, P]),
            w_router=sb("w_router", [P, EXPERTS]), bias=sb("bias", [P, EXPERTS]), rank=sb("rank", [P, EXPERTS]),
            experts_loaded=ctx.enter_context(nc.semaphore("experts_loaded")),
            hidden_tiles=ins["hidden"].rearrange("b (t p) d -> p (b t) d", p=P))
        setup_phase(nc, ins, st)
        for n, tag in enumerate(("global", "local")):
            with ExitStack() as layer:
                one = dict(st, **{k: st[k][n] for k in ("wall", "wo", "norm_w", "cos", "sin")})
                one["v_all"] = layer.enter_context(nc.sbuf_tensor(f"v_all_{tag}", [P, TILES, KV], F32))
                one["q_dram"] = nc.dram_tensor(f"q_parts_{tag}", [B, PARTS, HEADS * HD, S], BF16).ap()
                one["k_dram"] = nc.dram_tensor(f"k_parts_{tag}", [B, PARTS * KV, S], BF16).ap()
                prepare_phase(nc, tag, one)
                attention_phase(nc, tag, one, local=(n == 1))
        expert_phase(nc, ins, out, st)


def rotary(base):
    import numpy as np

    inv_freq = np.float32(1.0) / np.float32(base) ** (np.arange(0, HD, 2, dtype=np.float32) / np.float32(HD))
    angle = np.arange(S, dtype=np.float32)[:, None] * inv_freq[None, :].astype(np.float32)
    cos, sin = np.cos(angle), np.sin(angle)
    return np.repeat(cos, 2, axis=1), np.stack([-sin, sin], axis=-1).reshape(S, HD)


def kernel(**inputs):
    import numpy as np
    import concourse.bacc as bacc
    from concourse.bass_utils import run_bass_kernel_spmd

    a = {k.replace("L0_attn_", "").replace("L0_ffn_", ""): np.asarray(v) for k, v in inputs.items()}
    cos_g, sin_g = rotary(1000000.0)
    cos_l, sin_l = rotary(10000.0)

    def slices(shared, routed):
        return np.concatenate([shared[None], routed]).reshape(UNITS, P, D).transpose(2, 0, 1)

    down = np.concatenate([a["sd_w"][None], a["wd"]]).reshape(1 + EXPERTS, D, FF // P, P)
    arrays = {
        "hidden": a["hidden"], "norm1_w": a["norm1_w"], "norm2_w": a["norm2_w"],
        "g_wq": a["g_wq"], "g_kv_down_t": a["g_kv_down"].T,
        "g_kv_up": np.concatenate([a["g_k_up"], a["g_v_up"]], axis=1), "g_wo": a["g_wo"],
        "l_wqkv": np.concatenate([a["l_wq"], a["l_wk"], a["l_wv"]], axis=1), "l_wo": a["l_wo"],
        "cos_g": cos_g, "sin_g": sin_g, "cos_l": cos_l, "sin_l": sin_l,
        "w_gate": slices(a["sg_w"], a["wg"]), "w_up": slices(a["su_w"], a["wu"]),
        "w_down": down.transpose(3, 0, 2, 1).reshape(P, UNITS, D),
        "w_router": a["router_w"].T, "bias": a["routing_bias"],
        "rank": np.arange(EXPERTS, 0, -1).astype(np.float32),
    }
    arrays = {f"in_{k}": np.ascontiguousarray(v) for k, v in arrays.items()}
    nc = bacc.Bacc("TRN2", target_bir_lowering=False, num_devices=1)
    ins = {k[3:]: nc.dram_tensor(k, v.shape, mybir.dt.from_np(v.dtype), kind="ExternalInput").ap()
           for k, v in arrays.items()}
    out = nc.dram_tensor("out", (B, S, D), F32, kind="ExternalOutput").ap()
    program(nc, ins, out)
    return run_bass_kernel_spmd(nc, [arrays], core_ids=[0]).results[0]["out"]
```

```python
from contextlib import ExitStack

import concourse.bass as bass
from concourse import mybir

F32 = mybir.dt.float32
U32 = mybir.dt.uint32
BF16 = mybir.dt.bfloat16
ALU = mybir.AluOpType
ACT = mybir.ActivationFunctionType
AX = mybir.AxisListType

P = 128
D = 128
HEADS, GROUPS, HD = 16, 4, 8
REP = HEADS // GROUPS
B, S = 4, 1024
TPB = S // P
TILES = B * TPB
WINDOW = 32
CT = 4
CN = CT * P
CHUNKS = TILES // CT
QK = (HEADS + GROUPS) * HD
KV = GROUPS * HD
PROJ = QK + KV
PARTS = 3
ROWS = PARTS * PARTS * HD
KPAD = 96
VW = 32
EXPERTS, FF = 8, 256
UNITS = (1 + EXPERTS) * FF // P
EXPERT_LOADS = 7
RMS_EPS, LN_EPS = 1e-6, 1e-5
BANK = 512
SLOT = 3
NPROB = 4
PV_LAG = 3


AHEAD = 2


def count(unit, per, nth):
    return (unit + AHEAD) * per + nth


def pair_count(c, par):
    return (c - par) * 8 + (AHEAD + 1) * 16


def prime(engine, semaphore, per):
    engine.nop().then_inc(semaphore, AHEAD * per)


def nth(steps, name):
    return steps.index(name) + 1


def in_step(engine, stages):
    first, last = -max(ahead for _, ahead in STAGES), CHUNKS - 1 - min(ahead for _, ahead in STAGES)
    begin, end = -min(ahead for _, ahead in STAGES), CHUNKS - max(ahead for _, ahead in STAGES)

    def step(k, base, checked):
        for fn, ahead in stages:
            if not checked or 0 <= k + ahead < CHUNKS:
                fn(base + (k + ahead), (k + ahead) % 2)

    for k in range(first, begin):
        step(k, 0, True)
    with engine.Fori(0, (end - begin) // 2) as i:
        for k in range(begin, begin + 2):
            step(k, i * 2, False)
    for k in range(begin + (end - begin) // 2 * 2, last + 1):
        step(k, 0, True)


STAGES = [("scale_tokens", 3), ("project", 2), ("move_tokens", 2), ("rotate", 1), ("add_rope", 1),
          ("square_heads", 1), ("sum_heads", 0), ("root_heads", 0), ("normalise", 0),
          ("turn_parts", -1), ("move_parts", -1)]
AHEAD_OF = dict(STAGES)


def prepare_phase(nc, tag, st):
    x, wall, norm_w, cos, sin = st["x"], st["wall"], st["norm_w"], st["cos"], st["sin"]
    ident, ident_bf, eps, v_all, q_dram, k_dram = (
        st["ident"], st["ident_bf"], st["rms_eps"], st["v_all"], st["q_dram"], st["k_dram"])
    ROPE = ["cosine", "sine_even", "sine_odd", "values"]
    NORM = ["head_sum", "head_scale", "normed", "part1", "rest", "part2", "part3"]
    with ExitStack() as ctx:
        def sb(name, shape, dt=F32):
            return ctx.enter_context(nc.sbuf_tensor(f"{name}_{tag}", shape, dt))

        def ps(name, shape, dt=F32):
            return ctx.enter_context(nc.psum_tensor(f"{name}_{tag}", shape, dt))

        def sem(name):
            return ctx.enter_context(nc.semaphore(f"{name}_{tag}"))

        sq = [sb(f"sq{p}", [P, TPB, D]) for p in range(2)]
        rs = sb("rs", [P, TILES])
        xn = [sb(f"xn{p}", [P, CT, D]) for p in range(2)]
        xt = [sb(f"xt{p}", [P, CN]) for p in range(2)]
        tcos = [sb(f"tcos{p}", [P, CT * QK]) for p in range(2)]
        tsin = [sb(f"tsin{p}", [P, CT * QK]) for p in range(2)]
        roped = [sb(f"roped{p}", [P, CT * QK]) for p in range(2)]
        sqh = [sb(f"sqh{p}", [P, CT * QK]) for p in range(2)]
        hs = [sb(f"hs{p}", [P, CT * QK // HD]) for p in range(2)]
        hr = [sb(f"hr{p}", [P, CT * QK // HD]) for p in range(2)]
        hi = [sb(f"hi{p}", [P, CT * QK // HD]) for p in range(2)]
        part = [[sb(f"part{i}_{p}", [P, CT * QK], BF16) for i in range(PARTS)] for p in range(2)]
        zq = [sb(f"zq{p}", [P, PARTS, CN], BF16) for p in range(2)]
        zk = [sb(f"zk{p}", [PARTS * KV, CN], BF16) for p in range(2)]
        ps_x = [ps(f"ps_x{p}", [P, CT, D]) for p in range(2)]
        ps_p = [ps(f"ps_p{p}", [P, CT, 256]) for p in range(2)]
        ps_z = [ps(f"ps_z{p}", [P, 2, PARTS + 1, P], BF16) for p in range(2)]

        squared, summed, rooted, rs_ready = sem("squared"), sem("summed"), sem("rooted"), sem("rs_ready")
        xn_ready, xt_turned, xt_ready = sem("xn_ready"), sem("xt_turned"), sem("xt_ready")
        projected, rope, roped_ready, head_squared = (
            sem("projected"), sem("rope"), sem("roped_ready"), sem("head_squared"))
        head_rooted, norm, turned, parts_out = (
            sem("head_rooted"), sem("norm"), sem("turned"), sem("parts_out"))
        stored = [sem(f"stored{p}") for p in range(2)]

        def heads(ap):
            return ap.rearrange("p (n d) -> p n d", d=HD)

        block = ctx.enter_context(nc.Block())

        @block.gpsimd
        def _(pool):
            def scale_tokens(c, par):
                pool.wait_ge(xt_turned, count(c, 1, -1))
                pool.tensor_tensor(xn[par][:], x[:, bass.ds(c * CT, CT), :],
                                   rs[:, bass.ds(c * CT, CT)].unsqueeze(2).to_broadcast([P, CT, D]),
                                   ALU.mult).then_inc(xn_ready, 1)

            def add_rope(c, par):
                pool.wait_ge(rope, count(c, len(ROPE), nth(ROPE, "sine_odd")))
                pool.wait_ge(head_squared, count(c, 1, -1))
                pool.wait_ge(norm, count(c - 2, len(NORM), nth(NORM, "normed")))
                pool.tensor_tensor(roped[par][:], tcos[par][:], tsin[par][:], ALU.add).then_inc(roped_ready, 1)

            prime(pool, xn_ready, 1)
            prime(pool, roped_ready, 1)
            pool.wait_ge(rs_ready, 1)
            in_step(pool, [(fn, AHEAD_OF[fn.__name__]) for fn in (add_rope, scale_tokens)])

        @block.vector
        def _(dve):
            prime(dve, rope, len(ROPE))
            prime(dve, norm, len(NORM))
            for b in range(B):
                dve.wait_ge(squared, b + 1)
                dve.tensor_reduce(rs[:, b * TPB:(b + 1) * TPB], sq[b % 2][:], AX.X, ALU.add).then_inc(summed, 1)
            dve.wait_ge(rooted, 1)
            dve.reciprocal(rs[:], rs[:]).then_inc(rs_ready, 1)

            def rotate(c, par):
                dve.wait_ge(projected, count(c, 1, 1))
                dve.wait_ge(roped_ready, count(c, 1, -1))
                dve.wait_ge(norm, count(c - 2, len(NORM), nth(NORM, "part3")))
                pq = ps_p[par][:, :, 0:QK]
                half = pq.rearrange("p t (h i two) -> p t h i two", i=HD // 2, two=2)
                cs = cos[:, par * CT:(par + 1) * CT, :].unsqueeze(2).to_broadcast([P, CT, QK // HD, HD])
                dve.tensor_tensor(tcos[par][:].rearrange("p (t h d) -> p t h d", t=CT, d=HD),
                                  pq.rearrange("p t (h d) -> p t h d", d=HD), cs, ALU.mult).then_inc(rope, 1)
                out = tsin[par][:].rearrange("p (t h i two) -> p t h i two", t=CT, i=HD // 2, two=2)
                sn = sin[:, par * CT:(par + 1) * CT, :].rearrange("p t (i two) -> p t i two", two=2)
                for to in range(2):
                    dve.tensor_tensor(out[:, :, :, :, to], half[:, :, :, :, 1 - to],
                                      sn[:, :, :, to].unsqueeze(2).to_broadcast([P, CT, QK // HD, HD // 2]),
                                      ALU.mult).then_inc(rope, 1)
                dve.tensor_copy(v_all[:, bass.ds(c * CT, CT), :], ps_p[par][:, :, QK:PROJ]).then_inc(rope, 1)

            def sum_heads(c, par):
                dve.wait_ge(head_squared, count(c, 1, 1))
                dve.wait_ge(head_rooted, count(c, 1, -1))
                dve.tensor_reduce(hs[par][:], heads(sqh[par][:]), AX.X, ALU.add).then_inc(norm, 1)

            def normalise(c, par):
                def done(name):
                    dve.wait_ge(norm, count(c, len(NORM), nth(NORM, name)))
                dve.wait_ge(head_rooted, count(c, 1, 1))
                dve.reciprocal(hi[par][:], hr[par][:]).then_inc(norm, 1)
                done("head_scale")
                dve.tensor_tensor(heads(sqh[par][:]), heads(roped[par][:]),
                                  hi[par][:].unsqueeze(2).to_broadcast([P, CT * QK // HD, HD]),
                                  ALU.mult).then_inc(norm, 1)
                done("normed")
                dve.wait_ge(turned, count(c, 2, -2))
                dve.tensor_copy(part[par][0][:], sqh[par][:]).then_inc(norm, 1)
                done("part1")
                dve.tensor_tensor(tcos[par][:], sqh[par][:], part[par][0][:], ALU.subtract).then_inc(norm, 1)
                done("rest")
                dve.tensor_copy(part[par][1][:], tcos[par][:]).then_inc(norm, 1)
                done("part2")
                dve.tensor_tensor(part[par][2][:], tcos[par][:], part[par][1][:], ALU.subtract).then_inc(norm, 1)

            in_step(dve, [(fn, AHEAD_OF[fn.__name__]) for fn in (sum_heads, rotate, normalise)])

        @block.scalar
        def _(act):
            for s in (xt_ready, head_squared, head_rooted):
                prime(act, s, 1)
            prime(act, parts_out, 4)
            for b in range(B):
                if b >= 2:
                    act.wait_ge(summed, b - 1)
                act.activation(sq[b % 2][:], x[:, b * TPB:(b + 1) * TPB, :], ACT.Square).then_inc(squared, 1)
            act.wait_ge(summed, B)
            act.activation(rs[:], rs[:], ACT.Sqrt, scale=1.0 / D, bias=eps[:]).then_inc(rooted, 1)

            def move_tokens(c, par):
                act.wait_ge(xt_turned, count(c, 1, 1))
                act.wait_ge(projected, count(c, 1, -1))
                act.activation(xt[par][:], ps_x[par][:], ACT.Copy, scale=norm_w[:]).then_inc(xt_ready, 1)

            def square_heads(c, par):
                act.wait_ge(roped_ready, count(c, 1, 1))
                act.wait_ge(norm, count(c - 2, len(NORM), nth(NORM, "rest")))
                act.activation(sqh[par][:], roped[par][:], ACT.Square).then_inc(head_squared, 1)

            def root_heads(c, par):
                act.wait_ge(norm, count(c, len(NORM), nth(NORM, "head_sum")))
                act.activation(hr[par][:], hs[par][:], ACT.Sqrt, scale=1.0 / HD, bias=eps[:]).then_inc(head_rooted, 1)

            def move_parts(c, par):
                act.wait_ge(stored[par], (c - par) * 16 + AHEAD * 32)
                for h in range(2):
                    act.wait_ge(turned, count(c, 2, h + 1))
                    act.activation(zq[par][:].rearrange("p i (t n) -> p t i n", n=P)[:, 2 * h:2 * h + 2],
                                   ps_z[h][:, :, 0:PARTS, :], ACT.Copy).then_inc(parts_out, 1)
                    act.activation(zk[par][:].rearrange("p (t n) -> p t n", n=P)[:, 2 * h:2 * h + 2],
                                   ps_z[h][0:PARTS * KV, :, PARTS, :], ACT.Copy).then_inc(parts_out, 1)

            in_step(act, [(fn, AHEAD_OF[fn.__name__]) for fn in (root_heads, move_tokens, square_heads, move_parts)])

        @block.tensor
        def _(pe):
            for s in (xt_turned, projected):
                prime(pe, s, 1)
            prime(pe, turned, 2)

            def project(c, par):
                pe.wait_ge(xn_ready, count(c, 1, 1))
                pe.wait_ge(xt_ready, count(c, 1, -1))
                for t in range(CT):
                    last = pe.transpose(ps_x[par][:, t, :], xn[par][:, t, :], ident[:])
                last.then_inc(xt_turned, 1)
                pe.wait_ge(xt_ready, count(c, 1, 1))
                pe.wait_ge(rope, count(c - 2, len(ROPE), nth(ROPE, "values")))
                for t in range(CT):
                    last = pe.matmul(ps_p[par][:, t, 0:PROJ], xt[par][:, t * P:(t + 1) * P], wall[:],
                                     start=True, stop=True)
                last.then_inc(projected, 1)

            def turn_parts(c, par):
                pe.wait_ge(norm, count(c, len(NORM), nth(NORM, "part3")))
                for h in range(2):
                    pe.wait_ge(parts_out, count(c, 4, 2 * (h + 1) - 4))
                    for t in range(2):
                        at = (2 * h + t) * QK
                        for i in range(PARTS):
                            pe.transpose(ps_z[h][:, t, i, :], part[par][i][:, at:at + HEADS * HD], ident_bf[:])
                            last = pe.transpose(ps_z[h][i * KV:(i + 1) * KV, t, PARTS, :],
                                                part[par][i][:, at + HEADS * HD:at + QK], ident_bf[:])
                    last.then_inc(turned, 1)

            in_step(pe, [(fn, AHEAD_OF[fn.__name__]) for fn in (project, turn_parts)])

        @block.sync
        def _(sp):
            for s in stored:
                prime(sp, s, 32)

            def store(b, par):
                sp.wait_ge(parts_out, count(b * 2 + par, 4, 4))
                sp.dma_start(q_dram[b, :, :, par * CN:(par + 1) * CN].rearrange("i r n -> r i n"),
                             zq[par][:]).then_inc(stored[par], 16)
                sp.dma_start(k_dram[b, :, par * CN:(par + 1) * CN], zk[par][:]).then_inc(stored[par], 16)

            for b in range(B):
                for par in range(2):
                    store(b, par)
                if 1 <= b <= 2:
                    for s in stored:
                        sp.wait_ge(s, count(b - 1, 32, 32))
                    load_stacks(sp, st, b - 1, b - 1)
            for s in stored:
                sp.wait_ge(s, count(B, 32, 0))


STACK_DMAS = 2 * PARTS * PARTS


def load_stacks(sp, st, b, par):
    for i in range(PARTS):
        for j in range(PARTS):
            rows = slice((i * PARTS + j) * HD, (i * PARTS + j + 1) * HD)
            sp.dma_start(st["qs"][par][rows, :, :],
                         st["q_dram"][b, i].rearrange("(h d) n -> d h n", d=HD)).then_inc(st["stacks"][par], 16)
            sp.dma_start(st["ks"][par][rows, :, :],
                         st["k_dram"][b, j * KV:(j + 1) * KV].rearrange("(g d) n -> d g n", d=HD)
                         ).then_inc(st["stacks"][par], 16)


def slots_of(local):
    slots = []
    for par in range(2):
        if local:
            for qt in range(TPB):
                slots.append([("full", par, qt, qt, g, g * BANK) for g in range(SLOT)])
                last = [("full", par, qt, qt, SLOT, 0)]
                if qt:
                    last.append(("corner", par, qt, qt - 1, None, BANK))
                slots.append(last)
        else:
            flat = [("full", par, qt, kt, g) for qt in range(TPB)
                    for kt in [qt] + list(range(qt)) for g in range(GROUPS)]
            for n in range(0, len(flat), SLOT):
                slots.append([item + (k * BANK,) for k, item in enumerate(flat[n:n + SLOT])])
    return slots


def attention_phase(nc, tag, st, local):
    x, wo, ident, v_all, q_dram, k_dram = (st[k] for k in ("x", "wo", "ident", "v_all", "q_dram", "k_dram"))
    slots = slots_of(local)
    N = len(slots)
    OUTS = 2 * TPB
    q_of = lambda it: it[1] * TPB + it[2]
    first_of, last_of, last_of_batch = {}, {}, {}
    for n, items in enumerate(slots):
        for it in items:
            first_of.setdefault(q_of(it), n)
            last_of[q_of(it)] = n
            last_of_batch[it[1]] = n
    pool_masks, dve_masks, pool_upto, dve_upto = {}, {}, [], []
    for n, items in enumerate(slots):
        diagonal = [it for it in items if it[0] == "full" and it[2] == it[3]]
        if local and len(items) < SLOT:
            pool_masks[n] = items
        elif diagonal:
            dve_masks[n] = diagonal
        pool_upto.append(sum(len(m) for m in pool_masks.values()))
        dve_upto.append(len(dve_masks))
    n_pool, n_dve = pool_upto[-1], dve_upto[-1]

    weighed_upto = [sum(len(items) for items in slots[:n + 1]) for n in range(N)]
    order = [q_of(it) for items in slots for it in items]
    tile_weighed = [len(order) - order[::-1].index(q) for q in range(OUTS)]
    W = len(order)
    turn_step, free_step = [], 0
    for q in range(OUTS):
        turn_step.append(max(last_of[q] + PV_LAG + 1, free_step))
        free_step = turn_step[q] + 2
    steps = turn_step[-1] + 3
    work = [(turn_step[q] + 2, 0, "add", q) for q in range(OUTS)]
    work += [(n + 1, 1, "mask", n) for n in dve_masks]
    work += [(last_of[q] + PV_LAG, 2, "sums", q) for q in range(OUTS)]
    work += [(turn_step[q], 3, "heads", q) for q in range(OUTS)]
    work += [(turn_step[q] + 1, 3, "move", q) for q in range(OUTS)]
    work.sort()
    POST = ["denominators", "heads", "heads_moved", "added"]

    with ExitStack() as ctx:
        def sb(name, shape, dt=F32):
            return ctx.enter_context(nc.sbuf_tensor(f"{name}_{tag}", shape, dt))

        def ps(name, shape, dt=F32):
            return ctx.enter_context(nc.psum_tensor(f"{name}_{tag}", shape, dt))

        def sem(name):
            return ctx.enter_context(nc.semaphore(f"{name}_{tag}"))

        qs, ks, va, vc, stacks = (st[k] for k in ("qs", "ks", "va", "vc", "stacks"))
        prob = [sb(f"prob{n}", [P, SLOT * BANK]) for n in range(NPROB)]
        sums = [sb(f"sums{p}", [P, REP, P]) for p in range(2)]
        rden = sb("rden", [P, REP, GROUPS])
        on = sb("on", [P, GROUPS, REP, HD])
        ot = sb("ot", [P, P])
        band = sb("band", [P, P])
        edge = sb("edge", [P, WINDOW]) if local else None
        ps_s = [ps(f"ps_s{n}", [P, SLOT * BANK]) for n in range(2)]
        ps_v = ps("ps_v", [P, REP, P])
        ps_m = ps("ps_m", [P, REP, P])

        masks_made, values, rows_cleared = sem("masks_made"), sem("values"), sem("rows_cleared")
        corners = [sem(f"corners{p}") for p in range(2)]
        scored, exped, masked, masked_dve, weighed = (
            sem("scored"), sem("exped"), sem("masked"), sem("masked_dve"), sem("weighed"))
        post, sums_out, sums_turned, heads_turned, y_ready = (
            sem("post"), sem("sums_out"), sem("sums_turned"), sem("heads_turned"), sem("y_ready"))

        def post_value(pair, q, name):
            return count(pair * OUTS + q, len(POST), nth(POST, name))

        block = ctx.enter_context(nc.Block())

        @block.sync
        def _(sp):
            for s in corners:
                prime(sp, s, GROUPS * 16)
            if not local:
                clear = st["x_rows"].rearrange("(p n) d -> p (n d)", p=P).rearrange("p (a n) -> p a n", n=CN)
                sp.dma_start(clear, st["zeros"][:].unsqueeze(1).to_broadcast([P, clear.shape[1], CN])
                             ).then_inc(rows_cleared, 16)

            def copy_corners(pair, par):
                sp.wait_ge(values, count(pair, 2, par + 1))
                for g in range(GROUPS):
                    sp.dma_start(vc[par][g * WINDOW:(g + 1) * WINDOW, :, g, :],
                                 va[par][P - WINDOW:P, :, g, :]).then_inc(corners[par], 16)

            for pair in range(B // 2):
                for par in range(2):
                    if pair:
                        sp.wait_ge(weighed, count(pair - 1, W, weighed_upto[last_of_batch[par]]))
                        load_stacks(sp, st, pair * 2 + par, par)
                    if local:
                        copy_corners(pair, par)

            if not local:
                sp.wait_ge(rows_cleared, 16)

        @block.gpsimd
        def _(pool):
            prime(pool, values, 2)
            prime(pool, masked, max(n_pool, 1))
            pool.memset(band[:], 1.0).then_inc(masks_made, 1)
            if local:
                pool.memset(edge[:], 1.0).then_inc(masks_made, 1)
            made = 2 if local else 1
            pool.wait_ge(masks_made, made)
            pool.affine_select(out=band[:], in_=band[:], compare_op=ALU.is_ge, fill=0.0, base=0,
                               pattern=[[1, P]], channel_multiplier=-1).then_inc(masks_made, 1)
            made += 1
            if local:
                pool.wait_ge(masks_made, made)
                pool.affine_select(out=band[:], in_=band[:], compare_op=ALU.is_ge, fill=0.0, base=WINDOW - 1,
                                   pattern=[[-1, P]], channel_multiplier=1).then_inc(masks_made, 1)
                for g in range(GROUPS):
                    pool.wait_ge(masks_made, made + 1 + g)
                    rows = edge[g * WINDOW:(g + 1) * WINDOW, :]
                    pool.affine_select(out=rows, in_=rows, compare_op=ALU.is_gt, fill=0.0, base=0,
                                       pattern=[[-1, WINDOW]], channel_multiplier=1).then_inc(masks_made, 1)
                made += 1 + GROUPS
            pool.wait_ge(masks_made, made)
            with pool.Fori(0, B // 2) as pair:
                for par in range(2):
                    pool.wait_ge(weighed, count(pair - 1, W, weighed_upto[last_of_batch[par]]))
                    if local:
                        pool.wait_ge(corners[par], count(pair, GROUPS * 16, 0))
                    pool.tensor_copy(va[par][:, :, :, 0:HD],
                                     v_all[:, bass.ds((pair * 2 + par) * TPB, TPB), :].rearrange(
                                         "p t (g d) -> p t g d", d=HD)).then_inc(values, 1)
                    for n in sorted(pool_masks):
                        items = pool_masks[n]
                        if items[0][1] != par:
                            continue
                        pool.wait_ge(exped, count(pair, N, n + 1))
                        for it in items:
                            full = it[0] == "full"
                            mask, width = (band, P) if full else (edge, WINDOW)
                            region = prob[n % NPROB][:, it[5]:it[5] + REP * width].rearrange(
                                "p (r q) -> p r q", r=REP)
                            pool.tensor_tensor(region, region, mask[:].unsqueeze(1).to_broadcast([P, REP, width]),
                                               ALU.mult).then_inc(masked, 1)

        @block.scalar
        def _(act):
            prime(act, exped, N)
            with act.Fori(0, B // 2) as pair:
                for n, items in enumerate(slots):
                    act.wait_ge(scored, count(pair, N, n + 1))
                    act.wait_ge(weighed, count(pair, W, weighed_upto[n - NPROB] if n >= NPROB
                                               else weighed_upto[n - NPROB] - W))
                    width = sum(REP * (P if it[0] == "full" else WINDOW) for it in items)
                    act.activation(prob[n % NPROB][:, 0:width], ps_s[n % 2][:, 0:width], ACT.Exp,
                                   scale=HD ** -0.5).then_inc(exped, 1)

        @block.vector
        def _(dve):
            prime(dve, post, len(POST))
            prime(dve, sums_out, OUTS)
            prime(dve, masked_dve, max(n_dve, 1))
            dve.wait_ge(masks_made, 2 + 2 + GROUPS if local else 2)

            def sums_of(pair, q):
                dve.wait_ge(weighed, count(pair, W, tile_weighed[q]))
                dve.wait_ge(sums_turned, count(pair, OUTS, q - 1))
                dve.tensor_copy(sums[q % 2][:], ps_v[:]).then_inc(sums_out, 1)

            def heads_of(pair, q):
                dve.wait_ge(sums_turned, count(pair, OUTS, q + 1))
                by_group = ps_m[:].rearrange("p r (g v) -> p r g v", v=VW)
                dve.reciprocal(rden[:], by_group[:, :, :, HD]).then_inc(post, 1)
                dve.wait_ge(post, post_value(pair, q, "denominators"))
                dve.tensor_tensor(on[:].rearrange("p g r d -> p r g d"), by_group[:, :, :, 0:HD],
                                  rden[:].unsqueeze(3).to_broadcast([P, REP, GROUPS, HD]),
                                  ALU.mult).then_inc(post, 1)

            def move_heads(pair, q):
                dve.wait_ge(heads_turned, count(pair, OUTS, q + 1))
                dve.tensor_copy(ot[:], ps_m[:, 0, :]).then_inc(post, 1)

            def add_tokens(pair, q):
                dve.wait_ge(y_ready, count(pair, OUTS, q + 1))
                tile = x[:, bass.ds(pair * OUTS + q, 1), :]
                dve.tensor_tensor(tile, tile, ps_m[:, 1:2, :], ALU.add).then_inc(post, 1)

            def mask_slot(pair, n):
                dve.wait_ge(exped, count(pair, N, n + 1))
                at, width = dve_masks[n][0][5], len(dve_masks[n]) * REP
                region = prob[n % NPROB][:, at:at + width * P].rearrange("p (r q) -> p r q", q=P)
                dve.tensor_tensor(region, region, band[:].unsqueeze(1).to_broadcast([P, width, P]),
                                  ALU.mult).then_inc(masked_dve, 1)

            do = {"sums": sums_of, "heads": heads_of, "move": move_heads, "add": add_tokens, "mask": mask_slot}
            with dve.Fori(0, B // 2) as pair:
                for _, _, what, which in work:
                    do[what](pair, which)

        @block.tensor
        def _(pe):
            prime(pe, scored, N)
            prime(pe, weighed, W)
            for s in (sums_turned, heads_turned, y_ready):
                prime(pe, s, OUTS)

            def score(pair, n):
                par = slots[n][0][1]
                if n == 0 or slots[n - 1][0][1] != par:
                    pe.wait_ge(stacks[par], (pair + (1 + st["pairs_before"])) * (STACK_DMAS * 16))
                pe.wait_ge(exped, count(pair, N, n - 1))
                for kind, _, qt, kt, g, at in slots[n]:
                    if kind == "full":
                        last = pe.matmul(ps_s[n % 2][:, at:at + REP * P].rearrange("p (r q) -> p r q", q=P),
                                         ks[par][:, g, kt * P:(kt + 1) * P],
                                         qs[par][:, g * REP:(g + 1) * REP, qt * P:(qt + 1) * P],
                                         start=True, stop=True)
                        continue
                    for h in range(GROUPS):
                        last = pe.matmul(ps_s[n % 2][h * WINDOW:(h + 1) * WINDOW,
                                                     at:at + REP * WINDOW].rearrange("p (r q) -> p r q", r=REP),
                                         ks[par][:, h, (kt + 1) * P - WINDOW:(kt + 1) * P],
                                         qs[par][:, h * REP:(h + 1) * REP, qt * P:qt * P + WINDOW],
                                         start=True, stop=True)
                last.then_inc(scored, 1)

            def weigh(pair, m):
                par = slots[m][0][1]
                if m == 0 or slots[m - 1][0][1] != par:
                    pe.wait_ge(values, count(pair, 2, par + 1))
                    if local:
                        pe.wait_ge(corners[par], count(pair, GROUPS * 16, GROUPS * 16))
                pe.wait_ge(exped, count(pair, N, m + 1))
                if m in pool_masks:
                    pe.wait_ge(masked, count(pair, n_pool, pool_upto[m]))
                if m in dve_masks:
                    pe.wait_ge(masked_dve, count(pair, n_dve, dve_upto[m]))
                for it in slots[m]:
                    kind, _, qt, kt, g, at = it
                    q = q_of(it)
                    first = kt == qt
                    if first and g == 0:
                        pe.wait_ge(sums_out, count(pair, OUTS, q))
                    if kind == "full":
                        pe.matmul(ps_v[g * VW:(g + 1) * VW, :, :], va[par][:, kt, g, :],
                                         prob[m % NPROB][:, at:at + REP * P].rearrange("p (r q) -> p r q", q=P),
                                         start=first, stop=(qt == 0 if local else kt == max(qt - 1, 0))
                                         ).then_inc(weighed, 1)
                        continue
                    for h in range(GROUPS):
                        last = pe.matmul(ps_v[h * VW:(h + 1) * VW, :, 0:WINDOW], vc[par][:, kt, h, :],
                                         prob[m % NPROB][:, at:at + REP * WINDOW].rearrange(
                                             "p (r q) -> p r q", r=REP), start=False, stop=True)
                    last.then_inc(weighed, 1)

            def turn_sums(pair, q):
                pe.wait_ge(sums_out, count(pair, OUTS, q + 1))
                pe.wait_ge(post, post_value(pair, q - 1, "added"))
                for r in range(REP):
                    last = pe.transpose(ps_m[:, r, :], sums[q % 2][:, r, :], ident[:])
                last.then_inc(sums_turned, 1)

            def turn_heads(pair, q):
                pe.wait_ge(post, post_value(pair, q, "heads"))
                pe.transpose(ps_m[:, 0, :], on[:].rearrange("p g r d -> p (g r d)"), ident[:]
                             ).then_inc(heads_turned, 1)

            def project(pair, q):
                pe.wait_ge(post, post_value(pair, q, "heads_moved"))
                pe.matmul(ps_m[:, 1, :], ot[:], wo[:], start=True, stop=True).then_inc(y_ready, 1)

            with pe.Fori(0, B // 2) as pair:
                for n in range(steps):
                    if n - 2 in turn_step:
                        project(pair, turn_step.index(n - 2))
                    if n < N:
                        score(pair, n)
                    if 0 <= n - PV_LAG < N:
                        weigh(pair, n - PV_LAG)
                    if n in turn_step:
                        turn_sums(pair, turn_step.index(n))
                    if n - 1 in turn_step:
                        turn_heads(pair, turn_step.index(n - 1))


HALVES = 2
HT = TILES // HALVES
HC = CHUNKS // HALVES
BLOCKS = 2 * HT + EXPERTS
PAIRS = HALVES * BLOCKS // 2
SHARED = HT // 2
FIRST_ROUTED, FIRST_LAST = SHARED, SHARED + PAIRS
ALL_PAIRS = FIRST_LAST + SHARED
SCAN = 8
RING = 4
LOOPS = {SHARED + 6: 5}
BEGIN_AT = {c: -10 + c for c in range(HC)} | dict(zip(range(HC, CHUNKS), (0, 1, 3, 4)))
PICK_AT = {0: {"logit": -4, "first": -3, "second": -3, "ranks": -2, "slots": -2, "blocks": -1, "weights": -1},
           1: {"logit": 7, "first": 8, "second": 9, "ranks": 10, "slots": 11, "blocks": 12, "weights": 13}}
END_AT = {f: SHARED + 26 + 4 * f for f in range(HC)} | dict(zip(range(HC, CHUNKS), (53, 56, 58, 60)))
STEPS = range(-10, 64)


def at_every_step(engine, work):
    step = STEPS[0]
    while step in STEPS:
        if step in LOOPS:
            with engine.Fori(0, LOOPS[step]) as i:
                for k in range(RING):
                    work(step + k, i)
            step += RING * LOOPS[step]
        else:
            work(step, 0)
            step += 1


def at(table, step, after=0):
    return [c for c, begin in table.items() if begin + after == step]


def expert_phase(nc, ins, out, st):
    x, ident = st["x"], st["ident"]
    w_gate_up, w_down, w_router, bias, rank = (
        st[k] for k in ("w_gate_up", "w_down", "w_router", "bias", "rank"))
    R_DVE = ["sum", "mean", "center"]
    R_VAR = ["var", "var_eps"]
    P_DVE = ["logit", "one_plus", "prob", "top1", "is1", "place1", "first1", "pick1", "others",
             "top2", "is2", "place2", "first2", "pick2", "picks",
             "totals", "scan1", "scan2", "scan4", "scan8", "over", "blocks", "ends", "ends1", "ends2",
             "ends4", "base", "slot", "slot_start", "chosen1", "slot1", "chosen2", "slot2",
             "index1", "index2", "past", "expert", "table", "total", "inverse", "weight1", "weight2"]
    F_DVE = ["weighted1", "sum1", "weighted2", "sum2", "mean", "center", "var", "var_eps", "result"]
    with ExitStack() as ctx:
        def sb(name, shape, dt=F32):
            return ctx.enter_context(nc.sbuf_tensor(name, shape, dt))

        def ps(name, shape, dt=F32):
            return ctx.enter_context(nc.psum_tensor(name, shape, dt))

        def sem(name):
            return ctx.enter_context(nc.semaphore(name))

        x_in = sb("x_in", [P, TILES, D])
        token = sb("token", [P, TILES, D])
        tokens_t = sb("tokens_t", [P, TILES * P])
        acc = sb("acc", [P, TILES, D])
        centered = [sb(f"centered{p}", [P, CT, D]) for p in range(2)]
        squares = [sb(f"squares{p}", [P, CT, D]) for p in range(2)]
        total, var, rstd = ([sb(f"{n}{p}", [P, CT]) for p in range(2)] for n in ("total", "var", "rstd"))
        half = sb("half", [P, CT])
        small = {n: sb(f"route_{n}", [P, HT, EXPERTS]) for n in
                 ("logit", "exp", "one_plus", "prob", "is_", "place", "pick1", "others", "pick2", "picks",
                  "slot", "chosen")}
        tops = {n: sb(f"tops_{n}", [P, HT]) for n in ("top1", "first", "top2", "total", "slot1", "slot2")}
        scan = [sb(f"scan{p}", [P, SCAN + HT, EXPERTS]) for p in range(2)]
        over = sb("over", [P, EXPERTS, HT])
        ends = [sb(f"ends{p}", [P, 4 + EXPERTS]) for p in range(2)]
        base, blocks = sb("base", [P, EXPERTS]), sb("blocks", [P, EXPERTS])
        past, expert = sb("past", [P, BLOCKS, EXPERTS]), sb("expert", [P, BLOCKS])
        table = sb("table", [P, HALVES * BLOCKS], U32)
        index = sb("index", [P, TILES, 2], U32)
        weight = sb("weight", [P, TILES, 2])
        earlier, ones = sb("earlier", [P, P]), sb("ones", [P, P])
        rows = [sb(f"rows{p}", [P, 2, D]) for p in range(RING)]
        rows_t = [sb(f"rows_t{p}", [P, 2 * P]) for p in range(2)]
        gated = [sb(f"gated{p}", [P, 2, FF]) for p in range(2)]
        hidden = [sb(f"hidden{p}", [P, 2, FF]) for p in range(2)]
        hidden_t = [sb(f"hidden_t{p}", [P, 2, 2, P]) for p in range(2)]
        y = [sb(f"y{p}", [P, 2, D]) for p in range(RING)]
        gathered_y = [[sb(f"gathered_y{k}_{p}", [P, CT * D]) for k in range(2)] for p in range(2)]
        ending = [sb(f"ending{p}", [P, CT, D]) for p in range(2)]
        end_squares = [sb(f"end_squares{p}", [P, CT, D]) for p in range(2)]
        end_total, end_var, end_rstd = (
            [sb(f"{n}{p}", [P, CT]) for p in range(2)] for n in ("end_total", "end_var", "end_rstd"))
        result = [sb(f"result{p}", [P, CT, D]) for p in range(2)]
        x_rows = st["x_rows"]
        y_rows = nc.dram_tensor("y_rows", [HALVES * BLOCKS * P, D], F32).ap()
        ps_gu = [ps(f"ps_gu{p}", [P, 2, 2 * FF]) for p in range(2)]
        ps_h = ps("ps_h", [P, 2, 2, P])
        ps_y = ps("ps_y", [P, CT, D])
        ps_x = ps("ps_x", [P, CT, D])
        ps_r = ps("ps_r", [P, 4, HT, EXPERTS])

        x_loaded = [sem(f"x_loaded{c}") for c in range(CHUNKS)]
        const, r_dve, r_var, r_squared, r_rstd, r_token, r_turned, r_moved, r_logits = (
            sem(n) for n in ("const", "r_dve", "r_var", "r_squared", "r_rstd", "r_token", "r_turned", "r_moved", "r_logits"))
        p_dve, p_exped, p_ranked, dispatched = (sem(n) for n in ("p_dve", "p_exped", "p_ranked", "dispatched"))
        rows_loaded, y_stored = ([sem(f"{n}{p}") for p in range(RING)] for n in ("rows_loaded", "y_stored"))
        rows_turned, rows_moved = sem("rows_turned"), sem("rows_moved")
        gates, silus, hiddens, h_turned, h_moved, downs, y_out = (
            sem(n) for n in ("gates", "silus", "hiddens", "h_turned", "h_moved", "downs", "y_out"))
        gathered, out_stored = ([sem(f"{n}{p}") for p in range(2)] for n in ("gathered", "out_stored"))
        f_dve, f_squared, f_rstd = sem("f_dve"), sem("f_squared"), sem("f_rstd")

        def picked(h, name):
            return h * len(P_DVE) + nth(P_DVE, name)

        def routed(pair):
            return FIRST_ROUTED <= pair < FIRST_LAST

        def first_tile(pair):
            return 2 * pair if pair < SHARED else 2 * (pair - PAIRS)

        def ring_value(m, i):
            return (m // RING + i) * 16 + 32

        block = ctx.enter_context(nc.Block())

        @block.sync
        def _(sp):
            for c in range(CHUNKS):
                sp.dma_start(x_in[:, c * CT:(c + 1) * CT, :], st["hidden_tiles"][:, c * CT:(c + 1) * CT, :]
                             ).then_inc(x_loaded[c], 16)
            for s in rows_loaded:
                sp.nop().then_inc(s, 16)
            for h in range(HALVES):
                sp.wait_ge(dispatched, (h + 1) * 2 * HT * 16)
                with sp.Fori(0, BLOCKS // 2 // RING) as i:
                    for k in range(RING):
                        m = i * RING + (h * (BLOCKS // 2) + k)
                        sp.wait_ge(rows_turned, count(m - RING, 1, 1 + RING))
                        sp.dma_start(rows[k][:], x_rows[bass.ds(m * (2 * P), 2 * P), :].rearrange(
                            "(t p) d -> p t d", p=P)).then_inc(rows_loaded[k], 16)
            for s in out_stored:
                sp.wait_ge(s, count(CHUNKS // 2, 16, 0))

        @block.gpsimd
        def _(pool):
            prime(pool, r_token, 1)
            pool.memset(half[:], -0.5).then_inc(const, 1)
            pool.memset(ones[:], 1.0).then_inc(const, 1)
            pool.memset(earlier[:], 1.0).then_inc(const, 1)
            for p in range(2):
                pool.memset(scan[p][:], 0.0).then_inc(const, 1)
                pool.memset(ends[p][:], 0.0).then_inc(const, 1)
            pool.wait_ge(const, 7)
            pool.affine_select(out=earlier[:], in_=earlier[:], compare_op=ALU.is_gt, fill=0.0, base=0,
                               pattern=[[1, P]], channel_multiplier=-1).then_inc(const, 1)
            pool.wait_ge(const, 8)

            def scale(c):
                p = c % 2
                pool.wait_ge(r_var, count(c, len(R_VAR), nth(R_VAR, "var_eps")))
                pool.tensor_tensor(rstd[p][:], var[p][:], half[:], ALU.pow).then_inc(r_rstd, 1)
                pool.wait_ge(r_rstd, c + 1)
                pool.tensor_tensor(token[:, c * CT:(c + 1) * CT, :], centered[p][:],
                                   rstd[p][:].unsqueeze(2).to_broadcast([P, CT, D]), ALU.mult).then_inc(r_token, 1)

            def dispatch(c):
                pool.wait_ge(p_dve, picked(c // HC, "index2"))
                pool.wait_ge(r_token, count(c, 1, 1))
                for t in range(c * CT, (c + 1) * CT):
                    for k in range(2):
                        pool.indirect_dma_start(
                            x_rows, bass.IndirectOffsetOnAxis(ap=index[:, t, k:k + 1], axis=0), token[:, t, :], None
                        ).then_inc(dispatched, 16)

            def gather(f):
                if f % HC == 0:
                    for s in y_stored:
                        pool.wait_ge(s, 16 + (f // HC + 1) * BLOCKS // 2 // RING * 16)
                pool.wait_ge(f_dve, count(f - 2, len(F_DVE), nth(F_DVE, "sum2")))
                written = y_rows[0:(f // HC + 1) * BLOCKS * P, :]
                for t in range(CT):
                    for k in range(2):
                        pool.indirect_dma_start(
                            gathered_y[f % 2][k][:, t * D:(t + 1) * D], None, written,
                            bass.IndirectOffsetOnAxis(ap=index[:, f * CT + t, k:k + 1], axis=0)
                        ).then_inc(gathered[f % 2], 16)

            def end_power(f):
                pool.wait_ge(f_dve, count(f, len(F_DVE), nth(F_DVE, "var_eps")))
                pool.tensor_tensor(end_rstd[f % 2][:], end_var[f % 2][:], half[:], ALU.pow).then_inc(f_rstd, 1)

            for fn, c in ([(scale, c) for c in range(HC)]
                          + [(dispatch, 0), (scale, 4), (dispatch, 1), (scale, 5), (dispatch, 2), (scale, 6),
                             (scale, 7), (dispatch, 3)] + [(dispatch, c) for c in range(HC, CHUNKS)]):
                fn(c)
            for h in range(HALVES):
                gather(h * HC)
                for f in range(h * HC, (h + 1) * HC):
                    if f + 1 < (h + 1) * HC:
                        gather(f + 1)
                    end_power(f)

        @block.scalar
        def _(act):
            prime(act, silus, 1)
            prime(act, rows_moved, 1)
            prime(act, h_moved, 1)
            for s in y_stored:
                act.nop().then_inc(s, 16)
            for s in out_stored:
                prime(act, s, 16)

            def silu(n, i, p):
                act.wait_ge(gates, count(n + RING * i, 1, 1))
                act.wait_ge(hiddens, count(n + RING * i, 1, -1))
                act.activation(gated[p][:], ps_gu[p][:, :, 0:FF], ACT.Silu).then_inc(silus, 1)

            def move_rows(m, i, p):
                act.wait_ge(rows_turned, count(m + RING * i, 1, 1 + RING))
                act.wait_ge(gates, count(m + RING * i, 1, FIRST_ROUTED - 1))
                act.activation(rows_t[p][:].rearrange("p (t n) -> p t n", n=P), ps_x[:, 0:2, :], ACT.Copy
                               ).then_inc(rows_moved, 1)

            def move_hidden(n, i, p):
                act.wait_ge(h_turned, count(n + RING * i, 1, 1))
                act.wait_ge(downs, count(n + RING * i, 1, -1))
                act.activation(hidden_t[p][:], ps_h[:], ACT.Copy).then_inc(h_moved, 1)

            def store_y(m, i):
                act.wait_ge(y_out, count(m + RING * i, 1, FIRST_ROUTED + 1))
                act.dma_start(y_rows[bass.ds((m + RING * i) * (2 * P), 2 * P), :].rearrange("(t p) d -> p t d", p=P),
                              y[m % RING][:]).then_inc(y_stored[m % RING], 16)

            def work(step, i):
                if 0 <= step < ALL_PAIRS:
                    silu(step, i, step % 2)
                if routed(step + 1):
                    move_rows(step + 1 - FIRST_ROUTED, i, (step + 1) % 2)
                if 0 <= step - 1 < ALL_PAIRS:
                    move_hidden(step - 1, i, (step - 1) % 2)
                if routed(step - 3):
                    store_y(step - 3 - FIRST_ROUTED, i)
                for c in at(BEGIN_AT, step, 1):
                    act.wait_ge(r_dve, count(c, len(R_DVE), nth(R_DVE, "center")))
                    act.wait_ge(r_var, count(c - 2, len(R_VAR), nth(R_VAR, "var")))
                    act.activation(squares[c % 2][:], centered[c % 2][:], ACT.Square).then_inc(r_squared, 1)
                for c in at(BEGIN_AT, step, 2):
                    act.wait_ge(r_turned, c + 1)
                    act.activation(tokens_t[:, c * CN:(c + 1) * CN], ps_x[:], ACT.Copy).then_inc(r_moved, 1)
                for h in at({h: t["logit"] for h, t in PICK_AT.items()}, step):
                    act.wait_ge(p_dve, picked(h, "logit"))
                    act.activation(small["exp"][:], small["logit"][:], ACT.Exp, scale=-1.0).then_inc(p_exped, 1)
                for f in at(END_AT, step, 1):
                    act.wait_ge(f_dve, count(f, len(F_DVE), nth(F_DVE, "center")))
                    act.activation(end_squares[f % 2][:], ending[f % 2][:], ACT.Square).then_inc(f_squared, 1)
                for f in at(END_AT, step, 3):
                    act.wait_ge(f_dve, count(f, len(F_DVE), nth(F_DVE, "result")))
                    act.dma_start(out.rearrange("b (t p) d -> p (b t) d", p=P)[:, bass.ds((f) * CT, CT), :],
                                  result[f % 2][:]).then_inc(out_stored[f % 2], 16)

            at_every_step(act, work)

        @block.vector
        def _(dve):
            prime(dve, r_dve, len(R_DVE))
            prime(dve, r_var, len(R_VAR))
            prime(dve, f_dve, len(F_DVE))
            prime(dve, hiddens, 1)
            prime(dve, y_out, 1)
            dve.wait_ge(st["experts_loaded"], 16 * EXPERT_LOADS)
            dve.wait_ge(const, 8)

            def multiply(n, i, p):
                dve.wait_ge(silus, count(n + RING * i, 1, 1))
                dve.wait_ge(h_turned, count(n + RING * i, 1, -1))
                dve.tensor_tensor(hidden[p][:], ps_gu[p][:, :, FF:2 * FF], gated[p][:], ALU.mult
                                  ).then_inc(hiddens, 1)

            def move_y(n, i):
                dve.wait_ge(downs, count(n + RING * i, 1, 1))
                if routed(n):
                    m = n - FIRST_ROUTED
                    dve.wait_ge(y_stored[m % RING], ring_value(m, i) - 16)
                    dve.tensor_copy(y[m % RING][:], ps_y[:, 0:2, :]).then_inc(y_out, 1)
                else:
                    t = first_tile(n)
                    dve.tensor_tensor(acc[:, t:t + 2, :], token[:, t:t + 2, :], ps_y[:, 0:2, :], ALU.add
                                      ).then_inc(y_out, 1)

            class Steps:
                def __init__(self, steps, semaphore, value):
                    self.steps, self.semaphore, self.value = steps, semaphore, value

                def __call__(self, name, instruction, *operands):
                    before = self.value(nth(self.steps, name) - 1)
                    if not isinstance(before, int) or before:
                        dve.wait_ge(self.semaphore, before)
                    instruction(*operands).then_inc(self.semaphore, 1)

            def center(step, total, to):
                step("mean", dve.tensor_reduce, total[:], to[:], AX.X, ALU.add)
                step("center", dve.scalar_tensor_tensor, to[:], total[:].unsqueeze(2).to_broadcast([P, CT, D]),
                     -1.0 / D, to[:], ALU.mult, ALU.add)

            def variance(step, squares, var):
                step("var", dve.tensor_reduce, var[:], squares[:], AX.X, ALU.add)
                step("var_eps", dve.tensor_scalar, var[:], var[:], 1.0 / D, LN_EPS, ALU.mult, ALU.add)

            def pick(h, stage):
                step = Steps(P_DVE, p_dve, lambda n: h * len(P_DVE) + n)
                r, t = small, tops
                wide = lambda ap: ap[:].unsqueeze(2).to_broadcast([P, HT, EXPERTS])
                tiles = lambda ap: ap[:].unsqueeze(1).to_broadcast([P, HT, EXPERTS])
                of_half = slice(h * HT, (h + 1) * HT)
                if stage == "logit":
                    dve.wait_ge(r_logits, (h + 1) * HC)
                    step("logit", dve.tensor_tensor, r["logit"][:], ps_r[:, 0], tiles(bias), ALU.add)
                if stage == "first":
                    dve.wait_ge(p_exped, h + 1)
                    step("one_plus", dve.tensor_scalar, r["one_plus"][:], r["exp"][:], 1.0, None, ALU.add)
                    step("prob", dve.reciprocal, r["prob"][:], r["one_plus"][:])
                    step("top1", dve.tensor_reduce, t["top1"][:], r["prob"][:], AX.X, ALU.max)
                    step("is1", dve.tensor_tensor, r["is_"][:], r["prob"][:], wide(t["top1"]), ALU.is_equal)
                    step("place1", dve.tensor_tensor, r["place"][:], r["is_"][:], tiles(rank), ALU.mult)
                    step("first1", dve.tensor_reduce, t["first"][:], r["place"][:], AX.X, ALU.max)
                    step("pick1", dve.tensor_tensor, r["pick1"][:], r["place"][:], wide(t["first"]), ALU.is_equal)
                if stage == "second":
                    step("others", dve.scalar_tensor_tensor, r["others"][:], r["pick1"][:], -4.0, r["prob"][:],
                         ALU.mult, ALU.add)
                    step("top2", dve.tensor_reduce, t["top2"][:], r["others"][:], AX.X, ALU.max)
                    step("is2", dve.tensor_tensor, r["is_"][:], r["others"][:], wide(t["top2"]), ALU.is_equal)
                    step("place2", dve.tensor_tensor, r["place"][:], r["is_"][:], tiles(rank), ALU.mult)
                    step("first2", dve.tensor_reduce, t["first"][:], r["place"][:], AX.X, ALU.max)
                    step("pick2", dve.tensor_tensor, r["pick2"][:], r["place"][:], wide(t["first"]), ALU.is_equal)
                    step("picks", dve.tensor_tensor, r["picks"][:], r["pick1"][:], r["pick2"][:], ALU.add)
                if stage == "ranks":
                    dve.wait_ge(p_ranked, h + 1)
                    step("totals", dve.tensor_copy, scan[0][:, SCAN:, :], ps_r[:, 2])
                    for n, shift in enumerate((1, 2, 4, 8)):
                        step(f"scan{shift}", dve.tensor_tensor, scan[(n + 1) % 2][:, SCAN:, :],
                             scan[n % 2][:, SCAN:, :], scan[n % 2][:, SCAN - shift:SCAN - shift + HT, :], ALU.add)
                    step("over", dve.tensor_tensor, over[:],
                         scan[0][:, SCAN + HT - 1, :].unsqueeze(2).to_broadcast([P, EXPERTS, HT]),
                         st["multiples"][:].unsqueeze(1).to_broadcast([P, EXPERTS, HT]), ALU.is_gt)
                    step("blocks", dve.tensor_reduce, blocks[:], over[:], AX.X, ALU.add)
                    step("ends", dve.tensor_copy, ends[0][:, 4:], blocks[:])
                    for n, shift in enumerate((1, 2, 4)):
                        step(f"ends{shift}", dve.tensor_tensor, ends[(n + 1) % 2][:, 4:], ends[n % 2][:, 4:],
                             ends[n % 2][:, 4 - shift:4 - shift + EXPERTS], ALU.add)
                if stage == "slots":
                    step("base", dve.tensor_scalar, base[:], ends[1][:, 3:3 + EXPERTS], float(P),
                         float(h * BLOCKS * P), ALU.mult, ALU.add)
                    step("slot", dve.tensor_tensor, r["slot"][:], ps_r[:, 1], scan[0][:, SCAN - 1:SCAN - 1 + HT, :],
                         ALU.add)
                    step("slot_start", dve.tensor_tensor, r["slot"][:], r["slot"][:], tiles(base), ALU.add)
                    for n in ("1", "2"):
                        step("chosen" + n, dve.tensor_tensor, r["chosen"][:], r["slot"][:], r["pick" + n][:], ALU.mult)
                        step("slot" + n, dve.tensor_reduce, t["slot" + n][:], r["chosen"][:], AX.X, ALU.add)
                    for n in range(2):
                        step(f"index{n + 1}", dve.tensor_copy, index[:, of_half, n], t[f"slot{n + 1}"][:])
                if stage == "blocks":
                    step("past", dve.tensor_tensor, past[:],
                         st["numbers"][:].unsqueeze(2).to_broadcast([P, BLOCKS, EXPERTS]),
                         ends[1][:, 4:].unsqueeze(1).to_broadcast([P, BLOCKS, EXPERTS]), ALU.is_ge)
                    step("expert", dve.tensor_reduce, expert[:], past[:], AX.X, ALU.add)
                    step("table", dve.tensor_scalar, table[:, h * BLOCKS:(h + 1) * BLOCKS], expert[:],
                         float(EXPERTS - 1), 1.0, ALU.min, ALU.add)
                if stage == "weights":
                    step("total", dve.tensor_tensor, t["total"][:], t["top1"][:], t["top2"][:], ALU.add)
                    step("inverse", dve.reciprocal, t["total"][:], t["total"][:])
                    for n in range(2):
                        step(f"weight{n + 1}", dve.tensor_tensor, weight[:, of_half, n], t[f"top{n + 1}"][:],
                             t["total"][:], ALU.mult)

            def combine(f, p):
                step = Steps(F_DVE, f_dve, lambda n: count(f, len(F_DVE), n))
                chunk = bass.ds((f) * CT, CT)
                dve.wait_ge(gathered[p], (f // 2 + 1) * 2 * CT * 16)
                dve.wait_ge(y_out, count(2 * f + 1 + (PAIRS if f >= HC else 0), 1, 1))
                for n in range(2):
                    g = gathered_y[p][n][:].rearrange("p (t d) -> p t d", d=D)
                    step(f"weighted{n + 1}", dve.tensor_tensor, g, g,
                         weight[:, chunk, n:n + 1].to_broadcast([P, CT, D]), ALU.mult)
                    step(f"sum{n + 1}", dve.tensor_tensor, ending[p][:], ending[p][:] if n else acc[:, chunk, :], g,
                         ALU.add)
                center(step, end_total[p], ending[p])

            def work(step, i):
                if 0 <= step < ALL_PAIRS:
                    multiply(step, i, step % 2)
                if 0 <= step - 2 < ALL_PAIRS:
                    move_y(step - 2, i)
                for c in at(BEGIN_AT, step):
                    chain = Steps(R_DVE, r_dve, lambda n, c=c: count(c, len(R_DVE), n))
                    dve.wait_ge(x_loaded[c], 16)
                    dve.wait_ge(r_token, count(c, 1, -1))
                    chain("sum", dve.tensor_tensor, centered[c % 2][:], x[:, c * CT:(c + 1) * CT, :],
                          x_in[:, c * CT:(c + 1) * CT, :], ALU.add)
                    center(chain, total[c % 2], centered[c % 2])
                for c in at(BEGIN_AT, step, 1):
                    dve.wait_ge(r_squared, c + 1)
                    variance(Steps(R_VAR, r_var, lambda n, c=c: count(c, len(R_VAR), n)), squares[c % 2], var[c % 2])
                for h in range(HALVES):
                    for stage, when in PICK_AT[h].items():
                        if when == step:
                            pick(h, stage)
                for f in at(END_AT, step, 1):
                    dve.wait_ge(f_squared, f + 1)
                    variance(Steps(F_DVE, f_dve, lambda n, f=f: count(f, len(F_DVE), n)),
                             end_squares[f % 2], end_var[f % 2])
                for f in at(END_AT, step, 2):
                    chain = Steps(F_DVE, f_dve, lambda n, f=f: count(f, len(F_DVE), n))
                    dve.wait_ge(f_rstd, f + 1)
                    dve.wait_ge(out_stored[f % 2], pair_count(f - 2, f % 2))
                    chain("result", dve.tensor_tensor, result[f % 2][:], ending[f % 2][:],
                          end_rstd[f % 2][:].unsqueeze(2).to_broadcast([P, CT, D]), ALU.mult)

                for f in at(END_AT, step):
                    combine(f, f % 2)

            at_every_step(dve, work)

        @block.tensor
        def _(pe):
            for s in (gates, h_turned, downs, rows_turned):
                prime(pe, s, 1)
            pe.nop().then_inc(rows_turned, RING)
            pe.wait_ge(st["experts_loaded"], 16 * EXPERT_LOADS)

            def experts(n, i):
                if not routed(n):
                    return [0, 0]
                m = n - FIRST_ROUTED
                return [pe.value_load(table[0:1, bass.ds((m + RING * i) * 2 + t, 1)], min_val=0, max_val=EXPERTS)
                        for t in range(2)]

            def gate_up(n, i, p):
                weights_of = experts(n, i)
                if routed(n):
                    pe.wait_ge(rows_moved, count(n - FIRST_ROUTED + RING * i, 1, 1))
                pe.wait_ge(hiddens, count(n + RING * i, 1, -1))
                for t, e in enumerate(weights_of):
                    tile = rows_t[p][:, t * P:(t + 1) * P] if routed(n) else \
                        tokens_t[:, (first_tile(n) + t) * P:(first_tile(n) + t + 1) * P]
                    last = pe.matmul(ps_gu[p][:, t, :], tile, w_gate_up[:, bass.ds(e * (2 * FF), 2 * FF)],
                                     start=True, stop=True)
                last.then_inc(gates, 1)

            def turn_rows(n, i):
                m = n - FIRST_ROUTED
                pe.wait_ge(rows_loaded[m % RING], ring_value(m, i))
                pe.wait_ge(rows_moved, count(m + RING * i, 1, 0))
                for t in range(2):
                    last = pe.transpose(ps_x[:, t, :], rows[m % RING][:, t, :], ident[:])
                last.then_inc(rows_turned, 1)

            def down(n, i, p):
                weights_of = experts(n, i)
                pe.wait_ge(h_moved, count(n + RING * i, 1, 1))
                pe.wait_ge(y_out, count(n + RING * i, 1, 0))
                for t, e in enumerate(weights_of):
                    for f in range(2):
                        last = pe.matmul(ps_y[:, t, :], hidden_t[p][:, t, f, :],
                                         w_down[:, bass.ds(e * (2 * D) + f * D, D)], start=(f == 0), stop=(f == 1))
                last.then_inc(downs, 1)

            def turn_hidden(n, i, p):
                pe.wait_ge(hiddens, count(n + RING * i, 1, 1))
                pe.wait_ge(h_moved, count(n + RING * i, 1, 0))
                for t in range(2):
                    for f in range(2):
                        last = pe.transpose(ps_h[:, t, f, :], hidden[p][:, t, f * P:(f + 1) * P], ident[:])
                last.then_inc(h_turned, 1)

            def work(step, i):
                if 0 <= step < ALL_PAIRS:
                    if step == 0:
                        pe.wait_ge(r_moved, HC)
                    if step == FIRST_LAST:
                        pe.wait_ge(r_moved, CHUNKS)
                    if step == FIRST_ROUTED:
                        pe.wait_ge(p_dve, picked(0, "table"))
                    if step == PICK_AT[1]["blocks"] + 1:
                        pe.wait_ge(p_dve, picked(1, "table"))
                    gate_up(step, i, step % 2)
                if routed(step + 1):
                    if step + 1 == FIRST_ROUTED:
                        pe.wait_ge(r_moved, CHUNKS)
                    turn_rows(step + 1, i)
                if 0 <= step - 2 < ALL_PAIRS:
                    down(step - 2, i, step % 2)
                if 0 <= step - 1 < ALL_PAIRS:
                    turn_hidden(step - 1, i, (step - 1) % 2)
                for c in at(BEGIN_AT, step, 2):
                    pe.wait_ge(r_token, count(c, 1, 1))
                    if c:
                        pe.wait_ge(r_moved, c)
                    for t in range(CT):
                        last = pe.transpose(ps_x[:, t, :], token[:, c * CT + t, :], ident[:])
                    last.then_inc(r_turned, 1)
                    pe.wait_ge(r_moved, c + 1)
                    if c == HC:
                        pe.wait_ge(p_dve, picked(0, "slot"))
                    for t in range(CT):
                        at_tile = c * CT + t
                        last = pe.matmul(ps_r[:, 0, at_tile % HT, :], tokens_t[:, at_tile * P:(at_tile + 1) * P],
                                         w_router[:], start=True, stop=True)
                    last.then_inc(r_logits, 1)
                for h in at({h: t["second"] for h, t in PICK_AT.items()}, step):
                    pe.wait_ge(p_dve, picked(h, "picks"))
                    pe.matmul(ps_r[:, 1], earlier[:], small["picks"][:], start=True, stop=True)
                    pe.matmul(ps_r[:, 2], ones[:], small["picks"][:], start=True, stop=True).then_inc(p_ranked, 1)

            at_every_step(pe, work)


def setup_phase(nc, ins, st):
    with ExitStack() as ctx:
        down_t = ctx.enter_context(nc.sbuf_tensor("down_t", [32, D], F32))
        up = ctx.enter_context(nc.sbuf_tensor("up", [32, 2 * KV], F32))
        ps_w = ctx.enter_context(nc.psum_tensor("ps_w", [P, 2 * KV], F32))
        loaded, latent_loaded, made, folded, cleared = (
            ctx.enter_context(nc.semaphore(n)) for n in ("loaded", "latent_loaded", "made", "folded", "cleared"))
        block = ctx.enter_context(nc.Block())
        loads = [
            (st["x"][:], ins["hidden"].rearrange("b (t p) d -> p (b t) d", p=P)),
            (st["wall"][0][:, 0:D], ins["g_wq"]),
            (st["wall"][1][:], ins["l_wqkv"]),
            (st["wo"][0][:], ins["g_wo"]),
            (st["wo"][1][:], ins["l_wo"]),
            (st["norm_w"][0][:], ins["norm1_w"].rearrange("(p a) -> p a", a=1)),
            (st["norm_w"][1][:], ins["norm2_w"].rearrange("(p a) -> p a", a=1)),
            (st["cos"][0][:], ins["cos_g"].rearrange("(t p) d -> p t d", p=P)),
            (st["sin"][0][:], ins["sin_g"].rearrange("(t p) d -> p t d", p=P)),
            (st["cos"][1][:], ins["cos_l"].rearrange("(t p) d -> p t d", p=P)),
            (st["sin"][1][:], ins["sin_l"].rearrange("(t p) d -> p t d", p=P)),
        ]

        @block.sync
        def _(sp):
            sp.dma_start(down_t[:], ins["g_kv_down_t"]).then_inc(latent_loaded, 16)
            sp.dma_start(up[:], ins["g_kv_up"]).then_inc(latent_loaded, 16)
            for to, of in loads:
                sp.dma_start(to, of).then_inc(loaded, 16)
            sp.wait_ge(loaded, 16 * len(loads))

        @block.scalar
        def _(act):
            for to, of in ((st["w_gate_up"], ins["w_gate_up"]), (st["w_down"], ins["w_down"]),
                           (st["multiples"], ins["multiples"].partition_broadcast(P)),
                           (st["numbers"], ins["numbers"].partition_broadcast(P)),
                           (st["w_router"], ins["w_router"]), (st["bias"], ins["bias"].partition_broadcast(P)),
                           (st["rank"], ins["rank"].partition_broadcast(P))):
                act.dma_start(to[:], of).then_inc(st["experts_loaded"], 16)

        @block.gpsimd
        def _(pool):
            pool.memset(st["ident"][:], 0.0).then_inc(made, 1)
            pool.memset(st["ident_bf"][:], 0.0).then_inc(made, 1)
            pool.memset(st["rms_eps"][:], RMS_EPS).then_inc(made, 1)
            pool.memset(st["zeros"][:], 0.0).then_inc(made, 1)
            for p in range(2):
                pool.memset(st["va"][p][:], 0.0).then_inc(made, 1)
                pool.memset(st["vc"][p][:], 0.0).then_inc(made, 1)
            pool.wait_ge(made, 8)
            for p in range(2):
                pool.memset(st["va"][p][:, :, :, HD:HD + 1], 1.0).then_inc(made, 1)
            for m in ("ident", "ident_bf"):
                pool.affine_select(out=st[m][:], in_=st[m][:], compare_op=ALU.not_equal, fill=1.0, base=0,
                                   pattern=[[-1, P]], channel_multiplier=1).then_inc(made, 1)
            pool.wait_ge(made, 12)

        @block.tensor
        def _(pe):
            pe.wait_ge(latent_loaded, 32)
            pe.matmul(ps_w[:], down_t[:], up[:], start=True, stop=True).then_inc(folded, 1)

        @block.vector
        def _(dve):
            for p in range(2):
                for m in ("qs", "ks"):
                    dve.memset(st[m][p][64:KPAD, :, :].bitcast(mybir.dt.uint32), 0).then_inc(cleared, 1)
            dve.wait_ge(cleared, 4)
            dve.wait_ge(folded, 1)
            dve.tensor_copy(st["wall"][0][:, D:PROJ], ps_w[:]).then_inc(folded, 1)
            dve.wait_ge(folded, 2)


def program(nc, ins, out):
    with ExitStack() as ctx:
        def sb(name, shape, dt=F32):
            return ctx.enter_context(nc.sbuf_tensor(name, shape, dt))

        st = {
            "x": sb("x", [P, TILES, D]),
            "ident": sb("ident", [P, P]), "ident_bf": sb("ident_bf", [P, P], BF16),
            "rms_eps": sb("rms_eps", [P, 1]),
            "wall": [sb(f"wall{n}", [P, PROJ]) for n in range(2)],
            "wo": [sb(f"wo{n}", [P, D]) for n in range(2)],
            "norm_w": [sb(f"norm_w{n}", [P, 1]) for n in range(2)],
            "cos": [sb(f"cos{n}", [P, TPB, HD]) for n in range(2)],
            "sin": [sb(f"sin{n}", [P, TPB, HD]) for n in range(2)],
        }
        st.update(
            w_gate_up=sb("w_gate_up", [P, (1 + EXPERTS) * 2 * FF]), w_down=sb("w_down", [P, UNITS * D]),
            multiples=sb("multiples", [P, HT]), numbers=sb("numbers", [P, BLOCKS]), zeros=sb("zeros", [P, CN]),
            x_rows=nc.dram_tensor("x_rows", [HALVES * BLOCKS * P, D], F32).ap(),
            w_router=sb("w_router", [P, EXPERTS]), bias=sb("bias", [P, EXPERTS]), rank=sb("rank", [P, EXPERTS]),
            experts_loaded=ctx.enter_context(nc.semaphore("experts_loaded")),
            hidden_tiles=ins["hidden"].rearrange("b (t p) d -> p (b t) d", p=P))
        with ExitStack() as both:
            st.update(
                qs=[both.enter_context(nc.sbuf_tensor(f"qs{p}", [KPAD, HEADS, S], BF16)) for p in range(2)],
                ks=[both.enter_context(nc.sbuf_tensor(f"ks{p}", [KPAD, GROUPS, S], BF16)) for p in range(2)],
                va=[both.enter_context(nc.sbuf_tensor(f"va{p}", [P, TPB, GROUPS, VW], F32)) for p in range(2)],
                vc=[both.enter_context(nc.sbuf_tensor(f"vc{p}", [P, TPB, GROUPS, VW], F32)) for p in range(2)],
                stacks=[both.enter_context(nc.semaphore(f"stacks{p}")) for p in range(2)])
            setup_phase(nc, ins, st)
            attention_layers(nc, st)
        expert_phase(nc, ins, out, st)


def attention_layers(nc, st):
        for n, tag in enumerate(("global", "local")):
            with ExitStack() as layer:
                one = dict(st, **{k: st[k][n] for k in ("wall", "wo", "norm_w", "cos", "sin")})
                one["pairs_before"] = n * (B // 2)
                one["v_all"] = layer.enter_context(nc.sbuf_tensor(f"v_all_{tag}", [P, TILES, KV], F32))
                one["q_dram"] = nc.dram_tensor(f"q_parts_{tag}", [B, PARTS, HEADS * HD, S], BF16).ap()
                one["k_dram"] = nc.dram_tensor(f"k_parts_{tag}", [B, PARTS * KV, S], BF16).ap()
                prepare_phase(nc, tag, one)
                attention_phase(nc, tag, one, local=(n == 1))


def rotary(base):
    import numpy as np

    inv_freq = np.float32(1.0) / np.float32(base) ** (np.arange(0, HD, 2, dtype=np.float32) / np.float32(HD))
    angle = np.arange(S, dtype=np.float32)[:, None] * inv_freq[None, :].astype(np.float32)
    cos, sin = np.cos(angle), np.sin(angle)
    return np.repeat(cos, 2, axis=1), np.stack([-sin, sin], axis=-1).reshape(S, HD)


def kernel(**inputs):
    import numpy as np
    import concourse.bacc as bacc
    from concourse.bass_utils import run_bass_kernel_spmd

    a = {k.replace("L0_attn_", "").replace("L0_ffn_", ""): np.asarray(v) for k, v in inputs.items()}
    cos_g, sin_g = rotary(1000000.0)
    cos_l, sin_l = rotary(10000.0)

    def slices(shared, routed):
        return np.concatenate([shared[None], routed]).transpose(2, 0, 1)

    down = np.concatenate([a["sd_w"][None], a["wd"]]).reshape(1 + EXPERTS, D, FF // P, P)
    arrays = {
        "hidden": a["hidden"], "norm1_w": a["norm1_w"], "norm2_w": a["norm2_w"],
        "g_wq": a["g_wq"], "g_kv_down_t": a["g_kv_down"].T,
        "g_kv_up": np.concatenate([a["g_k_up"], a["g_v_up"]], axis=1), "g_wo": a["g_wo"],
        "l_wqkv": np.concatenate([a["l_wq"], a["l_wk"], a["l_wv"]], axis=1), "l_wo": a["l_wo"],
        "cos_g": cos_g, "sin_g": sin_g, "cos_l": cos_l, "sin_l": sin_l,
        "w_gate_up": np.concatenate([slices(a["sg_w"], a["wg"]), slices(a["su_w"], a["wu"])], axis=2).reshape(D, -1),
        "w_down": down.transpose(3, 0, 2, 1).reshape(P, UNITS * D),
        "multiples": np.arange(HT).astype(np.float32) * P, "numbers": np.arange(BLOCKS).astype(np.float32),
        "w_router": a["router_w"].T, "bias": a["routing_bias"],
        "rank": np.arange(EXPERTS, 0, -1).astype(np.float32),
    }
    arrays = {f"in_{k}": np.ascontiguousarray(v) for k, v in arrays.items()}
    nc = bacc.Bacc("TRN2", target_bir_lowering=False, num_devices=1)
    ins = {k[3:]: nc.dram_tensor(k, v.shape, mybir.dt.from_np(v.dtype), kind="ExternalInput").ap()
           for k, v in arrays.items()}
    out = nc.dram_tensor("out", (B, S, D), F32, kind="ExternalOutput").ap()
    program(nc, ins, out)
    return run_bass_kernel_spmd(nc, [arrays], core_ids=[0]).results[0]["out"]
```

```python
from contextlib import ExitStack

import concourse.bass as bass
from concourse import mybir

F32 = mybir.dt.float32
U32 = mybir.dt.uint32
BF16 = mybir.dt.bfloat16
ALU = mybir.AluOpType
ACT = mybir.ActivationFunctionType
AX = mybir.AxisListType

P = 128
D = 128
HEADS, GROUPS, HD = 16, 4, 8
REP = HEADS // GROUPS
B, S = 4, 1024
TPB = S // P
TILES = B * TPB
WINDOW = 32
CT = 4
CN = CT * P
CHUNKS = TILES // CT
QK = (HEADS + GROUPS) * HD
KV = GROUPS * HD
PROJ = QK + KV
PARTS = 3
ROWS = PARTS * PARTS * HD
KPAD = 96
VW = 32
EXPERTS, FF = 8, 256
WEIGHTS = 2 * FF + FF // P * D
EXPERT_LOADS = 6
RMS_EPS, LN_EPS = 1e-6, 1e-5
BANK = 512


AHEAD = 2


def count(unit, per, nth):
    return (unit + AHEAD) * per + nth


def pair_count(c, par):
    return (c - par) * 8 + (AHEAD + 1) * 16


def prime(engine, semaphore, per):
    engine.nop().then_inc(semaphore, AHEAD * per)


def nth(steps, name):
    return steps.index(name) + 1


BATCH_CHUNKS = TPB // CT
PREPARE = [(0, "square"), (1, "sum"), (2, "invert"), (3, "refine"), (4, "scale", 0), (6, "scale", 1),
           (5, "turn_tokens", 0), (6, "move_tokens", 0), (7, "turn_tokens", 1), (8, "move_tokens", 1),
           (9, "project", 0, 0), (10, "rotate", 0, 0), (11, "project", 0, 1), (12, "rotate", 0, 1),
           (13, "project", 1, 0), (14, "rotate", 1, 0), (15, "project", 1, 1), (16, "rotate", 1, 1),
           (13, "add", 0), (14, "square_heads", 0), (15, "sum_heads", 0), (16, "invert_heads", 0),
           (17, "normalise", 0), (18, "part1", 0), (19, "rest", 0), (20, "part23", 0),
           (18, "add", 1), (19, "square_heads", 1), (20, "sum_heads", 1), (21, "invert_heads", 1),
           (22, "normalise", 1), (24, "part1", 1), (25, "rest", 1), (26, "part23", 1),
           (21, "turn_parts", 0, 0), (22, "move_parts", 0, 0), (23, "turn_parts", 0, 1), (24, "move_parts", 0, 1),
           (27, "turn_parts", 1, 0), (28, "move_parts", 1, 0), (29, "turn_parts", 1, 1), (30, "move_parts", 1, 1),
           (24, "store", 0), (30, "store", 1)]
PREPARE_STEPS = 31
RING_SLOTS, RING_BANKS = 3, 2
TILE_SLOTS = (0, 3)
PROB_SLOTS = 6
TILE_PROBS = (0, 3, 5, 8)
PROB_BANKS = PROB_SLOTS * RING_BANKS
PV_LAG = 3
LAYERS = 2
RUNS = LAYERS * B


def slots_of_run(run):
    slots = []
    if run >= B:
        for qt in range(TPB):
            slots.append([("full", run, qt, qt, g, g * BANK) for g in range(3)])
            last = [("full", run, qt, qt, 3, 0)]
            if qt:
                last.append(("corner", run, qt, qt - 1, None, BANK))
            slots.append(last)
        return slots
    for qt in range(TPB):
        for kt in [qt] + list(range(qt)):
            for first in range(0, GROUPS, RING_BANKS):
                slots.append([("full", run, qt, kt, first + k, k * BANK) for k in range(RING_BANKS)])
    return slots


STACK_DMAS = 2 * PARTS * PARTS


def attention_layers(nc, st):
    x, ident, ident_bf, q_dram, k_dram = (st[k] for k in ("x", "ident", "ident_bf", "q_dram", "k_dram"))
    slots, first_slot = [], []
    for run in range(RUNS):
        first_slot.append(len(slots))
        slots += slots_of_run(run)
    first_slot.append(len(slots))
    N = len(slots)
    QTILES = RUNS * TPB
    q_of = lambda it: it[1] * TPB + it[2]
    last_of = {}
    for n, items in enumerate(slots):
        for it in items:
            last_of[q_of(it)] = n
    L1 = first_slot[B]
    assert L1 % RING_SLOTS == 0 and L1 % PROB_SLOTS == 0
    score_bank = [n % RING_SLOTS * RING_BANKS if n < L1 else TILE_SLOTS[(n - L1) % 2] for n in range(N)]
    prob_bank = [n % PROB_SLOTS * RING_BANKS if n < L1 else TILE_PROBS[(n - L1) % 4] for n in range(N)]
    score_ring = [RING_SLOTS if n < L1 else len(TILE_SLOTS) for n in range(N)]
    prob_ring = [PROB_SLOTS if n < L1 else len(TILE_PROBS) for n in range(N)]
    order = [q_of(it) for items in slots for it in items]
    weighed_upto = [sum(len(items) for items in slots[:n + 1]) for n in range(N)]
    tile_weighed = [len(order) - order[::-1].index(q) for q in range(QTILES)]
    run_weighed = [weighed_upto[first_slot[run + 1] - 1] for run in range(RUNS)]
    pool_masks, dve_masks, pool_upto, dve_upto = {}, {}, [], []
    for n, items in enumerate(slots):
        diagonal = [it for it in items if it[0] == "full" and it[2] == it[3]]
        if n >= L1 and (n - L1) % 2:
            pool_masks[n] = items
        elif diagonal:
            dve_masks[n] = diagonal
        pool_upto.append(sum(len(m) for m in pool_masks.values()))
        dve_upto.append(len(dve_masks))
    first_weighed = [min(n for n in range(N) if q_of(slots[n][0]) == q) + 1 + PV_LAG for q in range(QTILES)]
    stages_of_end, added_step = [], []
    for q in range(QTILES):
        pause = 2 if q < B * TPB and 2 <= q % TPB < TPB - 1 else 1
        begin = max(last_of[q] + PV_LAG + pause, added_step[-1] if q else 0)
        stages_of_end.append([begin, begin + pause, begin + 2 * pause])
        added_step.append(begin + 2 * pause)
    assert all(added_step[q] < first_weighed[q + 2] for q in range(QTILES - 2))

    def spare_bank(unit, step):
        if unit == RUNS - 1:
            return 2
        if unit == 0:
            return step // 2 % 2
        done = sum(added < step for added in added_step)
        limit = first_weighed[done + 1] if done + 1 < QTILES else step + 2
        return (done + 1) % 2 if step + 1 < limit else None

    bank_for = {}

    def plan(unit, begin):
        stages, shift = [], 0
        for when, name, *place in sorted(PREPARE, key=lambda stage: stage[0]):
            if name in ("turn_tokens", "project", "turn_parts"):
                while spare_bank(unit, begin + when + shift) is None:
                    shift += 1
                bank_for[unit, name, *place] = spare_bank(unit, begin + when + shift)
            stages.append((begin + when + shift, name, *place))
        return stages

    plans = [plan(0, -PREPARE_STEPS - 1)]
    for unit in range(1, RUNS):
        plans.append(plan(unit, max(plans[-1][-1][0] + 1, added_step[(unit - B + 1) * TPB - 1] + 1 if unit >= B else 0)))
    beside = {}
    for unit, stages in enumerate(plans):
        for when, *stage in stages:
            beside.setdefault(when, []).append((unit, *stage))
    planned = [stages[-1][0] + 1 for stages in plans]
    STEPS_ALL = range(plans[0][0][0], max(added_step[-1], max(beside)) + 1)
    POST = ["denominators", "heads", "heads_moved", "added"]
    ROPE = ["cosine", "sine_even", "sine_odd", "values"]
    NORM = ["head_sum", "head_mean", "head_square", "head_product", "head_factor", "head_scale", "normed"]
    SUM, SPLITS = 6, 3

    def layer(run):
        return run // B

    with ExitStack() as ctx:
        def sb(name, shape, dt=F32):
            return ctx.enter_context(nc.sbuf_tensor(name, shape, dt))

        def ps(name, shape, dt=F32):
            return ctx.enter_context(nc.psum_tensor(name, shape, dt))

        def sem(name):
            return ctx.enter_context(nc.semaphore(name))

        def two(name, shape, dt=F32):
            return [sb(f"{name}{p}", shape, dt) for p in range(2)]

        qs, ks, va, vc = (st[k] for k in ("qs", "ks", "va", "vc"))
        v_all = sb("v_all", [P, TILES, KV])
        prob = sb("prob", [P, PROB_BANKS * BANK])
        sums = sb("sums", [P, REP, P])
        rden = sb("rden", [P, REP, GROUPS])
        on = sb("on", [P, GROUPS, REP, HD])
        ot = sb("ot", [P, P])
        band, edge, window = sb("band", [P, P]), sb("edge", [P, WINDOW]), sb("window", [P, P])
        ps_s = ps("ps_s", [P, RING_SLOTS * RING_BANKS * BANK])
        ps_v = [ps(f"ps_v{p}", [P, REP, P]) for p in range(2)]

        def scores_at(n, at_col, width):
            first = score_bank[n] * BANK + at_col
            return ps_s[:, first:first + width]

        def probs_at(n, at_col, width):
            first = prob_bank[n] * BANK + at_col
            return prob[:, first:first + width]

        def side(bank):
            return ps_s[:, 5 * BANK:6 * BANK] if bank == 2 else ps_v[bank][:].rearrange("p r n -> p (r n)")

        def side_tokens(unit, c):
            return side(bank_for[unit, "turn_tokens", c])

        def side_projected(unit, c, h):
            return side(bank_for[unit, "project", c, h]).rearrange("p (t d) -> p t d", t=2)

        def side_parts(unit, c, h):
            return side(bank_for[unit, "turn_parts", c, h]).bitcast(BF16).rearrange("p (t i n) -> p t i n", t=2, n=P)

        mean, rstd, spare = (sb(n, [P, TPB]) for n in ("mean", "rstd", "spare"))
        xn, xt = sb("xn", [P, CT, D]), two("xt", [P, CN])
        tcos, tsin, roped = (sb(n, [P, CT * QK]) for n in ("tcos", "tsin", "roped"))
        squares = sb("squares", [P, 2 * CT * QK])
        sqh = [squares[:, c * CT * QK:(c + 1) * CT * QK] for c in range(2)]
        sq = squares[:, 0:TPB * D].rearrange("p (t d) -> p t d", d=D)
        hs, hi, head_spare = (sb(n, [P, CT * QK // HD]) for n in ("hs", "hi", "head_spare"))
        part = [sb(f"part{i}", [P, CT * QK], BF16) for i in range(PARTS)]
        zq, zk = two("zq", [P, PARTS, CN], BF16), sb("zk", [PARTS * KV, CN], BF16)

        masks_made, values, rows_cleared = sem("masks_made"), sem("values"), sem("rows_cleared")
        corners = [sem(f"corners{p}") for p in range(2)]
        stacks = [sem(f"stacks{p}") for p in range(2)]
        first_stack = sem("first_stack")
        stored = [sem(f"stored{p}") for p in range(2)]
        scored, exped, masked, masked_dve, weighed = (
            sem(n) for n in ("scored", "exped", "masked", "masked_dve", "weighed"))
        post, sums_out, sums_turned, heads_turned, y_ready = (
            sem(n) for n in ("post", "sums_out", "sums_turned", "heads_turned", "y_ready"))
        squared, summed, logged, inverted = (sem(n) for n in ("squared", "summed", "logged", "inverted"))
        xn_ready, xt_turned, xt_ready, projected, rope, roped_ready = (
            sem(n) for n in ("xn_ready", "xt_turned", "xt_ready", "projected", "rope", "roped_ready"))
        head_squared, head_logged, head_inverted, norm, rest_ready, split, turned, parts_out = (
            sem(n) for n in ("head_squared", "head_logged", "head_inverted", "norm", "rest_ready", "split",
                             "turned", "parts_out"))

        def after(engine, semaphore, value):
            if value > 0:
                engine.wait_ge(semaphore, value)

        def post_value(q, name):
            return q * len(POST) + nth(POST, name)

        def chunk_of(unit, c):
            return unit * BATCH_CHUNKS + c

        def rope_value(k, h, name):
            return (2 * k + h) * len(ROPE) + nth(ROPE, name)

        def norm_value(k, name):
            return k * len(NORM) + nth(NORM, name)

        def heads(ap):
            return ap.rearrange("p (n d) -> p n d", d=HD)

        def tiles_of(unit, c=None):
            first = unit % B * TPB
            return slice(first, first + TPB) if c is None else slice(first + c * CT, first + (c + 1) * CT)

        def at_every_step(attend, stages):
            for step in STEPS_ALL:
                attend(step)
                for unit, name, *where in beside.get(step, []):
                    if name in stages:
                        stages[name](unit, *where)

        block = ctx.enter_context(nc.Block())

        @block.sync
        def _(sp):
            def store(unit, c):
                k = chunk_of(unit, c)
                sp.wait_ge(parts_out, 4 * (k + 1))
                part_of = slice(c * CN, (c + 1) * CN)
                sp.dma_start(q_dram[unit, :, :, part_of].rearrange("i r n -> r i n"), zq[c][:]
                             ).then_inc(stored[c], 16)
                sp.dma_start(k_dram[unit, :, part_of], zk[:]).then_inc(stored[c], 16)

            def load_stacks(run, chunks=range(BATCH_CHUNKS), loaded=None):
                par = run % 2
                cols = slice(chunks[0] * CN, (chunks[-1] + 1) * CN)
                loaded = loaded or stacks[par]
                for c in chunks:
                    sp.wait_ge(stored[c], 32 * (run + 1))
                if run >= 2:
                    sp.wait_ge(weighed, run_weighed[run - 2])
                for i in range(PARTS):
                    for j in range(PARTS):
                        rows = slice((i * PARTS + j) * HD, (i * PARTS + j + 1) * HD)
                        sp.dma_start(qs[par][rows, :, cols], q_dram[run, i, :, cols].rearrange(
                            "(h d) n -> d h n", d=HD)).then_inc(loaded, 16)
                        sp.dma_start(ks[par][rows, :, cols], k_dram[run, j * KV:(j + 1) * KV, cols].rearrange(
                            "(g d) n -> d g n", d=HD)).then_inc(loaded, 16)

            def copy_corners(run):
                sp.wait_ge(values, run + 1)
                for g in range(GROUPS):
                    sp.dma_start(vc[run % 2][g * WINDOW:(g + 1) * WINDOW, :, g, :],
                                 va[run % 2][P - WINDOW:P, :, g, :]).then_inc(corners[run % 2], 16)

            def load_experts():
                for name in ("weights", "w_router", "bias", "rank", "multiples", "numbers"):
                    source = st["expert_ins"][name]
                    sp.dma_start(st[name][:], source if len(source.shape) > 1 else source.partition_broadcast(P)
                                 ).then_inc(st["experts_loaded"], 16)
                clear = st["x_rows"].rearrange("(p n) d -> p (n d)", p=P).rearrange("p (a n) -> p a n", n=D)
                sp.dma_start(clear, st["zeros"][:].unsqueeze(1).to_broadcast([P, clear.shape[1], D])
                             ).then_inc(rows_cleared, 16)

            transfers = [(when, 0, store, (unit, *stage[1:])) for unit, stages in enumerate(plans)
                         for when, *stage in stages if stage[0] == "store"]
            for run in range(RUNS):
                free = max(planned[run], first_slot[run - 1] + PV_LAG if run >= 2 else 0)
                if run:
                    transfers.append((free, 1, load_stacks, (run,)))
                if run >= B:
                    transfers.append((free, 2, copy_corners, (run,)))
            first_store, last_store = sorted(when for when, name, *_ in plans[0] if name == "store")
            transfers.append((first_store, 1, load_stacks, (0, [0], first_stack)))
            transfers.append((last_store, 1, load_stacks, (0, [1])))
            for b in range(1, B):
                tiles = slice(b * TPB, (b + 1) * TPB)
                sp.dma_start(x[:, tiles, :], st["hidden_tiles"][:, tiles, :]).then_inc(st["x_loaded"][b], 16)
            transfers.append((planned[1], 3, load_experts, ()))
            for _, _, transfer, where in sorted(transfers, key=lambda t: t[:2]):
                transfer(*where)
            sp.wait_ge(rows_cleared, 16)

        @block.gpsimd
        def _(pool):
            def scale(unit, c):
                k = chunk_of(unit, c)
                pool.wait_ge(summed, SUM * (unit + 1))
                after(pool, xt_turned, k)
                pool.tensor_tensor(xn[:], x[:, tiles_of(unit, c), :],
                                   rstd[:, c * CT:(c + 1) * CT].unsqueeze(2).to_broadcast([P, CT, D]),
                                   ALU.mult).then_inc(xn_ready, 1)

            def add(unit, c):
                k = chunk_of(unit, c)
                pool.wait_ge(rope, rope_value(k, 1, "sine_odd"))
                after(pool, norm, norm_value(k - 1, "normed"))
                pool.tensor_tensor(roped[:], tcos[:], tsin[:], ALU.add).then_inc(roped_ready, 1)

            def square_heads(unit, c):
                k = chunk_of(unit, c)
                pool.wait_ge(roped_ready, k + 1)
                after(pool, split, SPLITS * (k - 1))
                pool.tensor_tensor(sqh[c], roped[:], roped[:], ALU.mult).then_inc(head_squared, 1)

            def rest(unit, c):
                pool.wait_ge(split, SPLITS * chunk_of(unit, c) + 1)
                pool.tensor_tensor(sqh[c], sqh[c], part[0][:], ALU.subtract).then_inc(rest_ready, 1)

            def copy_values(run):
                par = run % 2
                pool.wait_ge(rope, rope_value(chunk_of(run, 1), 1, "values"))
                if run >= 2:
                    pool.wait_ge(weighed, run_weighed[run - 2])
                if run >= B + 2:
                    pool.wait_ge(corners[par], GROUPS * 16 * ((run - B) // 2))
                pool.tensor_copy(va[par][:, :, :, 0:HD],
                                 v_all[:, tiles_of(run), :].rearrange("p t (g d) -> p t g d", d=HD)
                                 ).then_inc(values, 1)

            for m in (band, window, edge):
                pool.memset(m[:], 1.0).then_inc(masks_made, 1)
            pool.wait_ge(masks_made, 3)
            for m in (band, window):
                pool.affine_select(out=m[:], in_=m[:], compare_op=ALU.is_ge, fill=0.0, base=0,
                                   pattern=[[1, P]], channel_multiplier=-1).then_inc(masks_made, 1)
            pool.wait_ge(masks_made, 5)
            pool.affine_select(out=window[:], in_=window[:], compare_op=ALU.is_ge, fill=0.0, base=WINDOW - 1,
                               pattern=[[-1, P]], channel_multiplier=1).then_inc(masks_made, 1)
            for g in range(GROUPS):
                pool.wait_ge(masks_made, 6 + g)
                rows = edge[g * WINDOW:(g + 1) * WINDOW, :]
                pool.affine_select(out=rows, in_=rows, compare_op=ALU.is_gt, fill=0.0, base=0,
                                   pattern=[[-1, WINDOW]], channel_multiplier=1).then_inc(masks_made, 1)
            pool.wait_ge(masks_made, 6 + GROUPS)

            copy_step = {max(planned[run], first_slot[run - 1] + PV_LAG if run >= 2 else 0): run
                         for run in range(RUNS)}

            def attend(step):
                if step - 1 in pool_masks:
                    n = step - 1
                    pool.wait_ge(exped, n + 1)
                    for it in pool_masks[n]:
                        full = it[0] == "full"
                        mask, width = (window, P) if full else (edge, WINDOW)
                        region = probs_at(n, it[5], REP * width).rearrange("p (r q) -> p r q", r=REP)
                        pool.tensor_tensor(region, region, mask[:].unsqueeze(1).to_broadcast([P, REP, width]),
                                           ALU.mult).then_inc(masked, 1)
                if step in copy_step:
                    copy_values(copy_step[step])

            at_every_step(attend, {"scale": scale, "add": add, "square_heads": square_heads, "rest": rest})

        @block.scalar
        def _(act):
            def square(unit):
                if unit < B:
                    act.wait_ge(st["x_loaded"][unit], 16)
                else:
                    act.wait_ge(post, post_value((unit - B + 1) * TPB - 1, "added"))
                after(act, split, 2 * SPLITS * unit)
                act.activation(sq, x[:, tiles_of(unit), :], ACT.Square).then_inc(squared, 1)

            def invert(unit):
                act.wait_ge(summed, SUM * unit + 2)
                after(act, xn_ready, 2 * unit)
                act.activation(rstd[:], mean[:], ACT.Ln).then_inc(logged, 1)
                act.wait_ge(logged, unit + 1)
                act.activation(rstd[:], rstd[:], ACT.Exp, scale=-0.5).then_inc(inverted, 1)

            def move_tokens(unit, c):
                k = chunk_of(unit, c)
                act.wait_ge(xt_turned, k + 1)
                after(act, projected, 2 * (k - 1))
                act.activation(xt[c][:], side_tokens(unit, c), ACT.Copy, scale=st["norm_w"][layer(unit)][:]
                               ).then_inc(xt_ready, 1)

            def invert_heads(unit, c):
                k = chunk_of(unit, c)
                act.wait_ge(norm, norm_value(k, "head_mean"))
                act.activation(hi[:], hs[:], ACT.Ln).then_inc(head_logged, 1)
                act.wait_ge(head_logged, k + 1)
                act.activation(hi[:], hi[:], ACT.Exp, scale=-0.5).then_inc(head_inverted, 1)

            def move_parts(unit, c, h):
                k = chunk_of(unit, c)
                act.wait_ge(turned, 2 * k + h + 1)
                after(act, stored[c], 32 * unit)
                after(act, stored[1 - c], 32 * (unit + c))
                act.activation(zq[c][:].rearrange("p i (t n) -> p t i n", n=P)[:, 2 * h:2 * h + 2],
                               side_parts(unit, c, h)[:, :, 0:PARTS, :], ACT.Copy).then_inc(parts_out, 1)
                act.activation(zk[:].rearrange("p (t n) -> p t n", n=P)[:, 2 * h:2 * h + 2],
                               side_parts(unit, c, h)[0:PARTS * KV, :, PARTS, :], ACT.Copy).then_inc(parts_out, 1)

            def attend(step):
                for q in range(B * TPB, QTILES):
                    if last_of[q] + PV_LAG == step:
                        act.wait_ge(weighed, tile_weighed[q])
                        act.wait_ge(sums_turned, q)
                        act.activation(sums[:], ps_v[q % 2][:], ACT.Copy).then_inc(sums_out, 1)
                if not 0 <= step < N:
                    return
                act.wait_ge(scored, step + 1)
                if step >= prob_ring[step]:
                    act.wait_ge(weighed, weighed_upto[step - prob_ring[step]])
                width = sum(REP * (P if it[0] == "full" else WINDOW) for it in slots[step])
                act.activation(probs_at(step, 0, width), scores_at(step, 0, width), ACT.Exp,
                               scale=HD ** -0.5).then_inc(exped, 1)

            nc.scalar.preload_act_table_set("natural_log_exp_and_others")
            at_every_step(attend, {"square": square, "invert": invert, "move_tokens": move_tokens,
                                   "invert_heads": invert_heads,
                                   "move_parts": move_parts})

        @block.vector
        def _(dve):
            def sum_squares(unit):
                dve.wait_ge(squared, unit + 1)
                dve.tensor_reduce(mean[:], sq, AX.X, ALU.add).then_inc(summed, 1)
                dve.wait_ge(summed, SUM * unit + 1)
                dve.tensor_scalar(mean[:], mean[:], 1.0 / D, RMS_EPS, ALU.mult, ALU.add).then_inc(summed, 1)

            def refine(value, of, spare, semaphore, done):
                steps = [(dve.tensor_tensor, spare, value, value, ALU.mult),
                         (dve.tensor_tensor, spare, spare, of, ALU.mult),
                         (dve.tensor_scalar, spare, spare, -0.5, 1.5, ALU.mult, ALU.add),
                         (dve.tensor_tensor, value, value, spare, ALU.mult)]
                for n, (instruction, *operands) in enumerate(steps):
                    if n:
                        dve.wait_ge(semaphore, done + n)
                    instruction(*operands).then_inc(semaphore, 1)

            def refine_tokens(unit):
                dve.wait_ge(inverted, unit + 1)
                refine(rstd[:], mean[:], spare[:], summed, SUM * unit + 2)

            def rotate(unit, c, h):
                k = chunk_of(unit, c)
                dve.wait_ge(projected, 2 * k + h + 1)
                after(dve, roped_ready, k)
                if unit >= B:
                    dve.wait_ge(values, unit - B + 1)
                pq = side_projected(unit, c, h)[:, :, 0:QK]
                half = pq.rearrange("p t (h i two) -> p t h i two", i=HD // 2, two=2)
                tile = c * CT + 2 * h
                cos, sin = st["cos"][layer(unit)], st["sin"][layer(unit)]
                cols = slice(2 * h * QK, 2 * (h + 1) * QK)
                cs = cos[:, tile:tile + 2, :].unsqueeze(2).to_broadcast([P, 2, QK // HD, HD])
                dve.tensor_tensor(tcos[:, cols].rearrange("p (t h d) -> p t h d", t=2, d=HD),
                                  pq.rearrange("p t (h d) -> p t h d", d=HD), cs, ALU.mult).then_inc(rope, 1)
                out = tsin[:, cols].rearrange("p (t h i two) -> p t h i two", t=2, i=HD // 2, two=2)
                sn = sin[:, tile:tile + 2, :].rearrange("p t (i two) -> p t i two", two=2)
                for to in range(2):
                    dve.tensor_tensor(out[:, :, :, :, to], half[:, :, :, :, 1 - to],
                                      sn[:, :, :, to].unsqueeze(2).to_broadcast([P, 2, QK // HD, HD // 2]),
                                      ALU.mult).then_inc(rope, 1)
                at_tile = unit % B * TPB + tile
                dve.tensor_copy(v_all[:, at_tile:at_tile + 2, :], side_projected(unit, c, h)[:, :, QK:PROJ]).then_inc(rope, 1)

            def sum_heads(unit, c):
                k = chunk_of(unit, c)
                dve.wait_ge(head_squared, k + 1)
                dve.tensor_reduce(hs[:], heads(sqh[c]), AX.X, ALU.add).then_inc(norm, 1)
                dve.wait_ge(norm, norm_value(k, "head_sum"))
                dve.tensor_scalar(hs[:], hs[:], 1.0 / HD, RMS_EPS, ALU.mult, ALU.add).then_inc(norm, 1)

            def normalise(unit, c):
                k = chunk_of(unit, c)
                dve.wait_ge(head_inverted, k + 1)
                refine(hi[:], hs[:], head_spare[:], norm, norm_value(k, "head_mean"))
                dve.wait_ge(norm, norm_value(k, "head_scale"))
                dve.tensor_tensor(heads(sqh[c]), heads(roped[:]),
                                  hi[:].unsqueeze(2).to_broadcast([P, CT * QK // HD, HD]),
                                  ALU.mult).then_inc(norm, 1)

            def part1(unit, c):
                k = chunk_of(unit, c)
                dve.wait_ge(norm, norm_value(k, "normed"))
                after(dve, turned, 2 * k)
                dve.tensor_copy(part[0][:], sqh[c]).then_inc(split, 1)

            def part23(unit, c):
                k = chunk_of(unit, c)
                dve.wait_ge(rest_ready, k + 1)
                dve.tensor_copy(part[1][:], sqh[c]).then_inc(split, 1)
                dve.wait_ge(split, SPLITS * k + 2)
                dve.tensor_tensor(part[2][:], sqh[c], part[1][:], ALU.subtract).then_inc(split, 1)

            def sums_of(q):
                dve.wait_ge(weighed, tile_weighed[q])
                after(dve, sums_turned, q)
                dve.tensor_copy(sums[:], ps_v[q % 2][:]).then_inc(sums_out, 1)

            def heads_of(q):
                dve.wait_ge(sums_turned, q + 1)
                by_group = ps_v[q % 2][:].rearrange("p r (g v) -> p r g v", v=VW)
                dve.reciprocal(rden[:], by_group[:, :, :, HD]).then_inc(post, 1)
                dve.wait_ge(post, post_value(q, "denominators"))
                dve.tensor_tensor(on[:].rearrange("p g r d -> p r g d"), by_group[:, :, :, 0:HD],
                                  rden[:].unsqueeze(3).to_broadcast([P, REP, GROUPS, HD]),
                                  ALU.mult).then_inc(post, 1)

            def move_heads(q):
                dve.wait_ge(heads_turned, q + 1)
                dve.tensor_copy(ot[:], ps_v[q % 2][:, 0, :]).then_inc(post, 1)

            def add_tokens(q):
                dve.wait_ge(y_ready, q + 1)
                at_tile = q % TILES
                tile = x[:, at_tile:at_tile + 1, :]
                dve.tensor_tensor(tile, tile, ps_v[q % 2][:, 1:2, :], ALU.add).then_inc(post, 1)

            def mask_slot(n):
                dve.wait_ge(exped, n + 1)
                at_col, width = dve_masks[n][0][5], len(dve_masks[n]) * REP
                mask = window if dve_masks[n][0][1] >= B else band
                region = probs_at(n, at_col, width * P).rearrange("p (r q) -> p r q", q=P)
                dve.tensor_tensor(region, region, mask[:].unsqueeze(1).to_broadcast([P, width, P]),
                                  ALU.mult).then_inc(masked_dve, 1)

            dve.wait_ge(masks_made, 6 + GROUPS)
            work = {}
            for q in range(QTILES):
                turn_at, heads_at, add_at = stages_of_end[q]
                work.setdefault(add_at, []).append((0, add_tokens, q))
                if q < B * TPB:
                    work.setdefault(last_of[q] + PV_LAG, []).append((2, sums_of, q))
                work.setdefault(turn_at, []).append((3, heads_of, q))
                work.setdefault(heads_at, []).append((3, move_heads, q))
            for n in dve_masks:
                work.setdefault(n + 1, []).append((1, mask_slot, n))

            def attend(step):
                for _, do, which in sorted(work.get(step, []), key=lambda w: (w[0], w[2])):
                    do(which)

            at_every_step(attend, {"sum": sum_squares, "refine": refine_tokens, "rotate": rotate, "sum_heads": sum_heads,
                                   "normalise": normalise, "part1": part1, "part23": part23})

        @block.tensor
        def _(pe):
            reader = [None, None, (exped, L1)]

            def wait_for_reader(bank):
                if reader[bank]:
                    pe.wait_ge(*reader[bank])

            def turn_tokens(unit, c):
                k = chunk_of(unit, c)
                pe.wait_ge(xn_ready, k + 1)
                wait_for_reader(bank_for[unit, "turn_tokens", c])
                for t in range(CT):
                    last = pe.transpose(side_tokens(unit, c)[:, t * P:(t + 1) * P], xn[:, t, :], ident[:])
                last.then_inc(xt_turned, 1)
                reader[bank_for[unit, "turn_tokens", c]] = (xt_ready, k + 1)

            def project_tokens(unit, c, h):
                k = chunk_of(unit, c)
                pe.wait_ge(xt_ready, k + 1)
                wait_for_reader(bank_for[unit, "project", c, h])
                for t in range(2):
                    at_col = (2 * h + t) * P
                    last = pe.matmul(side_projected(unit, c, h)[:, t, 0:PROJ], xt[c][:, at_col:at_col + P], st["wall"][layer(unit)][:],
                                     start=True, stop=True)
                last.then_inc(projected, 1)
                reader[bank_for[unit, "project", c, h]] = (rope, rope_value(k, h, "values"))

            def turn_parts(unit, c, h):
                k = chunk_of(unit, c)
                pe.wait_ge(split, SPLITS * (k + 1))
                wait_for_reader(bank_for[unit, "turn_parts", c, h])
                for t in range(2):
                    at_col = (2 * h + t) * QK
                    for i in range(PARTS):
                        pe.transpose(side_parts(unit, c, h)[:, t, i, :], part[i][:, at_col:at_col + HEADS * HD], ident_bf[:])
                        last = pe.transpose(side_parts(unit, c, h)[i * KV:(i + 1) * KV, t, PARTS, :],
                                            part[i][:, at_col + HEADS * HD:at_col + QK], ident_bf[:])
                last.then_inc(turned, 1)
                reader[bank_for[unit, "turn_parts", c, h]] = (parts_out, 2 * (2 * k + h + 1))

            def score(n):
                run = slots[n][0][1]
                par = run % 2
                if n == 0:
                    pe.wait_ge(first_stack, STACK_DMAS * 16)
                if n == first_slot[run] and n or run == 0 and slots[n][0][2:4] == (CT, CT):
                    pe.wait_ge(stacks[par], (run // 2 + 1) * STACK_DMAS * 16)
                after(pe, exped, n - score_ring[n] + 1)
                for kind, _, qt, kt, g, at_col in slots[n]:
                    if kind == "full":
                        last = pe.matmul(scores_at(n, at_col, REP * P).rearrange("p (r q) -> p r q", q=P),
                                         ks[par][:, g, kt * P:(kt + 1) * P],
                                         qs[par][:, g * REP:(g + 1) * REP, qt * P:(qt + 1) * P],
                                         start=True, stop=True)
                        continue
                    for h in range(GROUPS):
                        last = pe.matmul(scores_at(n, at_col, REP * WINDOW)[h * WINDOW:(h + 1) * WINDOW, :].rearrange(
                                             "p (r q) -> p r q", r=REP),
                                         ks[par][:, h, (kt + 1) * P - WINDOW:(kt + 1) * P],
                                         qs[par][:, h * REP:(h + 1) * REP, qt * P:qt * P + WINDOW],
                                         start=True, stop=True)
                last.then_inc(scored, 1)

            def weigh(m):
                run = slots[m][0][1]
                par = run % 2
                if m == first_slot[run]:
                    pe.wait_ge(values, run + 1)
                    if run >= B:
                        pe.wait_ge(corners[par], GROUPS * 16 * ((run - B) // 2 + 1))
                pe.wait_ge(exped, m + 2)
                after(pe, masked, pool_upto[m + 1])
                after(pe, masked_dve, dve_upto[m + 1])
                for n, it in [(n, it) for n in (m, m + 1) for it in slots[n]]:
                    kind, _, qt, kt, g, at_col = it
                    q = q_of(it)
                    first = kt == qt
                    if first and g == 0:
                        wait_for_reader(q % 2)
                    if kind == "full":
                        pe.matmul(ps_v[q % 2][g * VW:(g + 1) * VW, :, :], va[par][:, kt, g, :],
                                  probs_at(n, at_col, REP * P).rearrange("p (r q) -> p r q", q=P),
                                  start=first, stop=(qt == 0 if run >= B else kt == max(qt - 1, 0))
                                  ).then_inc(weighed, 1)
                        continue
                    for h in range(GROUPS):
                        last = pe.matmul(ps_v[q % 2][h * VW:(h + 1) * VW, :, 0:WINDOW], vc[par][:, kt, h, :],
                                         probs_at(n, at_col, REP * WINDOW).rearrange(
                                             "p (r q) -> p r q", r=REP), start=False, stop=True)
                    last.then_inc(weighed, 1)

            def turn_sums(q):
                pe.wait_ge(sums_out, q + 1)
                for r in range(REP):
                    last = pe.transpose(ps_v[q % 2][:, r, :], sums[:, r, :], ident[:])
                last.then_inc(sums_turned, 1)

            def turn_heads(q):
                pe.wait_ge(post, post_value(q, "heads"))
                pe.transpose(ps_v[q % 2][:, 0, :], on[:].rearrange("p g r d -> p (g r d)"), ident[:]
                             ).then_inc(heads_turned, 1)

            def project_heads(q):
                pe.wait_ge(post, post_value(q, "heads_moved"))
                pe.matmul(ps_v[q % 2][:, 1, :], ot[:], st["wo"][q // (B * TPB)][:], start=True, stop=True
                          ).then_inc(y_ready, 1)
                reader[q % 2] = (post, post_value(q, "added"))

            turn_at, heads_at, project_at = ({stages[k]: q for q, stages in enumerate(stages_of_end)}
                                             for k in range(3))

            def attend(step):
                if step in project_at and step > L1:
                    project_heads(project_at[step])
                if 0 <= step < N:
                    score(step)
                if 0 <= step - PV_LAG < N and (step - PV_LAG) % 2:
                    weigh(step - PV_LAG - 1)
                if step in project_at and step <= L1:
                    project_heads(project_at[step])
                if step in turn_at:
                    turn_sums(turn_at[step])
                if step in heads_at:
                    turn_heads(heads_at[step])

            pe.wait_ge(st["padded"], 4 * 16)
            at_every_step(attend, {"turn_tokens": turn_tokens, "project": project_tokens, "turn_parts": turn_parts})


HALVES = 2
HT = TILES // HALVES
HC = CHUNKS // HALVES
BLOCKS = 2 * HT + EXPERTS
PAIRS = HALVES * BLOCKS // 2
SHARED = HT // 2
FIRST_ROUTED, FIRST_LAST = SHARED, SHARED + PAIRS
ALL_PAIRS = FIRST_LAST + SHARED
SCAN = 8
RING = 4
LOOPS = {SHARED + 6: 5}
BEGIN_AT = {c: -11 + c for c in range(HC)} | dict(zip(range(HC, CHUNKS), (0, 1, 2, 3)))
PICK_AT = {0: {"logit": -4, "first": -3, "second": -3, "ranks": -2, "slots": -2, "blocks": -1, "weights": -1},
           1: {"logit": 7, "first": 8, "second": 9, "ranks": 10, "slots": 11, "blocks": 12, "weights": 13}}
END_AT = {f: SHARED + 26 + 4 * f for f in range(HC)} | dict(zip(range(HC, CHUNKS), (53, 56, 58, 60)))
STEPS = range(-11, 64)


def at_every_step(engine, work, load=None, take=None):
    step = STEPS[0]
    while step in STEPS:
        if step in LOOPS:
            if load:
                load(step, 0)
            with engine.Fori(0, LOOPS[step]) as i:
                if take:
                    take(step)
                t = engine.snap(i * RING)
                for k in range(RING):
                    work(step + k, t)
                if load:
                    load(step + RING, t)
            step += RING * LOOPS[step]
        else:
            work(step, 0)
            step += 1


def at(table, step, after=0):
    return [c for c, begin in table.items() if begin + after == step]


def expert_phase(nc, ins, out, st):
    x, ident = st["x"], st["ident"]
    weights, w_router, bias, rank = (st[k] for k in ("weights", "w_router", "bias", "rank"))
    R_DVE = ["sum", "mean", "center"]
    R_VAR = ["var", "var_eps"]
    P_DVE = ["logit", "one_plus", "prob", "top1", "is1", "place1", "first1", "pick1", "others",
             "top2", "is2", "place2", "first2", "pick2", "picks",
             "totals", "scan1", "scan2", "scan4", "scan8", "over", "blocks", "ends", "ends1", "ends2",
             "ends4", "base", "slot", "slot_start", "chosen1", "slot1", "chosen2", "slot2",
             "index1", "index2", "past", "expert", "weights_at", "table", "total", "inverse", "weight1", "weight2"]
    F_DVE = ["weighted1", "sum1", "weighted2", "sum2", "mean", "center", "var", "var_eps", "result"]
    with ExitStack() as ctx:
        def sb(name, shape, dt=F32):
            return ctx.enter_context(nc.sbuf_tensor(name, shape, dt))

        def ps(name, shape, dt=F32):
            return ctx.enter_context(nc.psum_tensor(name, shape, dt))

        def sem(name):
            return ctx.enter_context(nc.semaphore(name))

        x_in = sb("x_in", [P, TILES, D])
        token = sb("token", [P, TILES, D])
        tokens_t = sb("tokens_t", [P, TILES * P])
        acc = sb("acc", [P, TILES, D])
        centered = [sb(f"centered{p}", [P, CT, D]) for p in range(3)]
        squares = [sb(f"squares{p}", [P, CT, D]) for p in range(2)]
        total, var, rstd = ([sb(f"{n}{p}", [P, CT]) for p in range(2)] for n in ("total", "var", "rstd"))
        half = sb("half", [P, CT])
        small = {n: sb(f"route_{n}", [P, HT, EXPERTS]) for n in
                 ("logit", "exp", "one_plus", "prob", "is_", "place", "pick1", "others", "pick2", "picks",
                  "slot", "chosen")}
        tops = {n: sb(f"tops_{n}", [P, HT]) for n in ("top1", "first", "top2", "total", "slot1", "slot2")}
        scan = [sb(f"scan{p}", [P, SCAN + HT, EXPERTS]) for p in range(2)]
        over = sb("over", [P, EXPERTS, HT])
        ends = [sb(f"ends{p}", [P, 4 + EXPERTS]) for p in range(2)]
        base, blocks = sb("base", [P, EXPERTS]), sb("blocks", [P, EXPERTS])
        past, expert = sb("past", [P, BLOCKS, EXPERTS]), sb("expert", [P, BLOCKS])
        table = sb("table", [P, HALVES * BLOCKS], U32)
        index = sb("index", [P, TILES, 2], U32)
        weight = sb("weight", [P, TILES, 2])
        earlier, ones = sb("earlier", [P, P]), sb("ones", [P, P])
        rows = [sb(f"rows{p}", [P, 2, D]) for p in range(RING)]
        rows_t = [sb(f"rows_t{p}", [P, 2 * P]) for p in range(2)]
        gated = [sb(f"gated{p}", [P, 2, FF]) for p in range(2)]
        hidden = [sb(f"hidden{p}", [P, 2, FF]) for p in range(2)]
        hidden_t = [sb(f"hidden_t{p}", [P, 2, 2, P]) for p in range(2)]
        y = [sb(f"y{p}", [P, 2, D]) for p in range(RING)]
        gathered_y = [[sb(f"gathered_y{k}_{p}", [P, CT * D]) for k in range(2)] for p in range(2)]
        ending = [sb(f"ending{p}", [P, CT, D]) for p in range(2)]
        end_squares = [sb(f"end_squares{p}", [P, CT, D]) for p in range(2)]
        end_total, end_var, end_rstd = (
            [sb(f"{n}{p}", [P, CT]) for p in range(2)] for n in ("end_total", "end_var", "end_rstd"))
        result = [sb(f"result{p}", [P, CT, D]) for p in range(2)]
        x_rows = st["x_rows"]
        y_rows = nc.dram_tensor("y_rows", [HALVES * BLOCKS * P, D], F32).ap()
        ps_gu = [ps(f"ps_gu{p}", [P, 2, 2 * FF]) for p in range(2)]
        ps_h = ps("ps_h", [P, 2, 2, P])
        ps_y = ps("ps_y", [P, CT, D])
        ps_x = ps("ps_x", [P, CT, D])
        ps_r = ps("ps_r", [P, 4, HT, EXPERTS])

        x_loaded = [sem(f"x_loaded{c}") for c in range(CHUNKS)]
        const, r_dve, r_var, r_squared, r_rstd, r_token, r_turned, r_moved, r_logits = (
            sem(n) for n in ("const", "r_dve", "r_var", "r_squared", "r_rstd", "r_token", "r_turned", "r_moved", "r_logits"))
        p_dve, p_exped, p_ranked, dispatched = (sem(n) for n in ("p_dve", "p_exped", "p_ranked", "dispatched"))
        rows_loaded, y_stored = ([sem(f"{n}{p}") for p in range(RING)] for n in ("rows_loaded", "y_stored"))
        rows_turned, rows_moved = sem("rows_turned"), sem("rows_moved")
        gates, silus, hiddens, h_turned, h_moved, downs, y_out = (
            sem(n) for n in ("gates", "silus", "hiddens", "h_turned", "h_moved", "downs", "y_out"))
        gathered, out_stored = ([sem(f"{n}{p}") for p in range(2)] for n in ("gathered", "out_stored"))
        f_dve, f_squared, f_rstd = sem("f_dve"), sem("f_squared"), sem("f_rstd")

        def picked(h, name):
            return h * len(P_DVE) + nth(P_DVE, name)

        def routed(pair):
            return FIRST_ROUTED <= pair < FIRST_LAST

        def first_tile(pair):
            return 2 * pair if pair < SHARED else 2 * (pair - PAIRS)

        def ring_value(m, i):
            return (m // RING) * 16 + 32 + i * (16 // RING)

        block = ctx.enter_context(nc.Block())

        @block.sync
        def _(sp):
            for c in range(CHUNKS):
                sp.dma_start(x_in[:, c * CT:(c + 1) * CT, :], st["hidden_tiles"][:, c * CT:(c + 1) * CT, :]
                             ).then_inc(x_loaded[c], 16)
            for s in rows_loaded:
                sp.nop().then_inc(s, 16)
            for h in range(HALVES):
                sp.wait_ge(dispatched, (h + 1) * 2 * HT * 16)
                with sp.Fori(0, BLOCKS // 2 // RING) as i:
                    for k in range(RING):
                        m = i * RING + (h * (BLOCKS // 2) + k)
                        sp.wait_ge(rows_turned, count(m - RING, 1, 1 + RING))
                        sp.dma_start(rows[k][:], x_rows[bass.ds(m * (2 * P), 2 * P), :].rearrange(
                            "(t p) d -> p t d", p=P)).then_inc(rows_loaded[k], 16)
            for s in out_stored:
                sp.wait_ge(s, count(CHUNKS // 2, 16, 0))

        @block.gpsimd
        def _(pool):
            pool.memset(half[:], -0.5).then_inc(const, 1)
            pool.memset(ones[:], 1.0).then_inc(const, 1)
            pool.memset(earlier[:], 1.0).then_inc(const, 1)
            for p in range(2):
                pool.memset(scan[p][:], 0.0).then_inc(const, 1)
                pool.memset(ends[p][:], 0.0).then_inc(const, 1)
            pool.wait_ge(const, 7)
            pool.affine_select(out=earlier[:], in_=earlier[:], compare_op=ALU.is_gt, fill=0.0, base=0,
                               pattern=[[1, P]], channel_multiplier=-1).then_inc(const, 1)
            pool.wait_ge(const, 8)

            def power(c):
                p = c % 2
                pool.wait_ge(r_var, count(c, len(R_VAR), nth(R_VAR, "var_eps")))
                pool.tensor_tensor(rstd[p][:], var[p][:], half[:], ALU.pow).then_inc(r_rstd, 1)

            def dispatch(c):
                pool.wait_ge(p_dve, picked(c // HC, "index2"))
                pool.wait_ge(r_token, count(c, 1, 1))
                for t in range(c * CT, (c + 1) * CT):
                    for k in range(2):
                        pool.indirect_dma_start(
                            x_rows, bass.IndirectOffsetOnAxis(ap=index[:, t, k:k + 1], axis=0), token[:, t, :], None
                        ).then_inc(dispatched, 16)

            def gather(f):
                if f % HC == 0:
                    for s in y_stored:
                        pool.wait_ge(s, 16 + (f // HC + 1) * BLOCKS // 2 // RING * 16)
                pool.wait_ge(f_dve, count(f - 2, len(F_DVE), nth(F_DVE, "sum2")))
                written = y_rows[0:(f // HC + 1) * BLOCKS * P, :]
                for t in range(CT):
                    for k in range(2):
                        pool.indirect_dma_start(
                            gathered_y[f % 2][k][:, t * D:(t + 1) * D], None, written,
                            bass.IndirectOffsetOnAxis(ap=index[:, f * CT + t, k:k + 1], axis=0)
                        ).then_inc(gathered[f % 2], 16)

            def end_power(f):
                pool.wait_ge(f_dve, count(f, len(F_DVE), nth(F_DVE, "var_eps")))
                pool.tensor_tensor(end_rstd[f % 2][:], end_var[f % 2][:], half[:], ALU.pow).then_inc(f_rstd, 1)

            for fn, c in ([(power, c) for c in range(HC)]
                          + [(dispatch, 0), (power, 4), (dispatch, 1), (power, 5), (dispatch, 2), (power, 6),
                             (power, 7), (dispatch, 3)] + [(dispatch, c) for c in range(HC, CHUNKS)]):
                fn(c)
            for h in range(HALVES):
                gather(h * HC)
                for f in range(h * HC, (h + 1) * HC):
                    if f + 1 < (h + 1) * HC:
                        gather(f + 1)
                    end_power(f)

        @block.scalar
        def _(act):
            prime(act, silus, 1)
            prime(act, rows_moved, 1)
            prime(act, h_moved, 1)
            for s in y_stored:
                act.nop().then_inc(s, 16)
            for s in out_stored:
                prime(act, s, 16)

            def silu(n, i, p):
                act.wait_ge(gates, count(n + i, 1, 1))
                act.wait_ge(hiddens, count(n + i, 1, -1))
                act.activation(gated[p][:], ps_gu[p][:, :, 0:FF], ACT.Silu).then_inc(silus, 1)

            def move_rows(m, i, p):
                act.wait_ge(rows_turned, count(m + i, 1, 1 + RING))
                act.wait_ge(gates, count(m + i, 1, FIRST_ROUTED - 1))
                act.activation(rows_t[p][:].rearrange("p (t n) -> p t n", n=P), ps_x[:, 0:2, :], ACT.Copy
                               ).then_inc(rows_moved, 1)

            def move_hidden(n, i, p):
                act.wait_ge(h_turned, count(n + i, 1, 1))
                act.wait_ge(downs, count(n + i, 1, -1))
                act.activation(hidden_t[p][:], ps_h[:], ACT.Copy).then_inc(h_moved, 1)

            def store_y(m, i):
                act.wait_ge(y_out, count(m + i, 1, FIRST_ROUTED + 1))
                act.dma_start(y_rows[bass.ds((m + i) * (2 * P), 2 * P), :].rearrange("(t p) d -> p t d", p=P),
                              y[m % RING][:]).then_inc(y_stored[m % RING], 16)

            def work(step, i):
                if 0 <= step < ALL_PAIRS:
                    silu(step, i, step % 2)
                if routed(step + 1):
                    move_rows(step + 1 - FIRST_ROUTED, i, (step + 1) % 2)
                if 0 <= step - 1 < ALL_PAIRS:
                    move_hidden(step - 1, i, (step - 1) % 2)
                if routed(step - 3):
                    store_y(step - 3 - FIRST_ROUTED, i)
                for c in at(BEGIN_AT, step, 1):
                    act.wait_ge(r_dve, count(c, len(R_DVE), nth(R_DVE, "center")))
                    act.wait_ge(r_var, count(c - 2, len(R_VAR), nth(R_VAR, "var")))
                    act.activation(squares[c % 2][:], centered[c % 3][:], ACT.Square).then_inc(r_squared, 1)
                for c in at(BEGIN_AT, step, 3):
                    act.wait_ge(r_turned, c + 1)
                    act.activation(tokens_t[:, c * CN:(c + 1) * CN], ps_x[:], ACT.Copy).then_inc(r_moved, 1)
                for h in at({h: t["logit"] for h, t in PICK_AT.items()}, step):
                    act.wait_ge(p_dve, picked(h, "logit"))
                    act.activation(small["exp"][:], small["logit"][:], ACT.Exp, scale=-1.0).then_inc(p_exped, 1)
                for f in at(END_AT, step, 1):
                    act.wait_ge(f_dve, count(f, len(F_DVE), nth(F_DVE, "center")))
                    act.activation(end_squares[f % 2][:], ending[f % 2][:], ACT.Square).then_inc(f_squared, 1)
                for f in at(END_AT, step, 3):
                    act.wait_ge(f_dve, count(f, len(F_DVE), nth(F_DVE, "result")))
                    act.dma_start(out.rearrange("b (t p) d -> p (b t) d", p=P)[:, bass.ds((f) * CT, CT), :],
                                  result[f % 2][:]).then_inc(out_stored[f % 2], 16)

            at_every_step(act, work)

        @block.vector
        def _(dve):
            prime(dve, r_token, 1)
            prime(dve, r_dve, len(R_DVE))
            prime(dve, r_var, len(R_VAR))
            prime(dve, f_dve, len(F_DVE))
            prime(dve, hiddens, 1)
            prime(dve, y_out, 1)
            dve.wait_ge(st["experts_loaded"], 16 * EXPERT_LOADS)
            dve.wait_ge(const, 8)

            def multiply(n, i, p):
                dve.wait_ge(silus, count(n + i, 1, 1))
                dve.wait_ge(h_turned, count(n + i, 1, -1))
                dve.tensor_tensor(hidden[p][:], ps_gu[p][:, :, FF:2 * FF], gated[p][:], ALU.mult
                                  ).then_inc(hiddens, 1)

            def move_y(n, i):
                dve.wait_ge(downs, count(n + i, 1, 1))
                if routed(n):
                    m = n - FIRST_ROUTED
                    dve.wait_ge(y_stored[m % RING], ring_value(m, i) - 16)
                    dve.tensor_copy(y[m % RING][:], ps_y[:, 0:2, :]).then_inc(y_out, 1)
                else:
                    t = first_tile(n)
                    dve.tensor_tensor(acc[:, t:t + 2, :], token[:, t:t + 2, :], ps_y[:, 0:2, :], ALU.add
                                      ).then_inc(y_out, 1)

            class Steps:
                def __init__(self, steps, semaphore, value):
                    self.steps, self.semaphore, self.value = steps, semaphore, value

                def __call__(self, name, instruction, *operands):
                    before = self.value(nth(self.steps, name) - 1)
                    if not isinstance(before, int) or before:
                        dve.wait_ge(self.semaphore, before)
                    instruction(*operands).then_inc(self.semaphore, 1)

            def center(step, total, to):
                step("mean", dve.tensor_reduce, total[:], to[:], AX.X, ALU.add)
                step("center", dve.scalar_tensor_tensor, to[:], total[:].unsqueeze(2).to_broadcast([P, CT, D]),
                     -1.0 / D, to[:], ALU.mult, ALU.add)

            def variance(step, squares, var):
                step("var", dve.tensor_reduce, var[:], squares[:], AX.X, ALU.add)
                step("var_eps", dve.tensor_scalar, var[:], var[:], 1.0 / D, LN_EPS, ALU.mult, ALU.add)

            def pick(h, stage):
                step = Steps(P_DVE, p_dve, lambda n: h * len(P_DVE) + n)
                r, t = small, tops
                wide = lambda ap: ap[:].unsqueeze(2).to_broadcast([P, HT, EXPERTS])
                tiles = lambda ap: ap[:].unsqueeze(1).to_broadcast([P, HT, EXPERTS])
                of_half = slice(h * HT, (h + 1) * HT)
                if stage == "logit":
                    dve.wait_ge(r_logits, (h + 1) * HC)
                    step("logit", dve.tensor_tensor, r["logit"][:], ps_r[:, 0], tiles(bias), ALU.add)
                if stage == "first":
                    dve.wait_ge(p_exped, h + 1)
                    step("one_plus", dve.tensor_scalar, r["one_plus"][:], r["exp"][:], 1.0, None, ALU.add)
                    step("prob", dve.reciprocal, r["prob"][:], r["one_plus"][:])
                    step("top1", dve.tensor_reduce, t["top1"][:], r["prob"][:], AX.X, ALU.max)
                    step("is1", dve.tensor_tensor, r["is_"][:], r["prob"][:], wide(t["top1"]), ALU.is_equal)
                    step("place1", dve.tensor_tensor, r["place"][:], r["is_"][:], tiles(rank), ALU.mult)
                    step("first1", dve.tensor_reduce, t["first"][:], r["place"][:], AX.X, ALU.max)
                    step("pick1", dve.tensor_tensor, r["pick1"][:], r["place"][:], wide(t["first"]), ALU.is_equal)
                if stage == "second":
                    step("others", dve.scalar_tensor_tensor, r["others"][:], r["pick1"][:], -4.0, r["prob"][:],
                         ALU.mult, ALU.add)
                    step("top2", dve.tensor_reduce, t["top2"][:], r["others"][:], AX.X, ALU.max)
                    step("is2", dve.tensor_tensor, r["is_"][:], r["others"][:], wide(t["top2"]), ALU.is_equal)
                    step("place2", dve.tensor_tensor, r["place"][:], r["is_"][:], tiles(rank), ALU.mult)
                    step("first2", dve.tensor_reduce, t["first"][:], r["place"][:], AX.X, ALU.max)
                    step("pick2", dve.tensor_tensor, r["pick2"][:], r["place"][:], wide(t["first"]), ALU.is_equal)
                    step("picks", dve.tensor_tensor, r["picks"][:], r["pick1"][:], r["pick2"][:], ALU.add)
                if stage == "ranks":
                    dve.wait_ge(p_ranked, h + 1)
                    step("totals", dve.tensor_copy, scan[0][:, SCAN:, :], ps_r[:, 2])
                    for n, shift in enumerate((1, 2, 4, 8)):
                        step(f"scan{shift}", dve.tensor_tensor, scan[(n + 1) % 2][:, SCAN:, :],
                             scan[n % 2][:, SCAN:, :], scan[n % 2][:, SCAN - shift:SCAN - shift + HT, :], ALU.add)
                    step("over", dve.tensor_tensor, over[:],
                         scan[0][:, SCAN + HT - 1, :].unsqueeze(2).to_broadcast([P, EXPERTS, HT]),
                         st["multiples"][:].unsqueeze(1).to_broadcast([P, EXPERTS, HT]), ALU.is_gt)
                    step("blocks", dve.tensor_reduce, blocks[:], over[:], AX.X, ALU.add)
                    step("ends", dve.tensor_copy, ends[0][:, 4:], blocks[:])
                    for n, shift in enumerate((1, 2, 4)):
                        step(f"ends{shift}", dve.tensor_tensor, ends[(n + 1) % 2][:, 4:], ends[n % 2][:, 4:],
                             ends[n % 2][:, 4 - shift:4 - shift + EXPERTS], ALU.add)
                if stage == "slots":
                    step("base", dve.tensor_scalar, base[:], ends[1][:, 3:3 + EXPERTS], float(P),
                         float(h * BLOCKS * P), ALU.mult, ALU.add)
                    step("slot", dve.tensor_tensor, r["slot"][:], ps_r[:, 1], scan[0][:, SCAN - 1:SCAN - 1 + HT, :],
                         ALU.add)
                    step("slot_start", dve.tensor_tensor, r["slot"][:], r["slot"][:], tiles(base), ALU.add)
                    for n in ("1", "2"):
                        step("chosen" + n, dve.tensor_tensor, r["chosen"][:], r["slot"][:], r["pick" + n][:], ALU.mult)
                        step("slot" + n, dve.tensor_reduce, t["slot" + n][:], r["chosen"][:], AX.X, ALU.add)
                    for n in range(2):
                        step(f"index{n + 1}", dve.tensor_copy, index[:, of_half, n], t[f"slot{n + 1}"][:])
                if stage == "blocks":
                    step("past", dve.tensor_tensor, past[:],
                         st["numbers"][:].unsqueeze(2).to_broadcast([P, BLOCKS, EXPERTS]),
                         ends[1][:, 4:].unsqueeze(1).to_broadcast([P, BLOCKS, EXPERTS]), ALU.is_ge)
                    step("expert", dve.tensor_reduce, expert[:], past[:], AX.X, ALU.add)
                    step("weights_at", dve.tensor_scalar, expert[:], expert[:], float(EXPERTS - 1), 1.0,
                         ALU.min, ALU.add)
                    step("table", dve.tensor_scalar, table[:, h * BLOCKS:(h + 1) * BLOCKS], expert[:],
                         float(WEIGHTS), None, ALU.mult)
                if stage == "weights":
                    step("total", dve.tensor_tensor, t["total"][:], t["top1"][:], t["top2"][:], ALU.add)
                    step("inverse", dve.reciprocal, t["total"][:], t["total"][:])
                    for n in range(2):
                        step(f"weight{n + 1}", dve.tensor_tensor, weight[:, of_half, n], t[f"top{n + 1}"][:],
                             t["total"][:], ALU.mult)

            def combine(f, p):
                step = Steps(F_DVE, f_dve, lambda n: count(f, len(F_DVE), n))
                chunk = bass.ds((f) * CT, CT)
                dve.wait_ge(gathered[p], (f // 2 + 1) * 2 * CT * 16)
                dve.wait_ge(y_out, count(2 * f + 1 + (PAIRS if f >= HC else 0), 1, 1))
                for n in range(2):
                    g = gathered_y[p][n][:].rearrange("p (t d) -> p t d", d=D)
                    step(f"weighted{n + 1}", dve.tensor_tensor, g, g,
                         weight[:, chunk, n:n + 1].to_broadcast([P, CT, D]), ALU.mult)
                    step(f"sum{n + 1}", dve.tensor_tensor, ending[p][:], ending[p][:] if n else acc[:, chunk, :], g,
                         ALU.add)
                center(step, end_total[p], ending[p])

            def work(step, i):
                if 0 <= step < ALL_PAIRS:
                    multiply(step, i, step % 2)
                if 0 <= step - 2 < ALL_PAIRS:
                    move_y(step - 2, i)
                for c in at(BEGIN_AT, step):
                    chain = Steps(R_DVE, r_dve, lambda n, c=c: count(c, len(R_DVE), n))
                    dve.wait_ge(x_loaded[c], 16)
                    if c >= 3:
                        dve.wait_ge(r_token, count(c, 1, -2))
                    chain("sum", dve.tensor_tensor, centered[c % 3][:], x[:, c * CT:(c + 1) * CT, :],
                          x_in[:, c * CT:(c + 1) * CT, :], ALU.add)
                    center(chain, total[c % 2], centered[c % 3])
                for c in at(BEGIN_AT, step, 1):
                    dve.wait_ge(r_squared, c + 1)
                    variance(Steps(R_VAR, r_var, lambda n, c=c: count(c, len(R_VAR), n)), squares[c % 2], var[c % 2])
                for c in at(BEGIN_AT, step, 2):
                    dve.wait_ge(r_rstd, c + 1)
                    dve.tensor_tensor(token[:, c * CT:(c + 1) * CT, :], centered[c % 3][:],
                                      rstd[c % 2][:].unsqueeze(2).to_broadcast([P, CT, D]), ALU.mult
                                      ).then_inc(r_token, 1)
                for h in range(HALVES):
                    for stage, when in PICK_AT[h].items():
                        if when == step:
                            pick(h, stage)
                for f in at(END_AT, step, 1):
                    dve.wait_ge(f_squared, f + 1)
                    variance(Steps(F_DVE, f_dve, lambda n, f=f: count(f, len(F_DVE), n)),
                             end_squares[f % 2], end_var[f % 2])
                for f in at(END_AT, step, 2):
                    chain = Steps(F_DVE, f_dve, lambda n, f=f: count(f, len(F_DVE), n))
                    dve.wait_ge(f_rstd, f + 1)
                    dve.wait_ge(out_stored[f % 2], pair_count(f - 2, f % 2))
                    chain("result", dve.tensor_tensor, result[f % 2][:], ending[f % 2][:],
                          end_rstd[f % 2][:].unsqueeze(2).to_broadcast([P, CT, D]), ALU.mult)

                for f in at(END_AT, step):
                    combine(f, f % 2)

            at_every_step(dve, work)

        @block.tensor
        def _(pe):
            for s in (gates, h_turned, downs, rows_turned):
                prime(pe, s, 1)
            pe.nop().then_inc(rows_turned, RING)
            pe.wait_ge(st["experts_loaded"], 16 * EXPERT_LOADS)

            ahead = [pe.alloc_register(f"ahead{k}") for k in range(2 * (RING + 2))]
            weights_at = {}

            def load_weights(step, i):
                m = step - FIRST_ROUTED + i
                pe.load(ahead, table[0:1, bass.ds((m - 2) * 2, len(ahead))])

            def take_weights(step):
                for k in range(RING + 2):
                    weights_at[step - 2 + k] = [pe.snap(r, min_val=0, max_val=EXPERTS * WEIGHTS)
                                                for r in ahead[2 * k:2 * k + 2]]

            def experts(n):
                if not routed(n):
                    return [0, 0]
                if n not in weights_at:
                    weights_at[n] = [pe.value_load(table[0:1, 2 * (n - FIRST_ROUTED) + t:2 * (n - FIRST_ROUTED) + t + 1],
                                                   min_val=0, max_val=EXPERTS * WEIGHTS) for t in range(2)]
                return weights_at[n]

            def gate_up(n, i, p):
                weights_of = experts(n)
                if routed(n):
                    pe.wait_ge(rows_moved, count(n - FIRST_ROUTED + i, 1, 1))
                pe.wait_ge(hiddens, count(n + i, 1, -1))
                for t, e in enumerate(weights_of):
                    tile = rows_t[p][:, t * P:(t + 1) * P] if routed(n) else \
                        tokens_t[:, (first_tile(n) + t) * P:(first_tile(n) + t + 1) * P]
                    last = pe.matmul(ps_gu[p][:, t, :], tile, weights[:, bass.ds(e, 2 * FF)],
                                     start=True, stop=True)
                last.then_inc(gates, 1)

            def turn_rows(n, i):
                m = n - FIRST_ROUTED
                pe.wait_ge(rows_loaded[m % RING], ring_value(m, i))
                pe.wait_ge(rows_moved, count(m + i, 1, 0))
                for t in range(2):
                    last = pe.transpose(ps_x[:, t, :], rows[m % RING][:, t, :], ident[:])
                last.then_inc(rows_turned, 1)

            def down(n, i, p):
                weights_of = experts(n)
                pe.wait_ge(h_moved, count(n + i, 1, 1))
                pe.wait_ge(y_out, count(n + i, 1, 0))
                for t, e in enumerate(weights_of):
                    for f in range(2):
                        last = pe.matmul(ps_y[:, t, :], hidden_t[p][:, t, f, :],
                                         weights[:, bass.ds(e + (2 * FF + f * D), D)], start=(f == 0), stop=(f == 1))
                last.then_inc(downs, 1)

            def turn_hidden(n, i, p):
                pe.wait_ge(hiddens, count(n + i, 1, 1))
                pe.wait_ge(h_moved, count(n + i, 1, 0))
                for t in range(2):
                    for f in range(2):
                        last = pe.transpose(ps_h[:, t, f, :], hidden[p][:, t, f * P:(f + 1) * P], ident[:])
                last.then_inc(h_turned, 1)

            def work(step, i):
                if 0 <= step < ALL_PAIRS:
                    if step == 0:
                        pe.wait_ge(r_moved, HC)
                    if step == FIRST_LAST:
                        pe.wait_ge(r_moved, CHUNKS)
                    if step == FIRST_ROUTED:
                        pe.wait_ge(p_dve, picked(0, "table"))
                    if step == PICK_AT[1]["blocks"] + 1:
                        pe.wait_ge(p_dve, picked(1, "table"))
                    gate_up(step, i, step % 2)
                if routed(step + 1):
                    if step + 1 == FIRST_ROUTED:
                        pe.wait_ge(r_moved, CHUNKS)
                    turn_rows(step + 1, i)
                if 0 <= step - 1 < ALL_PAIRS:
                    turn_hidden(step - 1, i, (step - 1) % 2)
                if 0 <= step - 2 < ALL_PAIRS:
                    down(step - 2, i, step % 2)
                for c in at(BEGIN_AT, step, 3):
                    pe.wait_ge(r_token, count(c, 1, 1))
                    if c:
                        pe.wait_ge(r_moved, c)
                    for t in range(CT):
                        last = pe.transpose(ps_x[:, t, :], token[:, c * CT + t, :], ident[:])
                    last.then_inc(r_turned, 1)
                    pe.wait_ge(r_moved, c + 1)
                    if c == HC:
                        pe.wait_ge(p_dve, picked(0, "slot"))
                    for t in range(CT):
                        at_tile = c * CT + t
                        last = pe.matmul(ps_r[:, 0, at_tile % HT, :], tokens_t[:, at_tile * P:(at_tile + 1) * P],
                                         w_router[:], start=True, stop=True)
                    last.then_inc(r_logits, 1)
                for h in at({h: t["second"] for h, t in PICK_AT.items()}, step):
                    pe.wait_ge(p_dve, picked(h, "picks"))
                    pe.matmul(ps_r[:, 1], earlier[:], small["picks"][:], start=True, stop=True)
                    pe.matmul(ps_r[:, 2], ones[:], small["picks"][:], start=True, stop=True).then_inc(p_ranked, 1)

            at_every_step(pe, work, load_weights, take_weights)


def setup_phase(nc, ins, st):
    with ExitStack() as ctx:
        down_t = ctx.enter_context(nc.sbuf_tensor("down_t", [32, D], F32))
        up = ctx.enter_context(nc.sbuf_tensor("up", [32, 2 * KV], F32))
        ps_w = ctx.enter_context(nc.psum_tensor("ps_w", [P, 2 * KV], F32))
        loaded, latent_loaded, made, folded = (
            ctx.enter_context(nc.semaphore(n)) for n in ("loaded", "latent_loaded", "made", "folded"))
        block = ctx.enter_context(nc.Block())
        loads = [
            (st["wall"][0][:, 0:D], ins["g_wq"]),
            (st["wall"][1][:], ins["l_wqkv"]),
            (st["wo"][0][:], ins["g_wo"]),
            (st["wo"][1][:], ins["l_wo"]),
            (st["norm_w"][0][:], ins["norm1_w"].rearrange("(p a) -> p a", a=1)),
            (st["norm_w"][1][:], ins["norm2_w"].rearrange("(p a) -> p a", a=1)),
            (st["cos"][0][:], ins["cos_g"].rearrange("(t p) d -> p t d", p=P)),
            (st["sin"][0][:], ins["sin_g"].rearrange("(t p) d -> p t d", p=P)),
            (st["cos"][1][:], ins["cos_l"].rearrange("(t p) d -> p t d", p=P)),
            (st["sin"][1][:], ins["sin_l"].rearrange("(t p) d -> p t d", p=P)),
        ]

        @block.sync
        def _(sp):
            sp.dma_start(st["x"][:, 0:TPB, :], st["hidden_tiles"][:, 0:TPB, :]).then_inc(st["x_loaded"][0], 16)
            sp.dma_start(down_t[:], ins["g_kv_down_t"]).then_inc(latent_loaded, 16)
            sp.dma_start(up[:], ins["g_kv_up"]).then_inc(latent_loaded, 16)

        @block.scalar
        def _(act):
            for to, of in loads:
                act.dma_start(to, of).then_inc(loaded, 16)
            act.wait_ge(made, 1)
            for p in range(2):
                for m in ("qs", "ks"):
                    rows = st[m][p][ROWS:KPAD, :, :].rearrange("p h n -> p (h n)").bitcast(F32).rearrange(
                        "p (a n) -> p a n", n=D)
                    act.dma_start(rows, st["zeros"][0:KPAD - ROWS, :].unsqueeze(1).to_broadcast(
                        [KPAD - ROWS, rows.shape[1], D])).then_inc(st["padded"], 16)
            act.wait_ge(loaded, 16 * len(loads))

        @block.gpsimd
        def _(pool):
            pool.memset(st["zeros"][:], 0.0).then_inc(made, 1)
            pool.memset(st["ident"][:], 0.0).then_inc(made, 1)
            pool.memset(st["ident_bf"][:], 0.0).then_inc(made, 1)
            for p in range(2):
                pool.memset(st["va"][p][:], 0.0).then_inc(made, 1)
                pool.memset(st["vc"][p][:], 0.0).then_inc(made, 1)
            pool.wait_ge(made, 7)
            for p in range(2):
                pool.memset(st["va"][p][:, :, :, HD:HD + 1], 1.0).then_inc(made, 1)
            for m in ("ident", "ident_bf"):
                pool.affine_select(out=st[m][:], in_=st[m][:], compare_op=ALU.not_equal, fill=1.0, base=0,
                                   pattern=[[-1, P]], channel_multiplier=1).then_inc(made, 1)
            pool.wait_ge(made, 11)

        @block.tensor
        def _(pe):
            pe.wait_ge(latent_loaded, 32)
            pe.matmul(ps_w[:], down_t[:], up[:], start=True, stop=True).then_inc(folded, 1)

        @block.vector
        def _(dve):
            dve.wait_ge(folded, 1)
            dve.tensor_copy(st["wall"][0][:, D:PROJ], ps_w[:]).then_inc(folded, 1)
            dve.wait_ge(folded, 2)


def program(nc, ins, out):
    with ExitStack() as ctx:
        def sb(name, shape, dt=F32):
            return ctx.enter_context(nc.sbuf_tensor(name, shape, dt))

        st = {
            "x": sb("x", [P, TILES, D]),
            "ident": sb("ident", [P, P]), "ident_bf": sb("ident_bf", [P, P], BF16),
            "wall": [sb(f"wall{n}", [P, PROJ]) for n in range(2)],
            "wo": [sb(f"wo{n}", [P, D]) for n in range(2)],
            "norm_w": [sb(f"norm_w{n}", [P, 1]) for n in range(2)],
            "cos": [sb(f"cos{n}", [P, TPB, HD]) for n in range(2)],
            "sin": [sb(f"sin{n}", [P, TPB, HD]) for n in range(2)],
        }
        st.update(
            weights=sb("weights", [P, (1 + EXPERTS) * WEIGHTS]),
            multiples=sb("multiples", [P, HT]), numbers=sb("numbers", [P, BLOCKS]), zeros=sb("zeros", [P, D]),
            expert_ins=ins, x_loaded=[ctx.enter_context(nc.semaphore(f"x_in_batch{b}")) for b in range(B)],
            padded=ctx.enter_context(nc.semaphore("padded")),
            x_rows=nc.dram_tensor("x_rows", [HALVES * BLOCKS * P, D], F32).ap(),
            w_router=sb("w_router", [P, EXPERTS]), bias=sb("bias", [P, EXPERTS]), rank=sb("rank", [P, EXPERTS]),
            experts_loaded=ctx.enter_context(nc.semaphore("experts_loaded")),
            hidden_tiles=ins["hidden"].rearrange("b (t p) d -> p (b t) d", p=P))
        with ExitStack() as both:
            st.update(
                qs=[both.enter_context(nc.sbuf_tensor(f"qs{p}", [KPAD, HEADS, S], BF16)) for p in range(2)],
                ks=[both.enter_context(nc.sbuf_tensor(f"ks{p}", [KPAD, GROUPS, S], BF16)) for p in range(2)],
                va=[both.enter_context(nc.sbuf_tensor(f"va{p}", [P, TPB, GROUPS, VW], F32)) for p in range(2)],
                vc=[both.enter_context(nc.sbuf_tensor(f"vc{p}", [P, TPB, GROUPS, VW], F32)) for p in range(2)],
                q_dram=nc.dram_tensor("q_parts", [RUNS, PARTS, HEADS * HD, S], BF16).ap(),
                k_dram=nc.dram_tensor("k_parts", [RUNS, PARTS * KV, S], BF16).ap())
            setup_phase(nc, ins, st)
            attention_layers(nc, st)
        expert_phase(nc, ins, out, st)


def rotary(base):
    import numpy as np

    inv_freq = np.float32(1.0) / np.float32(base) ** (np.arange(0, HD, 2, dtype=np.float32) / np.float32(HD))
    angle = np.arange(S, dtype=np.float32)[:, None] * inv_freq[None, :].astype(np.float32)
    cos, sin = np.cos(angle), np.sin(angle)
    return np.repeat(cos, 2, axis=1), np.stack([-sin, sin], axis=-1).reshape(S, HD)


def kernel(**inputs):
    import numpy as np
    import concourse.bacc as bacc
    from concourse.bass_utils import run_bass_kernel_spmd

    a = {k.replace("L0_attn_", "").replace("L0_ffn_", ""): np.asarray(v) for k, v in inputs.items()}
    cos_g, sin_g = rotary(1000000.0)
    cos_l, sin_l = rotary(10000.0)

    def slices(shared, routed):
        return np.concatenate([shared[None], routed]).transpose(2, 0, 1)

    down = np.concatenate([a["sd_w"][None], a["wd"]]).reshape(1 + EXPERTS, D, FF // P, P).transpose(3, 0, 2, 1)
    arrays = {
        "hidden": a["hidden"], "norm1_w": a["norm1_w"], "norm2_w": a["norm2_w"],
        "g_wq": a["g_wq"], "g_kv_down_t": a["g_kv_down"].T,
        "g_kv_up": np.concatenate([a["g_k_up"], a["g_v_up"]], axis=1), "g_wo": a["g_wo"],
        "l_wqkv": np.concatenate([a["l_wq"], a["l_wk"], a["l_wv"]], axis=1), "l_wo": a["l_wo"],
        "cos_g": cos_g, "sin_g": sin_g, "cos_l": cos_l, "sin_l": sin_l,
        "weights": np.concatenate([slices(a["sg_w"], a["wg"]), slices(a["su_w"], a["wu"]),
                                   down.reshape(P, 1 + EXPERTS, -1)], axis=2).reshape(D, -1),
        "multiples": np.arange(HT).astype(np.float32) * P, "numbers": np.arange(BLOCKS).astype(np.float32),
        "w_router": a["router_w"].T, "bias": a["routing_bias"],
        "rank": np.arange(EXPERTS, 0, -1).astype(np.float32),
    }
    arrays = {f"in_{k}": np.ascontiguousarray(v) for k, v in arrays.items()}
    nc = bacc.Bacc("TRN2", target_bir_lowering=False, num_devices=1)
    ins = {k[3:]: nc.dram_tensor(k, v.shape, mybir.dt.from_np(v.dtype), kind="ExternalInput").ap()
           for k, v in arrays.items()}
    out = nc.dram_tensor("out", (B, S, D), F32, kind="ExternalOutput").ap()
    program(nc, ins, out)
    return run_bass_kernel_spmd(nc, [arrays], core_ids=[0]).results[0]["out"]
```
